# Optimizing a Trainium2 kernel written in Bass

```python
import numpy as np
import jax
import jax.numpy as jnp

def _softmax(x, axis=-1):
    return jax.nn.softmax(x, axis=axis)

def _gelu(x):
    return jax.nn.gelu(x, approximate=True)

def _silu(x):
    return jax.nn.silu(x)

def _sigmoid(x):
    return jax.nn.sigmoid(x)

def _layernorm(x, axis=-1, eps=1e-05):
    m = jnp.mean(x, axis=axis, keepdims=True)
    v = jnp.var(x, axis=axis, keepdims=True)
    return (x - m) / jnp.sqrt(v + eps)

def _scatter_add(tgt, idx, src, axis=0):
    return tgt.at[idx].add(src)

def _segment_sum(src, seg, n):
    return jax.ops.segment_sum(src, seg, n)
kernel_name = 'mk_recurrent_d2_jaxref_r8_c6e7fe'

def setup_inputs(seed: int=0):
    np.random.seed(seed)
    _w = jnp.asarray

    def _L0_attn_setup():
        import jax, jax.numpy as jnp
        import numpy as np
        import math
        HIDDEN = 128
        NUM_LAYERS = 12
        LAYER_ID = 6
        BATCH = 8
        SEQ = 256
        NEG_INF = -1e+38

        def _wkv_full(k, v, w, u):
            B, T, H = k.shape
            kt = jnp.swapaxes(k, 0, 1)
            vt = jnp.swapaxes(v, 0, 1)

            def step(carry, kv):
                aa, bb, pp = carry
                k_t, v_t = kv
                ww = u + k_t
                p = jnp.maximum(pp, ww)
                e1 = jnp.exp(pp - p)
                e2 = jnp.exp(ww - p)
                wkv_t = (e1 * aa + e2 * v_t) / (e1 * bb + e2 + 1e-09)
                ww2 = w + pp
                p2 = jnp.maximum(ww2, k_t)
                e1b = jnp.exp(ww2 - p2)
                e2b = jnp.exp(k_t - p2)
                return ((e1b * aa + e2b * v_t, e1b * bb + e2b, p2), wkv_t)
            init = (jnp.zeros((B, H), k.dtype), jnp.zeros((B, H), k.dtype), jnp.full((B, H), NEG_INF, k.dtype))
            _, wkvs = jax.lax.scan(step, init, (kt, vt))
            return jnp.swapaxes(wkvs, 0, 1)
        key = jax.random.key(seed)
        ks = jax.random.split(key, 5)
        x = jax.random.normal(ks[0], (BATCH, SEQ, HIDDEN), dtype=jnp.float32)
        ratio_0_to_1 = LAYER_ID / max(NUM_LAYERS - 1, 1)
        h = np.arange(HIDDEN, dtype=np.float64)
        decay = -5.0 + 8.0 * (h / (HIDDEN - 1)) ** (0.7 + 1.3 * ratio_0_to_1)
        time_decay = jnp.asarray(decay, dtype=jnp.float32)
        time_first = jnp.full((HIDDEN,), math.log(0.3), dtype=jnp.float32)
        time_mix_k = jnp.full((1, 1, HIDDEN), 0.65, dtype=jnp.float32)
        time_mix_v = jnp.full((1, 1, HIDDEN), 0.45, dtype=jnp.float32)
        time_mix_r = jnp.full((1, 1, HIDDEN), 0.0, dtype=jnp.float32)
        scale = 0.02
        W_k = jax.random.normal(ks[1], (HIDDEN, HIDDEN), dtype=jnp.float32) * scale
        W_v = jax.random.normal(ks[2], (HIDDEN, HIDDEN), dtype=jnp.float32) * scale
        W_r = jax.random.normal(ks[3], (HIDDEN, HIDDEN), dtype=jnp.float32) * scale
        W_o = jax.random.normal(ks[4], (HIDDEN, HIDDEN), dtype=jnp.float32) * scale
        return {'x': x, 'time_decay': time_decay, 'time_first': time_first, 'time_mix_k': time_mix_k, 'time_mix_v': time_mix_v, 'time_mix_r': time_mix_r, 'W_k': W_k, 'W_v': W_v, 'W_r': W_r, 'W_o': W_o}
    _L0_attn_in = _L0_attn_setup()

    def _L0_ffn_setup():
        import jax, jax.numpy as jnp
        import numpy as np
        EPS = 1e-06
        N_EXPERTS = 8

        def _rms_norm(x, scale, eps=EPS):
            mean_sq = jnp.mean(x.astype(jnp.float32) ** 2, axis=-1, keepdims=True)
            s = scale.astype(jnp.float32) * jax.lax.rsqrt(mean_sq + eps)
            return x * s.astype(x.dtype)

        def _dist2(x, y):
            nx = jnp.sum(x ** 2, axis=-1)[..., :, None]
            ny = jnp.sum(y ** 2, axis=-1)[..., None, :]
            return nx + ny - 2.0 * (x @ y.T)
        key = jax.random.key(seed)
        ks = jax.random.split(key, 5)
        dim, hidden, E = (128, 256, N_EXPERTS)
        x = jax.random.normal(ks[0], (4, 256, dim), dtype=jnp.float32)
        scale = jnp.ones((dim,), dtype=jnp.float32)
        centroids = jax.random.normal(ks[1], (E, dim), dtype=jnp.float32)
        up_w = jax.random.normal(ks[2], (E, dim, hidden * 2), dtype=jnp.float32) * dim ** (-0.5)
        down_w = jax.random.normal(ks[3], (E, hidden, dim), dtype=jnp.float32) * hidden ** (-0.5)
        return {'x': x, 'scale': scale, 'centroids': centroids, 'up_w': up_w, 'down_w': down_w}
    _L0_ffn_in = _L0_ffn_setup()

    def _L1_attn_setup():
        import jax, jax.numpy as jnp
        import numpy as np
        import math
        EMBED_DIM = 128
        NUM_HEADS = 16
        HEAD_DIM = EMBED_DIM // NUM_HEADS
        BLOCK = 64
        SCALE = 1.0 / math.sqrt(HEAD_DIM)

        def _flash_attn(Q, K, V):
            B, H, S, hd = Q.shape
            nkb = S // BLOCK
            Kb = K.reshape(B, H, nkb, BLOCK, hd).transpose(2, 0, 1, 3, 4)
            Vb = V.reshape(B, H, nkb, BLOCK, hd).transpose(2, 0, 1, 3, 4)
            out0 = jnp.zeros_like(Q)
            m0 = jnp.full((B, H, S, 1), -jnp.inf, dtype=Q.dtype)
            l0 = jnp.zeros((B, H, S, 1), dtype=Q.dtype)

            def body(carry, kv):
                out, m, l = carry
                K_blk, V_blk = kv
                scores = jnp.einsum('bhqd,bhkd->bhqk', Q, K_blk) * SCALE
                M_ij = scores.max(axis=-1, keepdims=True)
                m_new = jnp.maximum(m, M_ij)
                corr = jnp.exp(m - m_new)
                exp_scores = jnp.exp(scores - m_new)
                chunk_sum = exp_scores.sum(axis=-1, keepdims=True)
                l_new = chunk_sum * corr + chunk_sum
                out_new = out * corr + jnp.einsum('bhqk,bhkd->bhqd', exp_scores, V_blk)
                return ((out_new, m_new, l_new), None)
            (out, m, l), _ = jax.lax.scan(body, (out0, m0, l0), (Kb, Vb))
            return out / l
        key = jax.random.key(seed)
        ks = jax.random.split(key, 6)
        B, S, E = (4, 256, EMBED_DIM)
        std = 1.0 / math.sqrt(E)
        return {'x': jax.random.normal(ks[0], (B, S, E), dtype=jnp.float32), 'q_w': jax.random.normal(ks[1], (E, E), dtype=jnp.float32) * std, 'k_w': jax.random.normal(ks[2], (E, E), dtype=jnp.float32) * std, 'v_w': jax.random.normal(ks[3], (E, E), dtype=jnp.float32) * std, 'out_w': jax.random.normal(ks[4], (E, E), dtype=jnp.float32) * std, 'out_b': jnp.zeros((E,), dtype=jnp.float32)}
    _L1_attn_in = _L1_attn_setup()

    def _L1_ffn_setup():
        import jax, jax.numpy as jnp
        import numpy as np
        N_HEAD, N_ACTIVE, D_MODEL, D_ATTN = (16, 4, 128, 64)
        key = jax.random.key(seed)
        ks = jax.random.split(key, 12)
        s = 0.02
        B, S = (2, 512)
        return {'x': jax.random.normal(ks[0], (B, S, D_MODEL), dtype=jnp.float32), 'Wq': jax.random.normal(ks[1], (D_MODEL, N_HEAD * D_ATTN), dtype=jnp.float32) * s, 'bq': jnp.zeros((N_HEAD * D_ATTN,), dtype=jnp.float32), 'Wk': jax.random.normal(ks[2], (D_MODEL, N_HEAD * D_ATTN), dtype=jnp.float32) * s, 'bk': jnp.zeros((N_HEAD * D_ATTN,), dtype=jnp.float32), 'Wv': jax.random.normal(ks[3], (D_MODEL, N_HEAD * D_ATTN), dtype=jnp.float32) * s, 'bv': jnp.zeros((N_HEAD * D_ATTN,), dtype=jnp.float32), 'Wr': jax.random.normal(ks[4], (D_MODEL, N_HEAD), dtype=jnp.float32) * s, 'br': jnp.zeros((N_HEAD,), dtype=jnp.float32), 'Wo': jax.random.normal(ks[5], (N_ACTIVE * D_ATTN, D_MODEL), dtype=jnp.float32) * s, 'bo': jnp.zeros((D_MODEL,), dtype=jnp.float32)}
    _L1_ffn_in = _L1_ffn_setup()
    _d = {'L0_attn_x': _L0_attn_in['x'], 'L0_attn_time_decay': _L0_attn_in['time_decay'], 'L0_attn_time_first': _L0_attn_in['time_first'], 'L0_attn_time_mix_k': _L0_attn_in['time_mix_k'], 'L0_attn_time_mix_v': _L0_attn_in['time_mix_v'], 'L0_attn_time_mix_r': _L0_attn_in['time_mix_r'], 'L0_attn_W_k': _L0_attn_in['W_k'], 'L0_attn_W_v': _L0_attn_in['W_v'], 'L0_attn_W_r': _L0_attn_in['W_r'], 'L0_attn_W_o': _L0_attn_in['W_o'], 'L0_ffn_scale': _L0_ffn_in['scale'], 'L0_ffn_centroids': _L0_ffn_in['centroids'], 'L0_ffn_up_w': _L0_ffn_in['up_w'], 'L0_ffn_down_w': _L0_ffn_in['down_w'], 'L1_attn_q_w': _L1_attn_in['q_w'], 'L1_attn_k_w': _L1_attn_in['k_w'], 'L1_attn_v_w': _L1_attn_in['v_w'], 'L1_attn_out_w': _L1_attn_in['out_w'], 'L1_attn_out_b': _L1_attn_in['out_b'], 'L1_ffn_Wq': _L1_ffn_in['Wq'], 'L1_ffn_bq': _L1_ffn_in['bq'], 'L1_ffn_Wk': _L1_ffn_in['Wk'], 'L1_ffn_bk': _L1_ffn_in['bk'], 'L1_ffn_Wv': _L1_ffn_in['Wv'], 'L1_ffn_bv': _L1_ffn_in['bv'], 'L1_ffn_Wr': _L1_ffn_in['Wr'], 'L1_ffn_br': _L1_ffn_in['br'], 'L1_ffn_Wo': _L1_ffn_in['Wo'], 'L1_ffn_bo': _L1_ffn_in['bo']}
    _x0 = _d['L0_attn_x']
    _d['L0_attn_x'] = jax.random.normal(jax.random.fold_in(jax.random.key(seed), 1), (32, 256, 128), dtype=_x0.dtype)
    del _x0
    return _d

def reference(L0_attn_x, L0_attn_time_decay, L0_attn_time_first, L0_attn_time_mix_k, L0_attn_time_mix_v, L0_attn_time_mix_r, L0_attn_W_k, L0_attn_W_v, L0_attn_W_r, L0_attn_W_o, L0_ffn_scale, L0_ffn_centroids, L0_ffn_up_w, L0_ffn_down_w, L1_attn_q_w, L1_attn_k_w, L1_attn_v_w, L1_attn_out_w, L1_attn_out_b, L1_ffn_Wq, L1_ffn_bq, L1_ffn_Wk, L1_ffn_bk, L1_ffn_Wv, L1_ffn_bv, L1_ffn_Wr, L1_ffn_br, L1_ffn_Wo, L1_ffn_bo):

    def _L0_attn_ref(x, time_decay, time_first, time_mix_k, time_mix_v, time_mix_r, W_k, W_v, W_r, W_o):
        import jax, jax.numpy as jnp
        import numpy as np
        import math
        HIDDEN = 128
        NUM_LAYERS = 12
        LAYER_ID = 6
        BATCH = 8
        SEQ = 256
        NEG_INF = -1e+38

        def _wkv_full(k, v, w, u):
            B, T, H = k.shape
            kt = jnp.swapaxes(k, 0, 1)
            vt = jnp.swapaxes(v, 0, 1)

            def step(carry, kv):
                aa, bb, pp = carry
                k_t, v_t = kv
                ww = u + k_t
                p = jnp.maximum(pp, ww)
                e1 = jnp.exp(pp - p)
                e2 = jnp.exp(ww - p)
                wkv_t = (e1 * aa + e2 * v_t) / (e1 * bb + e2 + 1e-09)
                ww2 = w + pp
                p2 = jnp.maximum(ww2, k_t)
                e1b = jnp.exp(ww2 - p2)
                e2b = jnp.exp(k_t - p2)
                return ((e1b * aa + e2b * v_t, e1b * bb + e2b, p2), wkv_t)
            init = (jnp.zeros((B, H), k.dtype), jnp.zeros((B, H), k.dtype), jnp.full((B, H), NEG_INF, k.dtype))
            _, wkvs = jax.lax.scan(step, init, (kt, vt))
            return jnp.swapaxes(wkvs, 0, 1)
        x_prev = jnp.pad(x[:, :-1, :], ((0, 0), (1, 0), (0, 0)))
        xk = x * time_mix_k + x_prev * (1.0 - time_mix_k)
        xv = x * time_mix_v + x_prev * (1.0 - time_mix_v)
        xr = x * time_mix_r + x_prev * (1.0 - time_mix_r)
        k = jnp.einsum('bth,oh->bto', xk, W_k)
        v = jnp.einsum('bth,oh->bto', xv, W_v)
        r = jax.nn.sigmoid(jnp.einsum('bth,oh->bto', xr, W_r))
        wkv = _wkv_full(k, v, time_decay, time_first)
        out = jnp.einsum('bth,oh->bto', r * wkv, W_o)
        return out

    def _L0_ffn_ref(x, scale, centroids, up_w, down_w):
        import jax, jax.numpy as jnp
        import numpy as np
        EPS = 1e-06
        N_EXPERTS = 8

        def _rms_norm(x, scale, eps=EPS):
            mean_sq = jnp.mean(x.astype(jnp.float32) ** 2, axis=-1, keepdims=True)
            s = scale.astype(jnp.float32) * jax.lax.rsqrt(mean_sq + eps)
            return x * s.astype(x.dtype)

        def _dist2(x, y):
            nx = jnp.sum(x ** 2, axis=-1)[..., :, None]
            ny = jnp.sum(y ** 2, axis=-1)[..., None, :]
            return nx + ny - 2.0 * (x @ y.T)
        skip = x
        xn = _rms_norm(x, scale)
        ids = jnp.argmin(_dist2(xn, centroids), axis=-1)
        out = jnp.zeros_like(x)
        for e in range(N_EXPERTS):
            h = jnp.einsum('bsd,dh->bsh', xn, up_w[e])
            a, g = jnp.split(h, 2, axis=-1)
            y = jnp.einsum('bsh,hd->bsd', a * jax.nn.silu(g), down_w[e])
            out = jnp.where((ids == e)[..., None], y, out)
        return out + skip

    def _L1_attn_ref(x, q_w, k_w, v_w, out_w, out_b):
        import jax, jax.numpy as jnp
        import numpy as np
        import math
        EMBED_DIM = 128
        NUM_HEADS = 16
        HEAD_DIM = EMBED_DIM // NUM_HEADS
        BLOCK = 64
        SCALE = 1.0 / math.sqrt(HEAD_DIM)

        def _flash_attn(Q, K, V):
            B, H, S, hd = Q.shape
            nkb = S // BLOCK
            Kb = K.reshape(B, H, nkb, BLOCK, hd).transpose(2, 0, 1, 3, 4)
            Vb = V.reshape(B, H, nkb, BLOCK, hd).transpose(2, 0, 1, 3, 4)
            out0 = jnp.zeros_like(Q)
            m0 = jnp.full((B, H, S, 1), -jnp.inf, dtype=Q.dtype)
            l0 = jnp.zeros((B, H, S, 1), dtype=Q.dtype)

            def body(carry, kv):
                out, m, l = carry
                K_blk, V_blk = kv
                scores = jnp.einsum('bhqd,bhkd->bhqk', Q, K_blk) * SCALE
                M_ij = scores.max(axis=-1, keepdims=True)
                m_new = jnp.maximum(m, M_ij)
                corr = jnp.exp(m - m_new)
                exp_scores = jnp.exp(scores - m_new)
                chunk_sum = exp_scores.sum(axis=-1, keepdims=True)
                l_new = chunk_sum * corr + chunk_sum
                out_new = out * corr + jnp.einsum('bhqk,bhkd->bhqd', exp_scores, V_blk)
                return ((out_new, m_new, l_new), None)
            (out, m, l), _ = jax.lax.scan(body, (out0, m0, l0), (Kb, Vb))
            return out / l
        B, S, E = x.shape
        H, hd = (NUM_HEADS, HEAD_DIM)

        def split_heads(t):
            return t.reshape(B, S, H, hd).transpose(0, 2, 1, 3)
        Q = split_heads(x @ q_w.T)
        K = split_heads(x @ k_w.T)
        V = split_heads(x @ v_w.T)
        out = _flash_attn(Q, K, V)
        out = out.transpose(0, 2, 1, 3).reshape(B, S, E)
        return out @ out_w.T + out_b

    def _L1_ffn_ref(x, Wq, bq, Wk, bk, Wv, bv, Wr, br, Wo, bo):
        import jax, jax.numpy as jnp
        import numpy as np
        N_HEAD, N_ACTIVE, D_MODEL, D_ATTN = (16, 4, 128, 64)
        B, S, D = x.shape
        H, K, dh = (N_HEAD, N_ACTIVE, D_ATTN)
        dist = jax.nn.softmax(jnp.mean(x @ Wr + br, axis=1), axis=-1)
        top_vals, top_idx = jax.lax.top_k(dist, K)
        sparse = jnp.zeros_like(dist).at[jnp.arange(B)[:, None], top_idx].set(top_vals)
        gates_all = jax.nn.softmax(sparse, axis=1)
        g = jnp.take_along_axis(gates_all, top_idx, axis=1)[:, :, None, None]

        def proj(W, b):
            return (x @ W + b).reshape(B, S, H, dh).transpose(0, 2, 1, 3)
        Q, Kt, V = (proj(Wq, bq), proj(Wk, bk), proj(Wv, bv))
        idx = top_idx[:, :, None, None]
        Qk = jnp.take_along_axis(Q, idx, axis=1) * g
        Kk = jnp.take_along_axis(Kt, idx, axis=1) * g
        Vk = jnp.take_along_axis(V, idx, axis=1) * g
        scores = jnp.einsum('bksd,bktd->bkst', Qk, Kk) / jnp.sqrt(jnp.float32(dh))
        attn = jax.nn.softmax(scores, axis=-1)
        out = jnp.einsum('bkst,bktd->bksd', attn, Vk)
        out = out.transpose(0, 2, 1, 3).reshape(B, S, K * dh)
        return out @ Wo + bo
    x = L0_attn_x
    xn = _layernorm(x, axis=-1)
    s = _L0_attn_ref(xn, L0_attn_time_decay, L0_attn_time_first, L0_attn_time_mix_k, L0_attn_time_mix_v, L0_attn_time_mix_r, L0_attn_W_k, L0_attn_W_v, L0_attn_W_r, L0_attn_W_o)
    g = _silu(_L0_ffn_ref(xn, L0_ffn_scale, L0_ffn_centroids, L0_ffn_up_w, L0_ffn_down_w))
    x = x + s * g
    xn = _layernorm(x, axis=-1)
    s = _L1_attn_ref(xn, L1_attn_q_w, L1_attn_k_w, L1_attn_v_w, L1_attn_out_w, L1_attn_out_b)
    g = _silu(_L1_ffn_ref(xn, L1_ffn_Wq, L1_ffn_bq, L1_ffn_Wk, L1_ffn_bk, L1_ffn_Wv, L1_ffn_bv, L1_ffn_Wr, L1_ffn_br, L1_ffn_Wo, L1_ffn_bo))
    x = x + s * g
    return x

_drawn_inputs = setup_inputs


def setup_inputs(seed=0):
    import zlib

    import numpy as np

    out = dict(_drawn_inputs(seed))
    spreads = {'L0_attn_time_first': (-1.2039728164672852, 0.6),
     'L0_attn_time_mix_k': (0.6499999761581421, 0.6),
     'L0_attn_time_mix_v': (0.44999998807907104, 0.6),
     'L0_attn_time_mix_r': (0.0, 0.8),
     'L0_ffn_scale': (1.0, 0.6),
     'L1_attn_out_b': (0.0, 2.0),
     'L1_ffn_bq': (0.0, 2.0),
     'L1_ffn_bk': (0.0, 0.8),
     'L1_ffn_bv': (0.0, 2.0),
     'L1_ffn_br': (0.0, 0.8),
     'L1_ffn_bo': (0.0, 0.306)}
    factors = {'L0_attn_time_decay': 7.181,
     'L0_attn_W_k': 8.0,
     'L0_attn_W_v': 5.347,
     'L0_attn_W_r': 8.0,
     'L0_attn_W_o': 5.314,
     'L0_ffn_centroids': 8.0,
     'L0_ffn_up_w': 8.0,
     'L0_ffn_down_w': 8.0,
     'L1_attn_q_w': 2.843,
     'L1_ffn_Wq': 64.0,
     'L1_ffn_Wk': 64.0,
     'L1_ffn_Wv': 43.047,
     'L1_ffn_Wr': 8.0,
     'L1_ffn_Wo': 8.0}
    for name, (base, spread) in spreads.items():
        noise = np.random.default_rng([zlib.crc32(name.encode()), seed]).standard_normal(out[name].shape)
        drawn = base * np.exp(spread * noise) if base else spread * noise
        out[name] = jnp.asarray(drawn.astype(out[name].dtype))
    for name, factor in factors.items():
        out[name] = (out[name] * factor).astype(out[name].dtype)
    return out
```

```python
import concourse.bass as bass
from concourse import mybir
from contextlib import ExitStack

B, SEQ, D = 32, 256, 128
P = 128
TB = SEQ // P
NT = B * TB
NE, HID = 8, 256
NST = NT + NE
H, HD = 16, 8
BLK = 64
NBLK = SEQ // BLK
RH, RK, RD = 16, 4, 64
LN_EPS, RMS_EPS, WKV_EPS = 1e-5, 1e-6, 1e-9
NEG_INF = -1e38

fp32 = mybir.dt.float32
bf16 = mybir.dt.bfloat16
i32 = mybir.dt.int32
u32 = mybir.dt.uint32
ALU = mybir.AluOpType
ACT = mybir.ActivationFunctionType
AX = mybir.AxisListType


def after(eng, sem, count):
    if not (isinstance(count, int) and count <= 0):
        eng.wait_ge(sem, count)

SCRATCH = [("xs_dram", (NST * P, D), fp32), ("ys_dram", (NST * P, D), fp32),
           ("parts_dram", (2, 2, 3, P, SEQ), bf16), ("mrow_dram", (2, 3, H, SEQ), bf16)]


def apart(eng):
    eng.nop(nofuse=True)


class Chain:

    def __init__(self, eng, sem, n, batch):
        self.eng, self.sem, self.n, self.base, self.k = eng, sem, n, batch * n, 0

    def __call__(self, ins):
        self.k += 1
        ins.then_inc(self.sem, 1)
        self.eng.wait_ge(self.sem, self.base + self.k)

    def end(self):
        assert self.k == self.n, (self.k, self.n)


def program(nc, x, l0_w, l0_cols, rms_scale, centT, up_w, down_w, l1_w, out_b, qkv_w, qkv_b,
            wr, br, wo, bo, out, xs_dram, ys_dram, parts_dram, mrow_dram):
    ctx = ExitStack()
    with ctx:
        def sb(name, shape, dt=fp32):
            return ctx.enter_context(nc.sbuf_tensor(name, shape, dt))

        def sem(name):
            return ctx.enter_context(nc.semaphore(name))

        ident = sb("ident", [P, P])
        ones = sb("ones", [P, SEQ])
        earlier = sb("earlier", [P, P])
        iota8 = sb("iota8", [P, NE])
        iota_i = sb("iota_i", [P, NST], i32)
        iota_t = sb("iota_t", [P, NST])
        w0 = sb("w0", [P, 4, D])
        cols = sb("cols", [P, 5])
        ommix = sb("ommix", [P, 3])
        decay = sb("decay", [P, SEQ])
        scale_b = sb("scale_b", [P, D])
        cT = sb("cT", [P, NE])
        cTsq = sb("cTsq", [P, NE])
        cT2 = sb("cT2", [P, NE])
        neg1 = sb("neg1", [P, P])
        nny = sb("nny", [P, NE])
        zero_tile = sb("zero_tile", [P, D])
        X = sb("X", [P, NT, D])
        S = sb("S", [P, NT, D])
        mv = sb("mv", [P, NT, 2])
        rstd = sb("rstd", [P, NT])
        nmr = sb("nmr", [P, NT])
        rrms = sb("rrms", [P, NT])
        mhalf = sb("mhalf", [P, NT])
        onehot = sb("onehot", [P, NT, NE])
        slot = sb("slot", [P, NT], i32)
        tile_expert = sb("tile_expert", [P, NST], i32)

        e2 = ExitStack()
        ctx.enter_context(e2)
        XR = e2.enter_context(nc.sbuf_tensor("XR", [P, NT, D], fp32))
        up = e2.enter_context(nc.sbuf_tensor("up", [P, NE * 2 * HID], fp32))
        down = e2.enter_context(nc.sbuf_tensor("down", [P, NE * 2 * D], fp32))

        PS = [ctx.enter_context(nc.psum_tensor(f"PS{i}", [P, 512], fp32)) for i in range(8)]

        s_const = sem("consts_ready")
        s_x = sem("x_loaded")
        s_w = sem("weights_loaded")
        s_we = sem("expert_weights_loaded")
        s_zero = sem("sorted_zeroed")
        s_setup = sem("setup_chain_pool")
        s_setv = sem("setup_chain_dve")
        s_cent = sem("centroid_norms_ready")
        s_stat = sem("variances_ready")
        s_pow = sem("rsqrts_ready")

        e1 = ExitStack()
        ctx.enter_context(e1)
        block = e1.enter_context(nc.Block())

        def sb1(name, shape, dt=fp32):
            return e1.enter_context(nc.sbuf_tensor(name, shape, dt))

        def sem(name):
            return e1.enter_context(nc.semaphore(name))

        xn_t = [sb1(f"xn_t{i}", [P, TB, D]) for i in range(2)]
        xr_t = [sb1(f"xr_t{i}", [P, TB, D]) for i in range(2)]
        xnT = [sb1(f"xnT{i}", [P, SEQ + 1]) for i in range(2)]
        xrT = [sb1(f"xrT{i}", [P, SEQ]) for i in range(2)]
        xrTsq = [sb1(f"xrTsq{i}", [P, SEQ]) for i in range(2)]
        prevmix = [sb1(f"prevmix{i}", [P, 3, SEQ]) for i in range(2)]
        mixed = [sb1(f"mixed{i}", [P, 3, SEQ]) for i in range(2)]
        kv = [sb1(f"kv{i}", [P, 2, SEQ]) for i in range(2)]
        rtanh = [sb1(f"rtanh{i}", [P, SEQ]) for i in range(2)]
        pp = sb1("pp", [P, SEQ + 1])
        aa = sb1("aa", [P, SEQ + 1])
        bb = sb1("bb", [P, SEQ + 1])
        dcarry = sb1("dcarry", [P, SEQ])
        dout = sb1("dout", [P, SEQ])
        args = sb1("args", [P, 4, SEQ])
        ex = sb1("ex", [P, 4, SEQ])
        ev = sb1("ev", [P, 2, SEQ])
        num = sb1("num", [P, SEQ])
        den = sb1("den", [P, SEQ])
        rwkv = [sb1(f"rwkv{i}", [P, SEQ]) for i in range(2)]
        nd = [sb1(f"nd{i}", [P, TB, NE]) for i in range(2)]
        best = sb1("best", [P, TB, 8])
        besti = sb1("besti", [P, TB, 8], u32)

        s_norm = sem("normalized")
        s_xr = [sem(f"xr_kept{i}") for i in range(2)]
        s_tr = sem("transposed")
        s_xnT = sem("xnT_ready")
        s_xrT = sem("xrT_ready")
        s_xrsq = sem("xrT_squared")
        s_prevmix = sem("prevmix_ready")
        s_mix = sem("mixed_ready")
        s_kvr = sem("kvr_in_psum")
        s_kv = sem("kv_ready")
        s_th = sem("gate_tanh_ready")
        s_dist = sem("distances_in_psum")
        s_route = sem("routed")
        s_args = sem("exponents_ready")
        s_ex = sem("exponentials_ready")
        s_rwkv = sem("rwkv_ready")
        s_wkv = sem("wkv_chain")
        s_rchain = sem("route_chain")
        s_nchain = sem("norm_chain")
        st_all = sb1("st_all", [P, NT, 6])
        s_set2 = sem("setup_chain_dve2")
        s_so = sem("s_in_psum")
        s_s = sem("s_stored")

        psT, psKV, psR, psO, psD = PS[0:2], PS[2:4], PS[4:6], PS[6], PS[7]

        @block.sync
        def _(sp):
            sp.dma_start(X[:, :, :], x.rearrange("(t p) d -> p t d", p=P)).then_inc(s_x, 16)
            for dst, src in ((w0[:, :, :], l0_w), (cols[:, :], l0_cols), (cT[:, :], centT),
                             (scale_b[:, :], rms_scale.to_broadcast([P, D]))):
                sp.dma_start(dst, src).then_inc(s_w, 16)
            sp.wait_ge(s_const, 1)
            sp.dma_start(xs_dram.rearrange("(t p) d -> p t d", p=P),
                         zero_tile[:, :].unsqueeze(1).broadcast_to([P, NST, D])).then_inc(s_zero, 16)
            sp.dma_start(up[:, :], up_w).then_inc(s_we, 16)
            sp.dma_start(down[:, :], down_w).then_inc(s_we, 16)

            def keep(t, p):
                sp.wait_ge(s_norm, t + 1)
                apart(sp)
                sp.dma_start(XR[:, bass.ds(t * TB, TB), :], xr_t[p][:, :, :]).then_inc(s_xr[p], 16)
            keep(0, 0)
            keep(1, 1)
            keep(2, 0)
            with sp.Fori(1, B // 2 - 1) as pair:
                keep(2 * pair + 1, 1)
                keep(2 * pair + 2, 0)
            keep(B - 1, 1)
            for p in range(2):
                sp.wait_ge(s_xr[p], 16 * (B // 2))
            sp.wait_ge(s_zero, 16)
            sp.wait_ge(s_we, 32)

        @block.gpsimd
        def _(pool):
            ch = Chain(pool, s_setup, 3, 0)
            pool.memset(zero_tile[:, :], 0.0).then_inc(s_const, 1)
            pool.memset(ones[:, :], 1.0)
            pool.memset(neg1[:, :], -1.0)
            pool.memset(mhalf[:, :], -0.5)
            pool.memset(ident[:, :], 0.0)
            pool.iota(iota_i[:, :], pattern=[[1, NST]], base=0, channel_multiplier=0)
            for i in range(2):
                pool.memset(xnT[i][:, 0:1], 0.0)
            pool.memset(pp[:, 0:1], NEG_INF)
            pool.memset(aa[:, 0:1], 0.0)
            ch(pool.memset(bb[:, 0:1], 0.0))
            pool.affine_select(out=ident[:, :], in_=ident[:, :], compare_op=ALU.not_equal, fill=1.0, base=0,
                               pattern=[[-1, P]], channel_multiplier=1)
            pool.affine_select(out=earlier[:, :], in_=ones[:, 0:P], compare_op=ALU.is_gt, fill=0.0, base=0,
                               pattern=[[1, P]], channel_multiplier=-1)
            ch(pool.tensor_copy(iota_t[:, :], iota_i[:, :]))
            ch(pool.tensor_copy(iota8[:, :], iota_t[:, 0:NE]))
            ch.end()
            pool.sem_inc(s_const, 1)
            for k, r in enumerate((rstd, rrms)):
                pool.wait_ge(s_stat, k + 1)
                pool.tensor_tensor(r[:, :], r[:, :], mhalf[:, :], ALU.pow).then_inc(s_pow, 1)

            def square(t, p):
                pool.wait_ge(s_xrT, t + 1)
                after(pool, s_dist, t - 1)
                pool.tensor_tensor(xrTsq[p][:, :], xrT[p][:, :], xrT[p][:, :], ALU.mult).then_inc(s_xrsq, 1)
            square(0, 0)
            square(1, 1)
            square(2, 0)
            with pool.Fori(1, B // 2 - 1) as pair:
                square(2 * pair + 1, 1)
                square(2 * pair + 2, 0)
            square(B - 1, 1)

        @block.vector
        def _(dve):
            ch = Chain(dve, s_setv, 3, 0)
            dve.wait_ge(s_w, 16 * 4)
            dve.wait_ge(s_const, 2)
            dve.tensor_scalar(decay[:, :], ones[:, :],
                              cols[:, 0:1], None, ALU.mult)
            dve.tensor_scalar(ommix[:, :], cols[:, 2:5], -1.0, 1.0, ALU.mult, ALU.add)
            dve.tensor_scalar(cT2[:, :], cT[:, :], 2.0, None, ALU.mult)
            dve.tensor_scalar(w0[:, 3, :], w0[:, 3, :], 0.25, None, ALU.mult)
            dve.tensor_tensor(cTsq[:, :], cT[:, :], cT[:, :], ALU.mult).then_inc(s_cent, 1)
            dve.wait_ge(s_cent, 2)
            ch(dve.tensor_copy(nny[:, :], PS[7][:, 0:NE]))
            dve.wait_ge(s_x, 16)
            for t in range(NT):
                last = dve.bn_stats(st_all[:, t, :], X[:, t, :])
            ch(last)
            for t in range(NT):
                last = dve.bn_aggr(mv[:, t, :], st_all[:, t, :])
            ch(last)
            dve.tensor_scalar(rstd[:, :], mv[:, :, 1], LN_EPS, None, ALU.add).then_inc(s_stat, 1)
            dve.wait_ge(s_pow, 1)
            c2 = Chain(dve, s_set2, 2, 0)
            dve.scalar_tensor_tensor(nmr[:, :], mv[:, :, 0], -1.0, rstd[:, :], ALU.mult, ALU.mult)
            c2(dve.tensor_tensor(rrms[:, :], rstd[:, :], rstd[:, :], ALU.mult))
            c2(dve.tensor_tensor(rrms[:, :], rrms[:, :], mv[:, :, 1], ALU.mult))
            dve.tensor_scalar(rrms[:, :], rrms[:, :], RMS_EPS, None, ALU.add).then_inc(s_stat, 1)
            dve.wait_ge(s_pow, 2)

            def normalize(half, p):
                t = 2 * half + p
                c = Chain(dve, s_nchain, 1, t)
                after(dve, s_tr, t - 1)
                after(dve, s_xr[p], 16 * half)
                for j in range(TB):
                    n = t * TB + j
                    last = dve.tensor_scalar(xn_t[p][:, j:j + 1, :], X[:, bass.ds(n, 1), :],
                                             mv[:, bass.ds(n, 1), 0], rstd[:, bass.ds(n, 1)],
                                             ALU.subtract, ALU.mult)
                c(last)
                for j in range(TB):
                    n = t * TB + j
                    last = dve.scalar_tensor_tensor(xr_t[p][:, j, :], xn_t[p][:, j, :], rrms[:, bass.ds(n, 1)],
                                                    scale_b[:, :], ALU.mult, ALU.mult)
                last.then_inc(s_norm, 1)
                c.end()

            def mix(t, p):
                dve.wait_ge(s_prevmix, t + 1)
                dve.wait_ge(s_xnT, t + 1)
                after(dve, s_kvr, t - 1)
                for j in range(3):
                    last = dve.scalar_tensor_tensor(mixed[p][:, j, :], xnT[p][:, 1:SEQ + 1], cols[:, 2 + j:3 + j],
                                                    prevmix[p][:, j, :], ALU.mult, ALU.add)
                last.then_inc(s_mix, 1)

            def route(t, p):
                c = Chain(dve, s_rchain, 3, t)
                dve.wait_ge(s_dist, t + 1)
                for j in range(TB):
                    last = dve.tensor_tensor(nd[p][:, j, :], psD[:, NE * j:NE * j + NE],
                                             nny[:, :], ALU.add)
                c(last)
                apart(dve)
                for j in range(TB):
                    last = dve.max(best[:, j, :], nd[p][:, j, :])
                c(last)
                apart(dve)
                for j in range(TB):
                    last = dve.max_index(besti[:, j, :], best[:, j, :], nd[p][:, j, :])
                c(last)
                for j in range(TB):
                    last = dve.tensor_scalar(onehot[:, bass.ds(t * TB + j, 1), :], iota8[:, :],
                                             besti[:, j, 0:1], None, ALU.is_equal)
                last.then_inc(s_route, 1)
                c.end()

            def wkv_exponents(t, p):
                dve.wait_ge(s_kv, t + 1)
                k = kv[p][:, 0, :]
                c = Chain(dve, s_wkv, 7, t)
                c(dve.tensor_tensor_scan(pp[:, 1:SEQ + 1], decay[:, :], k, NEG_INF, ALU.add, ALU.max))
                dve.scalar_tensor_tensor(dcarry[:, :], pp[:, 0:SEQ], cols[:, 0:1], k, ALU.add, ALU.subtract)
                c(dve.scalar_tensor_tensor(dout[:, :], k, cols[:, 1:2], pp[:, 0:SEQ], ALU.add, ALU.subtract))
                dve.tensor_scalar(args[:, 0, :], dcarry[:, :], 0.0, None, ALU.min)
                dve.tensor_scalar(args[:, 1, :], dcarry[:, :], 0.0, -1.0, ALU.max, ALU.mult)
                dve.tensor_scalar(args[:, 2, :], dout[:, :], 0.0, None, ALU.min)
                dve.tensor_scalar(args[:, 3, :], dout[:, :], 0.0, -1.0, ALU.max, ALU.mult).then_inc(s_args, 1)
                return c

            def wkv_scans(t, p, c):
                dve.wait_ge(s_ex, t + 1)
                v = kv[p][:, 1, :]
                dve.tensor_tensor(ev[:, 0, :], ex[:, 1, :], v, ALU.mult)
                dve.tensor_tensor(ev[:, 1, :], ex[:, 2, :], v, ALU.mult)
                c(dve.tensor_tensor_scan(bb[:, 1:SEQ + 1], ex[:, 0, :], ex[:, 1, :], 0.0, ALU.mult, ALU.add))
                dve.tensor_tensor_scan(aa[:, 1:SEQ + 1], ex[:, 0, :], ev[:, 0, :], 0.0, ALU.mult, ALU.add)
                c(dve.tensor_tensor(den[:, :], ex[:, 3, :], bb[:, 0:SEQ], ALU.mult))
                dve.scalar_tensor_tensor(den[:, :], den[:, :], WKV_EPS, ex[:, 2, :], ALU.add, ALU.add)
                c(dve.tensor_tensor(num[:, :], ex[:, 3, :], aa[:, 0:SEQ], ALU.mult))
                dve.tensor_tensor(num[:, :], num[:, :], ev[:, 1, :], ALU.add)
                c(dve.reciprocal(den[:, :], den[:, :]))
                dve.wait_ge(s_th, t + 1)
                after(dve, s_so, t - 1)
                c(dve.scalar_tensor_tensor(num[:, :], rtanh[p][:, :], 1.0, num[:, :], ALU.add, ALU.mult))
                dve.tensor_tensor(rwkv[p][:, :], num[:, :], den[:, :], ALU.mult).then_inc(s_rwkv, 1)
                c.end()

            normalize(0, 0)
            normalize(0, 1)
            mix(0, 0)

            def step(t, p, more=True):
                c = wkv_exponents(t, p)
                if more:
                    mix(t + 1, 1 - p)
                route(t, p)
                wkv_scans(t, p, c)
            step(0, 0)
            def two_batches(pair):
                i = 2 * pair + 1
                normalize(pair + 1, 0)
                step(i, 1)
                normalize(pair + 1, 1)
                step(i + 1, 0)
            two_batches(0)
            with dve.Fori(1, B // 2 - 1) as pair:
                two_batches(pair)
            step(B - 1, 1, more=False)


        @block.scalar
        def _(act):
            act.wait_ge(s_cent, 1)
            act.wait_ge(s_setv, 1)

            def transposed(t, p):
                act.wait_ge(s_tr, t + 1)
                after(act, s_mix, t - 1)
                after(act, s_dist, t - 1)
                after(act, s_xrsq, t - 1)
                act.copy(xnT[p][:, 1:SEQ + 1], psT[p][:, 0:SEQ]).then_inc(s_xnT, 1)
                act.copy(xrT[p][:, :], psT[p][:, SEQ:2 * SEQ]).then_inc(s_xrT, 1)
                act.wait_ge(s_xnT, t + 1)
                for j in range(3):
                    last = act.activation(prevmix[p][:, j, :], xnT[p][:, 0:SEQ], ACT.Copy, scale=ommix[:, j:j + 1])
                last.then_inc(s_prevmix, 1)

            def gates(t, p):
                act.wait_ge(s_kvr, t + 1)
                after(act, s_rwkv, t - 1)
                act.copy(kv[p][:, :, :], psKV[p][:, :].rearrange("p (a n) -> p a n", a=2)).then_inc(s_kv, 1)
                act.activation(rtanh[p][:, :], psR[p][:, 0:SEQ], ACT.Tanh, scale=0.5).then_inc(s_th, 1)

            def exps(t, p):
                act.wait_ge(s_args, t + 1)
                act.activation(ex[:, :, :], args[:, :, :], ACT.Exp).then_inc(s_ex, 1)

            def store(t, p):
                act.wait_ge(s_so, t + 1)
                act.copy(S[:, bass.ds(t * TB, TB), :],
                         psO[:, 0:TB * D].rearrange("p (a n) -> p a n", a=TB)).then_inc(s_s, 1)

            transposed(0, 0)
            gates(0, 0)
            transposed(1, 1)
            exps(0, 0)
            gates(1, 1)
            def two_batches(pair):
                i = 2 * pair + 1
                transposed(i + 1, 0)
                exps(i, 1)
                store(i - 1, 0)
                gates(i + 1, 0)
                transposed(i + 2, 1)
                exps(i + 1, 0)
                store(i, 1)
                gates(i + 2, 1)
            two_batches(0)
            with act.Fori(1, B // 2 - 1) as pair:
                two_batches(pair)
            exps(B - 1, 1)
            store(B - 2, 0)
            store(B - 1, 1)

        @block.tensor
        def _(pe):
            pe.wait_ge(s_const, 2)
            pe.wait_ge(s_cent, 1)
            pe.matmul(PS[7][:, 0:NE], neg1[:, :], cTsq[:, :], start=True, stop=True).then_inc(s_cent, 1)
            pe.wait_ge(s_setv, 1)

            def flip(t, p):
                pe.wait_ge(s_norm, t + 1)
                after(pe, s_xrT, t - 1)
                for j in range(TB):
                    for k, src in enumerate((xn_t[p], xr_t[p])):
                        last = pe.transpose(psT[p][:, k * SEQ + j * P:k * SEQ + (j + 1) * P], src[:, j, :],
                                            ident[:, :])
                last.then_inc(s_tr, 1)

            def project(t, p):
                pe.wait_ge(s_mix, t + 1)
                after(pe, s_th, t - 1)
                pe.matmul(psKV[p][:, 0:SEQ], w0[:, 0, :], mixed[p][:, 0, :], start=True, stop=True)
                pe.matmul(psKV[p][:, SEQ:], w0[:, 1, :], mixed[p][:, 1, :], start=True, stop=True)
                pe.matmul(psR[p][:, 0:SEQ], w0[:, 2, :], mixed[p][:, 2, :], start=True, stop=True).then_inc(s_kvr, 1)

            def distances(t, p):
                pe.wait_ge(s_xrsq, t + 1)
                after(pe, s_route, t)
                for j in range(TB):
                    o = psD[:, NE * j:NE * j + NE]
                    pe.matmul(o, xrT[p][:, j * P:(j + 1) * P], cT2[:, :], start=True, stop=False)
                    last = pe.matmul(o, xrTsq[p][:, j * P:(j + 1) * P], neg1[:, 0:NE], start=False, stop=True)
                last.then_inc(s_dist, 1)

            def out_projection(t, p):
                pe.wait_ge(s_rwkv, t + 1)
                after(pe, s_s, t)
                for j in range(TB):
                    last = pe.matmul(psO[:, j * D:(j + 1) * D], rwkv[p][:, j * P:(j + 1) * P], w0[:, 3, :],
                                     start=True, stop=True)
                last.then_inc(s_so, 1)

            flip(0, 0)
            project(0, 0)
            distances(0, 0)
            flip(1, 1)
            project(1, 1)
            distances(1, 1)
            def two_batches(pair):
                i = 2 * pair + 1
                flip(i + 1, 0)
                out_projection(i - 1, 0)
                project(i + 1, 0)
                distances(i + 1, 0)
                flip(i + 2, 1)
                out_projection(i, 1)
                project(i + 2, 1)
                distances(i + 2, 1)
            two_batches(0)
            with pe.Fori(1, B // 2 - 1) as pair:
                two_batches(pair)
            out_projection(B - 2, 0)
            out_projection(B - 1, 1)

        e1.close()
        sort_and_experts(nc, onehot, earlier, ones, iota_t, ident, slot, tile_expert, XR, up, down, PS, xs_dram,
                         ys_dram)
        e2.close()
        layer_one(nc, X, S, mv, rstd, nmr, slot, ident, ones, mhalf, zero_tile, PS, ys_dram, parts_dram, mrow_dram, l1_w, out_b,
                  qkv_w, qkv_b, wr, br, wo, bo, out)


def sort_and_experts(nc, onehot, earlier, ones, iota_t, ident, slot, tile_expert, XR, up, down, PS, xs_dram,
                     ys_dram):
    with ExitStack() as ctx:
        def sb(name, shape, dt=fp32):
            return ctx.enter_context(nc.sbuf_tensor(name, shape, dt))

        def sem(name):
            return ctx.enter_context(nc.semaphore(name))

        tot = sb("tot", [P, NT, NE])
        cum = sb("cum", [P, NT, NE])
        rank = sb("rank", [P, NT, NE])
        over = sb("over", [P, NE, NT])
        thresholds = sb("thresholds", [P, NT])
        ntiles = sb("ntiles", [P, NE])
        end = sb("end", [P, NE])
        first = sb("first", [P, NE])
        past = sb("past", [P, NST, NE])
        slot_f = sb("slot_f", [P, NT])
        te_f = sb("te_f", [P, NST])
        xs_t = [sb(f"xs_t{i}", [P, D]) for i in range(2)]
        xsT = [sb(f"xsT{i}", [P, P]) for i in range(2)]
        gate = [sb(f"gate{i}", [P, HID]) for i in range(2)]
        hid = [sb(f"hid{i}", [P, HID]) for i in range(2)]
        hidT = [sb(f"hidT{i}", [P, 2, P]) for i in range(2)]
        ys_t = [sb(f"ys_t{i}", [P, D]) for i in range(2)]

        s_counts = sem("counts_in_psum")
        s_place = sem("place_chain")
        s_placed = sem("slots_ready")
        s_scat = sem("tokens_scattered")
        s_xs = [sem(f"xs_loaded{i}") for i in range(2)]
        s_fx = sem("xs_transposed")
        s_xsT = sem("xsT_ready")
        s_up = sem("hidden_in_psum")
        s_gate = sem("gate_tanh_ready2")
        s_gch = sem("gate_chain")
        s_hid = sem("hidden_ready")
        s_fh = sem("hidden_transposed")
        s_hidT = sem("hidT_ready")
        s_dn = sem("expert_out_in_psum")
        s_y = sem("expert_out_ready")
        s_ys = [sem(f"expert_out_stored{i}") for i in range(2)]
        s_back = sem("gathered_back")
        psX, psU, psH, psY = PS[0:2], PS[2:4], PS[4:6], PS[6:8]

        def lag(half, p, k):
            h, q = half + (p - k) // 2, (p - k) % 2
            return 2 * h + q, h, q

        def run(eng, step):
            for t in range(6):
                step(t // 2, t % 2)
            with eng.Fori(3, NST // 2) as half:
                step(half, 0)
                step(half, 1)
            for t in range(NST, NST + 3):
                step(t // 2, t % 2)

        def runs(t):
            return not isinstance(t, int) or 0 <= t < NST

        block = ctx.enter_context(nc.Block())

        @block.gpsimd
        def _(pool):
            pool.wait_ge(s_placed, 1)
            for t in range(NT):
                pool.indirect_dma_start(xs_dram, bass.IndirectOffsetOnAxis(slot[:, t:t + 1], axis=0),
                                        XR[:, t, :], None).then_inc(s_scat, 16)
            pool.wait_ge(s_scat, 16 * NT)

        @block.sync
        def _(sp):
            sp.wait_ge(s_scat, 16 * NT)

            def load(half, p):
                t = 2 * half + p
                if runs(t):
                    after(sp, s_fx, t - 1)
                    apart(sp)
                    sp.dma_start(xs_t[p][:, :], xs_dram[bass.ds(t * P, P), :]).then_inc(s_xs[p], 16)

            def store(half, p):
                t, h, q = lag(half, p, 3)
                if runs(t):
                    sp.wait_ge(s_y, t + 1)
                    apart(sp)
                    sp.dma_start(ys_dram[bass.ds(t * P, P), :], ys_t[q][:, :]).then_inc(s_ys[q], 16)

            load(0, 0)
            load(0, 1)

            def step(half, p):
                t = 2 * half + p
                if not isinstance(t, int) or t + 2 < NST:
                    load(half + 1, p)
                store(half, p)
            for t in range(6):
                step(t // 2, t % 2)
            with sp.Fori(3, NST // 2 - 1) as half:
                step(half, 0)
                step(half, 1)
            for t in range(NST - 2, NST + 3):
                step(t // 2, t % 2)
            for p in range(2):
                sp.wait_ge(s_ys[p], 16 * (NST // 2))

        @block.vector
        def _(dve):
            ch = Chain(dve, s_place, 12, 0)
            dve.tensor_scalar(thresholds[:, :], iota_t[:, 0:NT], float(P), None, ALU.mult)
            dve.wait_ge(s_counts, 1)
            ch(dve.tensor_copy(tot[:, :, :], PS[1][:, :].rearrange("p (t e) -> p t e", e=NE)))
            for e in range(NE):
                last = dve.tensor_tensor_scan(cum[:, :, e], ones[:, 0:NT], tot[:, :, e], 0.0, ALU.mult, ALU.add)
            ch(last)
            ch(dve.tensor_tensor(over[:, :, :], cum[:, NT - 1, :].unsqueeze(2).broadcast_to([P, NE, NT]),
                                 thresholds[:, :].unsqueeze(1).broadcast_to([P, NE, NT]), ALU.is_gt))
            ch(dve.tensor_reduce(ntiles[:, :], over[:, :, :], AX.X, ALU.add))
            ch(dve.tensor_tensor_scan(end[:, :], ones[:, 0:NE], ntiles[:, :], 0.0, ALU.mult, ALU.add))
            ch(dve.tensor_tensor(first[:, :], end[:, :], ntiles[:, :], ALU.subtract))
            dve.tensor_tensor(cum[:, :, :], cum[:, :, :], tot[:, :, :], ALU.subtract)
            ch(dve.tensor_scalar(first[:, :], first[:, :], float(P), None, ALU.mult))
            ch(dve.tensor_tensor(rank[:, :, :], PS[0][:, :].rearrange("p (t e) -> p t e", e=NE), cum[:, :, :], ALU.add))
            ch(dve.tensor_tensor(rank[:, :, :], rank[:, :, :], first[:, :].unsqueeze(1).broadcast_to([P, NT, NE]), ALU.add))
            dve.tensor_tensor(past[:, :, :], iota_t[:, :].unsqueeze(2).broadcast_to([P, NST, NE]),
                              end[:, :].unsqueeze(1).broadcast_to([P, NST, NE]), ALU.is_ge)
            ch(dve.tensor_tensor(rank[:, :, :], rank[:, :, :], onehot[:, :, :], ALU.mult))
            dve.tensor_reduce(te_f[:, :], past[:, :, :], AX.X, ALU.add)
            ch(dve.tensor_reduce(slot_f[:, :], rank[:, :, :], AX.X, ALU.add))
            ch(dve.tensor_scalar(te_f[:, :], te_f[:, :], float(NE - 1), None, ALU.min))
            ch.end()
            dve.tensor_copy(tile_expert[:, :], te_f[:, :])
            dve.tensor_copy(slot[:, :], slot_f[:, :]).then_inc(s_placed, 1)

            def step(half, p):
                t, h, q = lag(half, p, 1)
                if runs(t):
                    c = Chain(dve, s_gch, 1, t)
                    dve.wait_ge(s_gate, t + 1)
                    after(dve, s_fh, t - 1)
                    c(dve.scalar_tensor_tensor(gate[q][:, :], gate[q][:, :], 1.0, psU[q][:, HID:], ALU.add, ALU.mult))
                    dve.tensor_tensor(hid[q][:, :], psU[q][:, 0:HID], gate[q][:, :], ALU.mult).then_inc(s_hid, 1)
                    c.end()
                t, h, q = lag(half, p, 3)
                if runs(t):
                    dve.wait_ge(s_dn, t + 1)
                    after(dve, s_ys[q], 16 * h)
                    dve.tensor_scalar(ys_t[q][:, :], psY[q][:, 0:D], 0.5, None, ALU.mult).then_inc(s_y, 1)
            run(dve, step)

        @block.scalar
        def _(act):
            def step(half, p):
                t, h, q = lag(half, p, 0)
                if runs(t):
                    act.wait_ge(s_fx, t + 1)
                    after(act, s_up, t - 1)
                    act.copy(xsT[q][:, :], psX[q][:, 0:P]).then_inc(s_xsT, 1)
                t, h, q = lag(half, p, 1)
                if runs(t):
                    act.wait_ge(s_up, t + 1)
                    after(act, s_hid, t - 1)
                    act.activation(gate[q][:, :], psU[q][:, HID:], ACT.Tanh, scale=0.5).then_inc(s_gate, 1)
                t, h, q = lag(half, p, 2)
                if runs(t):
                    act.wait_ge(s_fh, t + 1)
                    after(act, s_dn, t - 1)
                    act.copy(hidT[q][:, :, :], psH[q][:, 0:2 * P].rearrange("p (c n) -> p c n", c=2)).then_inc(s_hidT, 1)
            run(act, step)

        @block.tensor
        def _(pe):
            pe.matmul(PS[0][:, :], earlier[:, :], onehot[:, :, :].rearrange("p t e -> p (t e)"), start=True, stop=True)
            pe.matmul(PS[1][:, :], ones[:, 0:P], onehot[:, :, :].rearrange("p t e -> p (t e)"),
                      start=True, stop=True).then_inc(s_counts, 1)
            pe.wait_ge(s_placed, 1)

            def step(half, p):
                t, h, q = lag(half, p, 0)
                if runs(t):
                    pe.wait_ge(s_xs[q], 16 * h + 16)
                    after(pe, s_xsT, t - 1)
                    pe.transpose(psX[q][:, 0:P], xs_t[q][:, :], ident[:, :]).then_inc(s_fx, 1)
                t, h, q = lag(half, p, 2)
                if runs(t):
                    pe.wait_ge(s_hid, t + 1)
                    after(pe, s_hidT, t - 1)
                    for c in range(2):
                        last = pe.transpose(psH[q][:, c * P:(c + 1) * P], hid[q][:, c * P:(c + 1) * P], ident[:, :])
                    last.then_inc(s_fh, 1)
                t, h, q = lag(half, p, 1)
                if runs(t):
                    e = pe.value_load(tile_expert[0:1, bass.ds(t, 1)], min_val=0, max_val=NE - 1)
                    pe.wait_ge(s_xsT, t + 1)
                    after(pe, s_hid, t - 1)
                    pe.matmul(psU[q][:, :], xsT[q][:, :], up[:, bass.ds(e * 2 * HID, 2 * HID)],
                              start=True, stop=True).then_inc(s_up, 1)
                t, h, q = lag(half, p, 3)
                if runs(t):
                    e = pe.value_load(tile_expert[0:1, bass.ds(t, 1)], min_val=0, max_val=NE - 1)
                    pe.wait_ge(s_hidT, t + 1)
                    after(pe, s_y, t - 1)
                    for c in range(2):
                        last = pe.matmul(psY[q][:, 0:D], hidT[q][:, c, :], down[:, bass.ds(e * 2 * D + c * D, D)],
                                         start=(c == 0), stop=(c == 1))
                    last.then_inc(s_dn, 1)
            run(pe, step)


def layer_one(nc, X, S, mv, rstd, nmr, slot, ident, ones, mhalf, zero_tile, PS, ys_dram, parts_dram, mrow_dram, l1_w, out_b,
              qkv_w, qkv_b, wr, br, wo, bo, out):
    with ExitStack() as ctx:
        def sb(name, shape, dt=fp32):
            return ctx.enter_context(nc.sbuf_tensor(name, shape, dt))

        def two(name, shape, dt=fp32):
            return [sb(f"{name}{i}", shape, dt) for i in range(2)]

        def sem(name):
            return ctx.enter_context(nc.semaphore(name))

        def sem2(name):
            return [sem(f"{name}{i}") for i in range(2)]

        NP3 = 3
        ROWS = [(0, 0), (0, 1), (0, 2), (1, 0), (1, 1), (2, 0)]
        MROW = 96
        VC = 32
        SS, CS, NS = 2, 5, 22

        identb = sb("identb", [P, P], bf16)
        w1 = sb("w1", [P, 4, D])
        outb_b = sb("outb_b", [P, D])
        bo_b = sb("bo_b", [P, D])
        br_b = sb("br_b", [P, RH])
        wr_s = sb("wr_s", [P, RH])
        wo_s = sb("wo_s", [P, 2, D])
        zerob = sb("zerob", [NP3, H * SEQ], bf16)
        Y = two("Y", [P, TB, D])
        slot_t = two("slot_t", [P, TB], i32)
        xnf = two("xnf", [P, TB, D])
        z = two("z", [P, TB, D])
        zt = two("zt", [P, TB, D])
        st = sb("st", [P, TB, 6])
        mva = sb("mva", [P, TB, 2])
        rs = sb("rs", [P, TB])
        xn1 = two("xn1", [P, TB, D])
        xT = two("xT", [P, SEQ])
        qk = sb("qk", [P, 2, SEQ])
        rest = sb("rest", [P, 2, SEQ])
        parts = two("parts", [P, 2, NP3, SEQ], bf16)
        xsum = sb("xsum", [P, 1])
        xsb = sb("xsb", [P, P])
        lg = sb("lg", [P, RH])
        top = sb("top", [P, 8])
        ntop = sb("ntop", [P, 1])
        prob = sb("prob", [P, RH])
        psum_ = sb("prob_sum", [P, 1])
        pinv = sb("prob_inv", [P, 1])
        ptop = sb("ptop", [P, 8])
        pidx = sb("pidx", [P, 8], u32)
        idx = two("idx", [1, 8], i32)
        nptop = sb("nptop", [P, 1])
        g5 = sb("g5", [P, RK + 1])
        gsum = sb("gsum", [P, 1])
        g4 = sb("g4", [P, RK])
        gc = two("gc", [P, 2, 3])
        QS = two("QS", [P, H, SEQ], bf16)
        KS = two("KS", [P, H, SEQ], bf16)
        bm = sb("bm", [P, TB, H, NBLK])
        m3 = sb("m3", [P, TB, H])
        nm = sb("nm", [P, TB, H])
        nmr_ = sb("nm_rest", [P, TB, H])
        cdiff = sb("cdiff", [P, TB, H])
        corr = sb("corr", [P, TB, H])
        fac = two("fac", [P, TB, H])
        mp = sb("mp", [P, TB, NP3, H], bf16)
        mT = two("mT", [NP3 * H, SEQ], bf16)
        V2 = two("V2", [P, TB, H, VC])
        wsel = two("wsel", [P, 2, 3, P])
        bsel = two("bsel", [P, 2, 3])
        gb = two("gb", [P, 2, 3])
        Qf = sb("Qf", [P, 2, SEQ])
        Kz = sb("Kz", [P, 2, 2, SEQ])
        Vf = sb("Vf", [P, TB, RK * RD])
        nmf = sb("nmf", [P, TB])
        Pf = sb("Pf", [P, TB, SEQ])
        lsum = sb("lsum", [P, TB, RK])
        linv = sb("linv", [P, TB * RK])
        PTf = sb("PTf", [P, TB, SEQ])
        On = sb("On", [P, TB * RK, RD])
        PT = [sb(f"PT{i}", [P, TB * SEQ]) for i in range(8)]
        OT = two("OT", [P, SEQ])
        lf = sb("lf", [P, TB, 4])
        attn = two("attn", [P, TB, H, HD])
        attnT = sb("attnT", [P, SEQ])
        OTf = sb("OTf", [P, 2, SEQ])
        y2 = sb("y2", [P, TB, D])
        y2t = sb("y2t", [P, TB, D])
        g2 = two("g2", [P, TB, D])
        s1 = sb("s1", [P, TB, D])
        o_t = two("o_t", [P, TB, D])

        s_w = sem("l1_weights")
        s_c0 = sem("l1_consts_pool")
        s_c1 = sem("l1_consts_dve")
        s_slot = sem("slots_copied")
        s_fac = sem("factor_ready")
        s_g2 = sem("gate_two_ready")
        s_gch = sem("gate_chain3")
        s_y = sem2("expert_out_gathered")
        s_xnf = sem("xn_ready")
        s_z = sem("z_ready")
        s_zt = sem("z_tanh_ready")
        s_gz = sem("z_gated")
        s_x1c = sem("x1_chain")
        s_x1 = sem("x1_ready")
        s_lnc = sem("ln_chain")
        s_ve = sem("x1_variance_ready")
        s_rs = sem("x1_rstd_ready")
        s_xn1 = sem("xn1_ready")
        s_f1 = sem("x1_transposed")
        s_xT = sem("xT_ready")
        s_qkp = sem("qk_in_psum")
        s_qk = sem("qk_ready")
        s_hi = sem("qk_high_ready")
        s_spc = sem("split_chain")
        s_parts = sem("parts_ready")
        s_pst = sem2("parts_stored")
        s_xsc = sem("xsum_chain")
        s_xsb = sem("xsum_ready")
        s_lgp = sem("logits_in_psum")
        s_lgc = sem("router_chain")
        s_lg = sem("logits_read")
        s_lg2 = sem("logit_max_ready")
        s_pe1 = sem("probs_exp_ready")
        s_pt = sem("prob_top_ready")
        s_pe2 = sem("gates_exp_ready")
        s_idx = sem("heads_chosen")
        s_gc = sem("gates_ready")
        s_wl = sem2("head_weights_loaded")
        s_ql = sem2("qs_ks_loaded")
        s_sp = sem("scores_in_psum")
        s_red = sem("block_maxima_read")
        s_mc = sem("max_chain")
        s_cd = sem("max_difference_ready")
        s_corr = sem("correction_ready")
        s_mp = sem("max_parts_ready")
        s_mTp = sem("max_transposed")
        s_mT = sem("mT_ready")
        s_ms = sem2("max_rows_stored")
        s_ml = sem2("max_rows_loaded")
        s_vp = sem("v_in_psum")
        s_v2 = sem("V2_ready")
        s_gb = sem("head_biases_ready")
        s_fqp = sem("head_qk_in_psum")
        s_fq = sem("head_qk_ready")
        s_fvp = sem("head_v_in_psum")
        s_fv = sem("head_v_ready")
        s_fs = sem("head_scores_in_psum")
        s_fm = sem("head_max_ready")
        s_pf = sem("head_probs_ready")
        s_ptp = sem("head_probs_transposed")
        s_ptf = sem("head_PT_ready")
        s_of = sem("head_out_in_psum")
        s_ofc = sem("head_out_chain")
        s_on = sem("head_out_ready")
        s_otp = sem("head_out_transposed")
        s_otf = sem("head_OT_ready")
        s_wop = sem("routed_out_in_psum")
        s_y2 = sem("routed_out_ready")
        s_y2t = sem("routed_tanh_ready")
        s_st = sem("shifted_scores_in_psum")
        s_exp = sem("exp_scores_ready")
        s_pv = sem("values_in_psum")
        s_oe = sem("OT_ready")
        s_ot = sem("O_transposed")
        s_nc = sem("norm_chain3")
        s_an = sem("attn_normalized")
        s_atp = sem("attn_transposed")
        s_at = sem("attnT_ready")
        s_op = sem("attn_out_in_psum")
        s_fc = sem("final_chain")
        s_fin = sem("attn_out_read")
        s_done = sem("out_ready")
        s_out = sem2("out_stored")

        bS, bT, bC, bA, bF1, bF2 = PS[0:2], PS[2:4], PS[4], PS[5], PS[6], PS[7]
        bAb = bA[:, :].bitcast(bf16)

        def lag(half, p, k):
            h, q = half + (p - k) // 2, (p - k) % 2
            return 2 * h + q, h, q

        def runs(t):
            return not isinstance(t, int) or 0 <= t < B

        def run(eng, step):
            for t in range(6):
                step(t // 2, t % 2)
            with eng.Fori(3, B // 2) as half:
                step(half, 0)
                step(half, 1)
            for t in range(B, B + 3):
                step(t // 2, t % 2)

        def most(t):
            return min(t, B) if isinstance(t, int) else t

        def tiles(t):
            return bass.ds(t * TB, TB)

        block = ctx.enter_context(nc.Block())

        @block.sync
        def _(sp):
            for dst, src in ((w1[:, :, :], l1_w), (outb_b[:, :], out_b.to_broadcast([P, D])),
                             (bo_b[:, :], bo.to_broadcast([P, D])), (br_b[:, :], br.to_broadcast([P, RH])),
                             (wr_s[:, :], wr), (wo_s[:, :, :], wo)):
                sp.dma_start(dst, src).then_inc(s_w, 16)
            sp.wait_ge(s_c1, 2)

            def load_qk(t, h, q):
                sp.wait_ge(s_pst[q], 16 * h + 16)
                apart(sp)
                after(sp, s_st, H * (t - 1))
                apart(sp)
                for r, parts_of in enumerate(ROWS):
                    for k, tile in enumerate((QS[q], KS[q])):
                        src = parts_dram[q, k, parts_of[k]].rearrange("(h d) t -> d h t", d=HD)
                        sp.dma_start(tile[r * HD:(r + 1) * HD, :, :], src).then_inc(s_ql[q], 16)
                sp.dma_start(QS[q][MROW:MROW + NP3, :, :].rearrange("p h t -> p (h t)"), zerob[:, :]).then_inc(s_ql[q], 16)

            def load_max(t, h, q):
                sp.wait_ge(s_mT, t + 1)
                apart(sp)
                sp.wait_ge(s_sp, H * (t + 1))
                apart(sp)
                sp.dma_start(mrow_dram[q].rearrange("a h t -> (a h) t"), mT[q][:, :]).then_inc(s_ms[q], 16)
                sp.wait_ge(s_ms[q], 16 * h + 16)
                apart(sp)
                sp.dma_start(QS[q][MROW:MROW + NP3, :, :], mrow_dram[q]).then_inc(s_ml[q], 16)

            def load_heads(t, h, q):
                sp.wait_ge(s_idx, t + 1)
                apart(sp)
                after(sp, s_fv, t - 1)
                apart(sp)
                after(sp, s_gb, t - 1)
                apart(sp)
                for j in range(RK):
                    head = sp.value_load(idx[q][0:1, j:j + 1], min_val=0, max_val=RH - 1)
                    i, jj = j // 2, j % 2
                    sp.dma_start(wsel[q][:, i, :, jj * RD:(jj + 1) * RD],
                                 qkv_w[bass.ds(head, 1), :, :, :].rearrange("a p c d -> (a p) c d")).then_inc(s_wl[q], 16)
                    sp.dma_start(bsel[q][jj * RD:(jj + 1) * RD, i, :],
                                 qkv_b[bass.ds(head, 1), :, :].rearrange("a d c -> (a d) c")).then_inc(s_wl[q], 16)

            def store_parts(t, h, q):
                sp.wait_ge(s_parts, t + 1)
                apart(sp)
                after(sp, s_ql[q], 16 * 13 * h)
                apart(sp)
                sp.dma_start(parts_dram[q].rearrange("k a p t -> p k a t"), parts[q][:, :, :, :]).then_inc(s_pst[q], 16)

            def step(half, p):
                a, b, c, d = (lag(half, p, k) for k in range(4))
                if runs(b[0]):
                    load_qk(*b)
                if runs(c[0]):
                    load_max(*c)
                if runs(d[0]):
                    t, h, q = d
                    sp.wait_ge(s_done, t + 1)
                    apart(sp)
                    sp.dma_start(out[bass.ds(t * SEQ, SEQ), :].rearrange("(j p) n -> p j n", p=P),
                                 o_t[q][:, :, :]).then_inc(s_out[q], 16)
                if runs(a[0]):
                    store_parts(*a)
                    load_heads(*a)
            run(sp, step)
            for q in range(2):
                sp.wait_ge(s_out[q], 16 * (B // 2))

        @block.gpsimd
        def _(pool):
            pool.memset(zerob[:, :], 0.0)
            for i in range(2):
                pool.memset(QS[i][:, :, :], 0.0)
                pool.memset(KS[i][:, :, :], 0.0)
                pool.memset(V2[i][:, :, :, :], 0.0)
            pool.memset(Kz[:, :, :, :], 0.0).then_inc(s_c0, 1)
            pool.wait_ge(s_c0, 1)
            pool.tensor_copy(identb[:, :], ident[:, :]).then_inc(s_c1, 1)

            def gather(t, h, q):
                after(pool, s_z, t - 1)
                apart(pool)
                for j in range(TB):
                    pool.indirect_dma_start(Y[q][:, j, :], None, ys_dram,
                                            bass.IndirectOffsetOnAxis(slot_t[q][:, j:j + 1], axis=0)).then_inc(s_y[q], 16)

            def step(half, p):
                t, h, q = lag(half, p, 0)
                if not runs(t):
                    return
                pool.tensor_copy(slot_t[q][:, :], slot[:, tiles(t)]).then_inc(s_slot, 1)
                pool.wait_ge(s_slot, t + 1)
                gather(t, h, q)
                pool.wait_ge(s_y[q], 32 * h + 32)
                pool.wait_ge(s_xnf, t + 1)
                after(pool, s_gz, t - 1)
                pool.tensor_tensor(z[q][:, :, :], Y[q][:, :, :], xnf[q][:, :, :], ALU.add).then_inc(s_z, 1)
                pool.wait_ge(s_gz, t + 1)
                ch = Chain(pool, s_x1c, 1, t)
                ch(pool.tensor_tensor(zt[q][:, :, :], zt[q][:, :, :], S[:, tiles(t), :], ALU.mult))
                ch.end()
                pool.tensor_tensor(X[:, tiles(t), :], X[:, tiles(t), :], zt[q][:, :, :], ALU.add).then_inc(s_x1, 1)
                pool.wait_ge(s_ve, t + 1)
                pool.tensor_tensor(rs[:, :], rs[:, :], mhalf[:, 0:TB], ALU.pow).then_inc(s_rs, 1)
                ch = Chain(pool, s_spc, 2, t)
                pool.wait_ge(s_hi, t + 1)
                ch(pool.tensor_tensor(rest[:, :, :], qk[:, :, :], parts[q][:, :, 0, :], ALU.subtract))
                apart(pool)
                ch(pool.tensor_copy(parts[q][:, :, 1, :], rest[:, :, :]))
                pool.tensor_tensor(parts[q][:, :, 2, :], rest[:, :, :], parts[q][:, :, 1, :], ALU.subtract).then_inc(s_parts, 1)
                ch.end()
            run(pool, step)

        @block.vector
        def _(dve):
            dve.wait_ge(s_w, 16 * 6)
            dve.wait_ge(s_c0, 1)
            for i in range(2):
                dve.memset(KS[i][MROW:MROW + NP3, :, :], 1.0)
                last = dve.memset(V2[i][P - BLK:P, TB - 1, :, HD:HD + 1], 1.0)
            last.then_inc(s_c1, 1)
            dve.wait_ge(s_c1, 2)

            def gated(t, h, q):
                dve.wait_ge(s_zt, t + 1)
                dve.scalar_tensor_tensor(zt[q][:, :, :].rearrange("p j n -> p (j n)"),
                                         zt[q][:, :, :].rearrange("p j n -> p (j n)"), 1.0,
                                         z[q][:, :, :].rearrange("p j n -> p (j n)"), ALU.add, ALU.mult).then_inc(s_gz, 1)

            def ln_stats(t, h, q):
                dve.wait_ge(s_x1, t + 1)
                ch = Chain(dve, s_lnc, 2, t)
                for j in range(TB):
                    last = dve.bn_stats(st[:, j, :], X[:, bass.ds(t * TB + j, 1), :].rearrange("p a n -> p (a n)"))
                ch(last)
                apart(dve)
                for j in range(TB):
                    last = dve.bn_aggr(mva[:, j, :], st[:, j, :])
                ch(last)
                ch.end()
                dve.tensor_scalar(rs[:, :], mva[:, :, 1], LN_EPS, None, ALU.add).then_inc(s_ve, 1)

            def ln_apply(t, h, q):
                dve.wait_ge(s_rs, t + 1)
                after(dve, s_f1, t - 1)
                for j in range(TB):
                    last = dve.tensor_scalar(xn1[q][:, j:j + 1, :], X[:, bass.ds(t * TB + j, 1), :],
                                             mva[:, j, 0:1], rs[:, j:j + 1], ALU.subtract, ALU.mult)
                last.then_inc(s_xn1, 1)

            def token_sum(t, h, q):
                dve.wait_ge(s_xT, t + 1)
                after(dve, s_lgp, t)
                ch = Chain(dve, s_xsc, 1, t)
                ch(dve.tensor_reduce(xsum[:, :], xT[q][:, :], AX.X, ALU.add))
                ch.end()
                dve.tensor_scalar(xsb[:, :], ones[:, 0:P], xsum[:, 0:1], 1.0 / SEQ, ALU.mult, ALU.mult).then_inc(s_xsb, 1)

            def route_a(t, h, q):
                dve.wait_ge(s_lgp, t + 1)
                ch = Chain(dve, s_lgc, 5, t)
                dve.tensor_tensor(lg[:, :], bA[:, 0:RH], br_b[:, :], ALU.add).then_inc(s_lg, 1)
                dve.wait_ge(s_lg, t + 1)
                apart(dve)
                ch(dve.max(top[:, :], lg[:, :]))
                dve.tensor_scalar(ntop[:, :], top[:, 0:1], -1.0, None, ALU.mult).then_inc(s_lg2, 1)
                return ch

            def route_b(t, h, q, ch):
                dve.wait_ge(s_pe1, t + 1)
                ch(dve.reciprocal(pinv[:, :], psum_[:, :]))
                ch(dve.tensor_scalar(prob[:, :], prob[:, :], pinv[:, 0:1], None, ALU.mult))
                apart(dve)
                ch(dve.max(ptop[:, :], prob[:, :]))
                dve.tensor_scalar(nptop[:, :], ptop[:, 0:1], -1.0, None, ALU.mult).then_inc(s_pt, 1)
                apart(dve)
                ch(dve.max_index(pidx[:, :], ptop[:, :], prob[:, :]))
                after(dve, s_wl[q], 128 * h)
                dve.tensor_copy(idx[q][:, :], pidx[0:1, :]).then_inc(s_idx, 1)
                ch.end()

            def route_c(t, h, q):
                dve.wait_ge(s_pe2, t + 1)
                ch = Chain(dve, s_gch, 5, t)
                ch(dve.tensor_reduce(gsum[:, :], g5[:, 0:RK], AX.X, ALU.add))
                ch(dve.scalar_tensor_tensor(gsum[:, :], g5[:, RK:RK + 1], float(RH - RK), gsum[:, :], ALU.mult, ALU.add))
                ch(dve.reciprocal(gsum[:, :], gsum[:, :]))
                ch(dve.tensor_scalar(g4[:, :], g5[:, 0:RK], gsum[:, 0:1], None, ALU.mult))
                g4v = g4[:, :].rearrange("p (i j) -> p i j", j=2)
                for jj in range(2):
                    rows = slice(jj * RD, (jj + 1) * RD)
                    last = dve.tensor_copy(gc[q][rows, :, :], g4v[rows, :, jj:jj + 1].broadcast_to([RD, 2, 3]))
                ch(last)
                ch.end()
                dve.tensor_scalar(gc[q][:, :, 0], gc[q][:, :, 0], RD ** -0.5, None, ALU.mult).then_inc(s_gc, 1)

            def head_biases(t, h, q):
                dve.wait_ge(s_gc, t + 1)
                dve.wait_ge(s_wl[q], 128 * h + 128)
                dve.tensor_tensor(gb[q][:, :, :], bsel[q][:, :, :], gc[q][:, :, :], ALU.mult).then_inc(s_gb, 1)

            def block_max(t, s):
                dve.wait_ge(s_sp, H * t + s + 1)
                qt, h0 = s // 8, 2 * (s % 8)
                dve.tensor_reduce(bm[:, qt, h0:h0 + 2, :],
                                  bS[s % 2][:, :].rearrange("p (h b k) -> p h b k", h=2, b=NBLK), AX.X, ALU.max)\
                   .then_inc(s_red, 1)

            def row_max(t, h, q):
                ch = Chain(dve, s_mc, 6, t)
                dve.wait_ge(s_red, H * (t + 1))
                ch(dve.tensor_reduce(m3[:, :, :], bm[:, :, :, 0:NBLK - 1], AX.X, ALU.max))
                ch(dve.tensor_tensor(nm[:, :, :], m3[:, :, :], bm[:, :, :, NBLK - 1], ALU.max))
                after(dve, s_corr, t)
                dve.tensor_tensor(cdiff[:, :, :], m3[:, :, :], nm[:, :, :], ALU.subtract).then_inc(s_cd, 1)
                ch(dve.tensor_scalar(nm[:, :, :], nm[:, :, :], -1.0, None, ALU.mult))
                after(dve, s_mTp, t)
                ch(dve.tensor_copy(mp[:, :, 0, :], nm[:, :, :]))
                ch(dve.tensor_tensor(nmr_[:, :, :], nm[:, :, :], mp[:, :, 0, :], ALU.subtract))
                ch(dve.tensor_copy(mp[:, :, 1, :], nmr_[:, :, :]))
                dve.tensor_tensor(mp[:, :, 2, :], nmr_[:, :, :], mp[:, :, 1, :], ALU.subtract).then_inc(s_mp, 1)
                ch.end()

            def factor(t, h, q):
                dve.wait_ge(s_corr, t + 1)
                dve.tensor_scalar(fac[q][:, :, :], corr[:, :, :], 1.0, None, ALU.add).then_inc(s_fac, 1)

            def head_max(t, j):
                dve.wait_ge(s_fs, RK * t + j + 1)
                after(dve, s_pf, RK * t + j)
                dve.tensor_reduce(nmf[:, :], bF1[:, :].rearrange("p (a k) -> p a k", a=TB), AX.X, ALU.max,
                                  negate=True).then_inc(s_fm, 1)

            def head_pt(t, j):
                dve.wait_ge(s_ptp, RK * t + j + 1)
                after(dve, s_of, RK * t + j)
                dve.tensor_copy(PTf[:, :, :], bF1[:, :].rearrange("p (a k) -> p a k", a=TB)).then_inc(s_ptf, 1)

            def head_out(t, h, q):
                dve.wait_ge(s_of, RK * (t + 1))
                after(dve, s_otp, t)
                ch = Chain(dve, s_ofc, 1, t)
                ch(dve.reciprocal(linv[:, :], lsum[:, :, :].rearrange("p a j -> p (a j)")))
                ch.end()
                dve.tensor_tensor(On[:, :, :], bF2[:, :].rearrange("p (n d) -> p n d", d=RD),
                                  linv[:, :].unsqueeze(2).broadcast_to([P, TB * RK, RD]), ALU.mult).then_inc(s_on, 1)

            def routed_out(t, h, q):
                dve.wait_ge(s_wop, t + 1)
                after(dve, s_y2t, t)
                dve.tensor_tensor(y2[:, :, :], bF2[:, 0:TB * D].rearrange("p (j n) -> p j n", j=TB),
                                  bo_b[:, :].unsqueeze(1).broadcast_to([P, TB, D]), ALU.add).then_inc(s_y2, 1)

            def routed_gate(t, h, q):
                dve.wait_ge(s_y2t, t + 1)
                dve.scalar_tensor_tensor(g2[q][:, :, :].rearrange("p j n -> p (j n)"),
                                         y2t[:, :, :].rearrange("p j n -> p (j n)"), 1.0,
                                         y2[:, :, :].rearrange("p j n -> p (j n)"), ALU.add, ALU.mult).then_inc(s_g2, 1)

            def attn_norm(t, h, q, g):
                dve.wait_ge(s_ot, 4 * t + g + 1)
                dve.wait_ge(s_fac, t + 1)
                after(dve, s_atp, t - 1)
                ch = Chain(dve, s_nc, 8, t)
                ch.k = 2 * g
                o = bC[:, 0:SEQ].rearrange("p (a j c) -> p a j c", a=TB, c=VC)
                ch(dve.tensor_tensor(lf[:, :, :], o[:, :, :, HD], fac[q][:, :, 4 * g:4 * g + 4], ALU.mult))
                ch(dve.reciprocal(lf[:, :, :], lf[:, :, :]))
                dve.tensor_tensor(attn[q][:, :, 4 * g:4 * g + 4, :], o[:, :, :, 0:HD],
                                  lf[:, :, :].unsqueeze(3).broadcast_to([P, TB, 4, HD]), ALU.mult).then_inc(s_an, 1)

            def final(t, h, q):
                dve.wait_ge(s_op, t + 1)
                dve.wait_ge(s_g2, t + 1)
                ch = Chain(dve, s_fc, 2, t)
                dve.tensor_tensor(s1[:, :, :], bC[:, 0:TB * D].rearrange("p (j n) -> p j n", j=TB),
                                  outb_b[:, :].unsqueeze(1).broadcast_to([P, TB, D]), ALU.add).then_inc(s_fin, 1)
                dve.wait_ge(s_fin, t + 1)
                f = "p j n -> p (j n)"
                ch(dve.scalar_tensor_tensor(s1[:, :, :].rearrange(f), s1[:, :, :].rearrange(f), 0.5,
                                            g2[q][:, :, :].rearrange(f), ALU.mult, ALU.mult))
                after(dve, s_out[q], 16 * h)
                ch(dve.tensor_tensor(o_t[q][:, :, :], s1[:, :, :], X[:, tiles(t), :], ALU.add))
                dve.sem_inc(s_done, 1)
                ch.end()

            def step(half, p):
                a, b, c, d = (lag(half, p, k) for k in range(4))
                A, Bb, C, Dd = (runs(x[0]) for x in (a, b, c, d))
                ch = None
                for s in range(NS):
                    if s == 0 and Bb:
                        head_biases(*b)
                    if s == 1 and C:
                        routed_out(*c)
                    if s == 2 and Dd:
                        attn_norm(*d, 3)
                    if s == 3 and A:
                        gated(*a)
                    if s == 4 and C:
                        routed_gate(*c)
                    if s == 6 and A:
                        ln_stats(*a)
                    if s == 6 and Dd:
                        final(*d)
                    if s == 7 and A:
                        ln_apply(*a)
                    if SS <= s < SS + H and Bb:
                        block_max(b[0], s - SS)
                    if s == 10 and A:
                        token_sum(*a)
                    if s == 12 and A:
                        ch = route_a(*a)
                    if s == 13 and A:
                        route_b(*a, ch)
                    if s == 15 and A:
                        route_c(*a)
                    if s - CS in (8, 12, 16) and C:
                        attn_norm(*c, (s - CS - 8) // 4)
                    if s in (5, 9, 13, 17) and Bb:
                        head_max(b[0], (s - 5) // 4)
                    if s in (7, 11, 15, 19) and Bb:
                        head_pt(b[0], (s - 7) // 4)
                    if s == 18 and Bb:
                        row_max(*b)
                    if s == 20 and Bb:
                        factor(*b)
                        head_out(*b)
            run(dve, step)

        @block.scalar
        def _(act):
            act.wait_ge(s_c1, 2)

            def normalized(t, h, q):
                after(act, s_z, t - 1)
                for j in range(TB):
                    n = bass.ds(t * TB + j, 1)
                    last = act.activation(xnf[q][:, j:j + 1, :], X[:, n, :], ACT.Identity, scale=rstd[:, n],
                                          bias=nmr[:, n])
                last.then_inc(s_xnf, 1)

            def z_tanh(t, h, q):
                act.wait_ge(s_z, t + 1)
                after(act, s_x1, t - 1)
                act.activation(zt[q][:, :, :], z[q][:, :, :], ACT.Tanh, scale=0.5).then_inc(s_zt, 1)

            def xT_copy(t, h, q):
                act.wait_ge(s_f1, t + 1)
                after(act, s_fv, t - 1)
                after(act, s_v2, t - 1)
                after(act, s_xsb, t - 1)
                act.copy(xT[q][:, :], bA[:, 0:SEQ]).then_inc(s_xT, 1)

            def qk_copy(t, h, q):
                act.wait_ge(s_qkp, t + 1)
                after(act, s_parts, t)
                act.mul(qk[:, 0, :], bA[:, 0:SEQ], HD ** -0.5)
                act.copy(qk[:, 1, :], bA[:, SEQ:]).then_inc(s_qk, 1)
                act.wait_ge(s_qk, t + 1)
                after(act, s_pst[q], 16 * h)
                act.copy(parts[q][:, :, 0, :], qk[:, :, :]).then_inc(s_hi, 1)

            def probs(t, h, q):
                act.wait_ge(s_lg2, t + 1)
                act.activation(prob[:, :], lg[:, :], ACT.Exp, bias=ntop[:, 0:1], accum_out=psum_[:, :]).then_inc(s_pe1, 1)

            def gate_exps(t, h, q):
                act.wait_ge(s_pt, t + 1)
                act.activation(g5[:, 0:RK], ptop[:, 0:RK], ACT.Exp, bias=nptop[:, 0:1])
                act.activation(g5[:, RK:RK + 1], nptop[:, 0:1], ACT.Exp).then_inc(s_pe2, 1)

            def v_copy(t, h, q):
                act.wait_ge(s_vp, t + 1)
                after(act, s_pv, 4 * (t - 1))
                act.copy(V2[q][:, :, :, 0:HD], bA[:, 0:TB * D].rearrange("p (a h d) -> p a h d", a=TB, h=H)).then_inc(s_v2, 1)

            def mT_copy(t, h, q):
                act.wait_ge(s_mTp, t + 1)
                after(act, s_ms[q], 16 * h)
                act.copy(mT[q][:, :], bAb[0:NP3 * H, 0:SEQ]).then_inc(s_mT, 1)

            def correction(t, h, q):
                act.wait_ge(s_cd, t + 1)
                after(act, s_fac, t)
                act.activation(corr[:, :, :], cdiff[:, :, :], ACT.Exp).then_inc(s_corr, 1)

            def head_qk(t, h, q, i):
                act.wait_ge(s_fqp, 2 * t + i + 1)
                if i == 0:
                    act.wait_ge(s_gb, t + 1)
                    after(act, s_fs, RK * t)
                act.activation(Qf[:, i, :], bF2[:, 0:SEQ], ACT.Identity, scale=gc[q][:, i, 0:1], bias=gb[q][:, i, 0:1])
                for jj in range(2):
                    rows = slice(jj * RD, (jj + 1) * RD)
                    last = act.activation(Kz[rows, i, jj, :], bF2[rows, SEQ:], ACT.Identity,
                                          scale=gc[q][rows, i, 1:2], bias=gb[q][rows, i, 1:2])
                last.then_inc(s_fq, 1)

            def head_v(t, h, q):
                act.wait_ge(s_fvp, t + 1)
                after(act, s_of, RK * t)
                act.copy(Vf[:, :, :], bF2[:, :].rearrange("p (a n) -> p a n", a=TB)).then_inc(s_fv, 1)

            def head_exp(t, j):
                act.wait_ge(s_fm, RK * t + j + 1)
                after(act, s_ptp, RK * t + j)
                if j == 0:
                    after(act, s_on, t)
                for qt in range(TB):
                    last = act.activation(Pf[:, qt, :], bF1[:, qt * SEQ:(qt + 1) * SEQ], ACT.Exp,
                                          bias=nmf[:, qt:qt + 1], accum_out=lsum[:, qt, j:j + 1])
                last.then_inc(s_pf, 1)

            def head_ot(t, h, q):
                act.wait_ge(s_otp, t + 1)
                after(act, s_wop, t)
                for i in range(2):
                    last = act.activation(OTf[:, i, :], bF2[:, i * SEQ:(i + 1) * SEQ], ACT.Identity,
                                          scale=gc[q][:, i, 2:3], bias=gb[q][:, i, 2:3])
                last.then_inc(s_otf, 1)

            def routed_tanh(t, h, q):
                act.wait_ge(s_y2, t + 1)
                after(act, s_g2, t)
                act.activation(y2t[:, :, :], y2[:, :, :], ACT.Tanh, scale=0.5).then_inc(s_y2t, 1)

            def exp_scores(t, h):
                act.wait_ge(s_st, H * t + h + 1)
                after(act, s_pv, 4 * t + h // 4 - 1)
                act.activation(PT[h % 8][:, :], bT[h % 2][:, :], ACT.Exp).then_inc(s_exp, 1)

            def ot_copy(t, g):
                act.wait_ge(s_pv, 4 * t + g + 1)
                after(act, s_ot, 4 * t + g - 1)
                act.copy(OT[g % 2][:, :], bC[:, 0:SEQ]).then_inc(s_oe, 1)

            def attnT_copy(t, h, q):
                act.wait_ge(s_atp, t + 1)
                after(act, s_op, t)
                act.copy(attnT[:, :], bC[:, 0:SEQ]).then_inc(s_at, 1)

            def step(half, p):
                a, b, c, d = (lag(half, p, k) for k in range(4))
                A, Bb, C, Dd = (runs(x[0]) for x in (a, b, c, d))
                for s in range(NS):
                    if s == 0 and A:
                        normalized(*a)
                    if s == 0 and Dd:
                        ot_copy(d[0], 3)
                    if s == 0 and C:
                        head_ot(*c)
                    if s == 1 and C:
                        mT_copy(*c)
                    if s == 2 and A:
                        z_tanh(*a)
                    if s == 2 and Bb:
                        head_qk(*b, 0)
                    if s == 3 and C:
                        routed_tanh(*c)
                    if s == 3 and Bb:
                        head_qk(*b, 1)
                    if s == 4 and Dd:
                        attnT_copy(*d)
                    if CS <= s < CS + H and C:
                        exp_scores(c[0], s - CS)
                    if s == 4 and Bb:
                        head_v(*b)
                    if s == 8 and A:
                        xT_copy(*a)
                    if s == 10 and A:
                        qk_copy(*a)
                    if s == 13 and A:
                        probs(*a)
                    if s == 14 and A:
                        gate_exps(*a)
                    if s == 14 and Bb:
                        v_copy(*b)
                    if s - CS in (6, 10, 14) and C:
                        ot_copy(c[0], (s - CS - 6) // 4)
                    if s in (6, 10, 14, 18) and Bb:
                        head_exp(b[0], (s - 6) // 4)
                    if s == 20 and Bb:
                        correction(*b)
            run(act, step)

        @block.tensor
        def _(pe):
            pe.wait_ge(s_w, 16 * 6)
            pe.wait_ge(s_c1, 2)

            def transpose_x(t, h, q):
                pe.wait_ge(s_xn1, t + 1)
                after(pe, s_mT, t - 1)
                for j in range(TB):
                    last = pe.transpose(bA[:, j * P:(j + 1) * P], xn1[q][:, j, :], ident[:, :])
                last.then_inc(s_f1, 1)

            def project_qk(t, h, q):
                pe.wait_ge(s_xT, t + 1)
                for k in range(2):
                    last = pe.matmul(bA[:, k * SEQ:(k + 1) * SEQ], w1[:, k, :], xT[q][:, :], start=True, stop=True)
                last.then_inc(s_qkp, 1)

            def logits(t, h, q):
                pe.wait_ge(s_qk, t + 1)
                pe.wait_ge(s_xsb, t + 1)
                pe.matmul(bA[:, 0:RH], xsb[:, :], wr_s[:, :], start=True, stop=True).then_inc(s_lgp, 1)

            def project_v(t, h, q):
                pe.wait_ge(s_lg, most(t + 2))
                for j in range(TB):
                    last = pe.matmul(bA[:, j * D:(j + 1) * D], xT[q][:, j * P:(j + 1) * P], w1[:, 2, :],
                                     start=True, stop=True)
                last.then_inc(s_vp, 1)

            def transpose_max(t, h, q):
                pe.wait_ge(s_mp, t + 1)
                pe.wait_ge(s_v2, most(t + 1))
                apart(pe)
                for j in range(TB):
                    last = pe.transpose(bAb[0:NP3 * H, j * P:(j + 1) * P],
                                        mp[:, j, :, :].rearrange("p a h -> p (a h)"), identb[:, :])
                last.then_inc(s_mTp, 1)

            def scores(t, h, q, s):
                if s == 0:
                    pe.wait_ge(s_ql[q], 16 * 13 * h + 16 * 13)
                after(pe, s_red, H * t + s - 1)
                qt, h0 = s // 8, 2 * (s % 8)
                for k in range(2):
                    last = pe.matmul(bS[s % 2][:, k * SEQ:(k + 1) * SEQ], QS[q][:, h0 + k, qt * P:(qt + 1) * P],
                                     KS[q][:, h0 + k, :], start=True, stop=True)
                last.then_inc(s_sp, 1)

            def shifted_scores(t, h_, q, h):
                if h == 0:
                    pe.wait_ge(s_ml[q], 16 * h_ + 16)
                after(pe, s_exp, H * t + h - 1)
                for kt in range(TB):
                    last = pe.matmul(bT[h % 2][:, kt * SEQ:(kt + 1) * SEQ], KS[q][:, h, kt * P:(kt + 1) * P],
                                     QS[q][:, h, :], start=True, stop=True)
                last.then_inc(s_st, 1)

            def values(t, q, g):
                pe.wait_ge(s_exp, H * t + 4 * g + 4)
                pe.wait_ge(s_v2, t + 1)
                if g == 0:
                    after(pe, s_fin, t)
                else:
                    pe.wait_ge(s_an, 4 * t + g)
                for kt in range(TB):
                    for j in range(4):
                        last = pe.matmul(bC[j * VC:(j + 1) * VC, 0:SEQ], V2[q][:, kt, 4 * g + j, :],
                                         PT[(4 * g + j) % 8][:, kt * SEQ:(kt + 1) * SEQ],
                                         start=(kt == 0), stop=(kt == TB - 1))
                last.then_inc(s_pv, 1)

            def transpose_o(t, g):
                pe.wait_ge(s_oe, 4 * t + g + 1)
                for qt in range(TB):
                    last = pe.transpose(bC[:, qt * P:(qt + 1) * P], OT[g % 2][:, qt * P:(qt + 1) * P], ident[:, :])
                last.then_inc(s_ot, 1)

            def transpose_attn(t, h, q):
                pe.wait_ge(s_an, 4 * t + 4)
                for qt in range(TB):
                    last = pe.transpose(bC[:, qt * P:(qt + 1) * P], attn[q][:, qt, :, :].rearrange("p h d -> p (h d)"),
                                        ident[:, :])
                last.then_inc(s_atp, 1)

            def project_out(t, h, q):
                pe.wait_ge(s_at, t + 1)
                for qt in range(TB):
                    last = pe.matmul(bC[:, qt * D:(qt + 1) * D], attnT[:, qt * P:(qt + 1) * P], w1[:, 3, :],
                                     start=True, stop=True)
                last.then_inc(s_op, 1)

            def head_qk(t, h, q, i):
                if i == 0:
                    pe.wait_ge(s_wl[q], 128 * h + 128)
                    after(pe, s_y2, t)
                else:
                    pe.wait_ge(s_fq, 2 * t + 1)
                for k in range(2):
                    last = pe.matmul(bF2[:, k * SEQ:(k + 1) * SEQ], wsel[q][:, i, k, :], xT[q][:, :],
                                     start=True, stop=True)
                last.then_inc(s_fqp, 1)

            def head_v(t, h, q):
                pe.wait_ge(s_fq, 2 * t + 2)
                for kt in range(TB):
                    last = pe.matmul(bF2[:, kt * SEQ:(kt + 1) * SEQ], xT[q][:, kt * P:(kt + 1) * P],
                                     wsel[q][:, :, 2, :], start=True, stop=True)
                last.then_inc(s_fvp, 1)

            def head_scores(t, j):
                i, jj = j // 2, j % 2
                pe.wait_ge(s_fq, 2 * t + i + 1)
                after(pe, s_ptf, RK * t + j)
                for qt in range(TB):
                    last = pe.matmul(bF1[:, qt * SEQ:(qt + 1) * SEQ], Qf[:, i, qt * P:(qt + 1) * P], Kz[:, i, jj, :],
                                     start=True, stop=True)
                last.then_inc(s_fs, 1)

            def head_transpose(t, j):
                pe.wait_ge(s_pf, RK * t + j + 1)
                for kt in range(TB):
                    for qt in range(TB):
                        last = pe.transpose(bF1[:, kt * SEQ + qt * P:kt * SEQ + (qt + 1) * P],
                                            Pf[:, qt, kt * P:(kt + 1) * P], ident[:, :])
                last.then_inc(s_ptp, 1)

            def head_out(t, j):
                pe.wait_ge(s_fv, t + 1)
                pe.wait_ge(s_ptf, RK * t + j + 1)
                for qt in range(TB):
                    for kt in range(TB):
                        last = pe.matmul(bF2[:, qt * SEQ + j * RD:qt * SEQ + (j + 1) * RD],
                                         PTf[:, kt, qt * P:(qt + 1) * P], Vf[:, kt, j * RD:(j + 1) * RD],
                                         start=(kt == 0), stop=(kt == TB - 1))
                last.then_inc(s_of, 1)

            def head_ot(t, h, q):
                pe.wait_ge(s_on, t + 1)
                for i in range(2):
                    for qt in range(TB):
                        last = pe.transpose(bF2[:, i * SEQ + qt * P:i * SEQ + (qt + 1) * P],
                                            On[:, qt * RK + 2 * i:qt * RK + 2 * i + 2, :].rearrange("p j d -> p (j d)"),
                                            ident[:, :])
                last.then_inc(s_otp, 1)

            def routed_out(t, h, q):
                pe.wait_ge(s_otf, t + 1)
                for qt in range(TB):
                    for i in range(2):
                        last = pe.matmul(bF2[:, qt * D:(qt + 1) * D], OTf[:, i, qt * P:(qt + 1) * P], wo_s[:, i, :],
                                         start=(i == 0), stop=(i == 1))
                last.then_inc(s_wop, 1)

            def step(half, p):
                a, b, c, d = (lag(half, p, k) for k in range(4))
                A, Bb, C, Dd = (runs(x[0]) for x in (a, b, c, d))
                for s in range(NS):
                    if s == 0 and Dd:
                        values(d[0], d[2], 3)
                    if s == 0 and C:
                        head_ot(*c)
                    if s == 1 and C:
                        transpose_max(*c)
                    if s == 1 and Dd:
                        transpose_o(d[0], 3)
                    if s == 1 and C:
                        routed_out(*c)
                    if s == 2 and Bb:
                        head_qk(*b, 0)
                    if s == 3 and Bb:
                        head_qk(*b, 1)
                    if s == 3 and Dd:
                        transpose_attn(*d)
                    if SS <= s < SS + H and Bb:
                        scores(*b, s - SS)
                    if CS <= s < CS + H and C:
                        shifted_scores(*c, s - CS)
                    if s == 4 and Bb:
                        head_v(*b)
                    if s == 5 and Dd:
                        project_out(*d)
                    if s == 7 and A:
                        transpose_x(*a)
                    if s == 9 and A:
                        project_qk(*a)
                    if s == 11 and A:
                        logits(*a)
                    if s == 13 and Bb:
                        project_v(*b)
                    if s - CS in (5, 9, 13) and C:
                        values(c[0], c[2], (s - CS - 5) // 4)
                    if s - CS in (7, 11, 15) and C:
                        transpose_o(c[0], (s - CS - 7) // 4)
                    if s in (5, 9, 13, 17) and Bb:
                        head_scores(b[0], (s - 5) // 4)
                    if s in (7, 11, 15, 19) and Bb:
                        head_transpose(b[0], (s - 7) // 4)
                    if s in (8, 12, 16, 20) and Bb:
                        head_out(b[0], (s - 8) // 4)
            run(pe, step)


def arrange(inputs):
    import numpy as np
    c = np.ascontiguousarray
    a = {k: np.asarray(v) for k, v in inputs.items()}
    heads = [a[f"L1_ffn_W{n}"].reshape(D, RH, RD) for n in "qkv"]
    return {
        "x": c(a["L0_attn_x"].reshape(B * SEQ, D)),
        "l0_w": c(np.stack([a[f"L0_attn_W_{n}"].T for n in "kvro"], axis=1)),
        "l0_cols": c(np.stack([a["L0_attn_time_decay"], a["L0_attn_time_first"]]
                              + [a[f"L0_attn_time_mix_{n}"].reshape(D) for n in "kvr"], axis=1)),
        "rms_scale": c(a["L0_ffn_scale"].reshape(1, D)),
        "centT": c(a["L0_ffn_centroids"].T),
        "up_w": c(a["L0_ffn_up_w"].transpose(1, 0, 2).reshape(D, NE * 2 * HID)),
        "down_w": c(a["L0_ffn_down_w"].reshape(NE, 2, P, D).transpose(2, 0, 1, 3).reshape(P, NE * 2 * D)),
        "l1_w": c(np.stack([a[f"L1_attn_{n}_w"].T for n in ("q", "k", "v", "out")], axis=1)),
        "out_b": c(a["L1_attn_out_b"].reshape(1, D)),
        "qkv_w": c(np.stack(heads, axis=2).transpose(1, 0, 2, 3)),
        "qkv_b": c(np.stack([a[f"L1_ffn_b{n}"].reshape(RH, RD) for n in "qkv"], axis=2)),
        "wr": c(a["L1_ffn_Wr"]),
        "br": c(a["L1_ffn_br"].reshape(1, RH)),
        "wo": c(a["L1_ffn_Wo"].reshape(2, P, D).transpose(1, 0, 2)),
        "bo": c(a["L1_ffn_bo"].reshape(1, D)),
    }


def kernel(**inputs):
    import concourse.bacc as bacc
    from concourse.bass_utils import run_bass_kernel_spmd

    nc = bacc.Bacc("TRN2", target_bir_lowering=False, num_devices=1)
    arrays = arrange(inputs)
    args = [nc.dram_tensor(f"in_{n}", v.shape, mybir.dt.from_np(v.dtype), kind="ExternalInput").ap()
            for n, v in arrays.items()]
    args.append(nc.dram_tensor("out_x", (B * SEQ, D), fp32, kind="ExternalOutput").ap())
    args += [nc.dram_tensor(n, shape, dt, kind="Internal").ap() for n, shape, dt in SCRATCH]
    program(nc, *args)
    r = run_bass_kernel_spmd(nc, [{f"in_{n}": v for n, v in arrays.items()}], core_ids=[0])
    return r.results[0]["out_x"].reshape(B, SEQ, D)
```

```python
import concourse.bass as bass
from concourse import mybir
from contextlib import ExitStack

B, SEQ, D = 32, 256, 128
P = 128
TB = SEQ // P
NT = B * TB
NE, HID = 8, 256
NST = NT + NE
H, HD = 16, 8
BLK = 64
NBLK = SEQ // BLK
RH, RK, RD = 16, 4, 64
LN_EPS, RMS_EPS, WKV_EPS = 1e-5, 1e-6, 1e-9
NEG_INF = -1e38

fp32 = mybir.dt.float32
bf16 = mybir.dt.bfloat16
i32 = mybir.dt.int32
u32 = mybir.dt.uint32
ALU = mybir.AluOpType
ACT = mybir.ActivationFunctionType
AX = mybir.AxisListType


def after(eng, sem, count):
    if not (isinstance(count, int) and count <= 0):
        eng.wait_ge(sem, count)

SCRATCH = [("xs_dram", (NST * P, D), fp32), ("ys_dram", (NST * P, D), fp32),
           ("parts_dram", (2, 2, 3, P, SEQ), bf16), ("mrow_dram", (2, 3, H, SEQ), bf16)]


def apart(eng):
    eng.nop(nofuse=True)


class Chain:

    def __init__(self, eng, sem, n, batch):
        self.eng, self.sem, self.n, self.base, self.k = eng, sem, n, batch * n, 0

    def __call__(self, ins):
        self.k += 1
        ins.then_inc(self.sem, 1)
        self.eng.wait_ge(self.sem, self.base + self.k)

    def end(self):
        assert self.k == self.n, (self.k, self.n)


def program(nc, x, l0_w, l0_cols, rms_scale, centT, up_w, down_w, l1_w, out_b, qkv_w, qkv_b,
            wr, br, wo, bo, out, xs_dram, ys_dram, parts_dram, mrow_dram):
    with ExitStack() as ctx:
        def sb(name, shape, dt=fp32):
            return ctx.enter_context(nc.sbuf_tensor(name, shape, dt))

        ident = sb("ident", [P, P])
        ones = sb("ones", [P, SEQ])
        mhalf = sb("mhalf", [P, NT])
        X = sb("X", [P, NT, D])
        S = sb("S", [P, NT, D])
        rstd = sb("rstd", [P, NT])
        nmr = sb("nmr", [P, NT])
        slot = sb("slot", [P, NT], i32)
        PS = [ctx.enter_context(nc.psum_tensor(f"PS{i}", [P, 512], fp32)) for i in range(8)]
        with ExitStack() as front:
            def sbf(name, shape, dt=fp32):
                return front.enter_context(nc.sbuf_tensor(name, shape, dt))

            XR = sbf("XR", [P, NT, D])
            up = sbf("up", [P, NE * 2 * HID])
            down = sbf("down", [P, NE * 2 * D])
            earlier = sbf("earlier", [P, P])
            iota_t = sbf("iota_t", [P, NST])
            onehot = sbf("onehot", [P, NT, NE])
            cols = sbf("cols", [P, 5])
            decay = sbf("decay", [P, SEQ])
            wmix = sbf("wmix", [P, 2, 3, D])
            w_out = sbf("w_out", [P, D])
            choose_experts(nc, x, l0_w, l0_cols, rms_scale, centT, up_w, down_w, xs_dram, ident, ones, mhalf, X, XR,
                           rstd, nmr, up, down, earlier, iota_t, onehot, cols, decay, wmix, w_out, PS)
            experts_and_recurrence(nc, X, S, rstd, nmr, onehot, earlier, ones, iota_t, ident, slot, XR, up, down, cols,
                                   decay, wmix, w_out, PS, xs_dram, ys_dram)
        layer_one(nc, X, S, rstd, nmr, slot, ident, ones, mhalf, PS, ys_dram, parts_dram, mrow_dram, l1_w, out_b,
                  qkv_w, qkv_b, wr, br, wo, bo, out)


def choose_experts(nc, x, l0_w, l0_cols, rms_scale, centT, up_w, down_w, xs_dram, ident, ones, mhalf, X, XR,
                   rstd, nmr, up, down, earlier, iota_t, onehot, cols, decay, wmix, w_out, PS):
    with ExitStack() as ctx:
        def sb(name, shape, dt=fp32):
            return ctx.enter_context(nc.sbuf_tensor(name, shape, dt))

        def sem(name):
            return ctx.enter_context(nc.semaphore(name))

        NCH = 4
        CH = NT // NCH
        iota_i = sb("iota_i", [P, NST], i32)
        w0 = sb("w0", [P, 4, D])
        ommix = sb("ommix", [P, 3])
        scale_b = sb("scale_b", [P, D])
        cT = sb("cT", [P, NE])
        cTsq = sb("cTsq", [P, NE])
        cT2 = sb("cT2", [P, NE])
        neg1 = sb("neg1", [P, P])
        nny = sb("nny", [P, NE])
        zero_tile = sb("zero_tile", [P, D])
        st = sb("stats_x", [P, NT, 6])
        mv = sb("mv", [P, NT, 2])
        rrms = sb("rrms", [P, NT])
        r2 = sb("r2", [P, NT])
        nmr2 = sb("nmr2", [P, NT])
        xh_t = [sb(f"xh_t{i}", [P, TB, D]) for i in range(2)]
        xr_t = [sb(f"xr_t{i}", [P, TB, D]) for i in range(2)]
        xrT = [sb(f"xrT{i}", [P, SEQ]) for i in range(2)]
        xrTsq = [sb(f"xrTsq{i}", [P, SEQ]) for i in range(2)]
        nd = sb("nd", [P, NT, NE])
        best = sb("best", [P, NT])
        falling = sb("falling", [P, NE])
        takes = sb("takes", [P, NT, NE])

        s_const = sem("consts_ready")
        s_x = [sem(f"x_loaded{i}") for i in range(NCH)]
        s_w = sem("weights_loaded")
        s_we = sem("expert_weights_loaded")
        s_zero = sem("sorted_zeroed")
        s_setup = sem("setup_chain_pool")
        s_setv = sem("setup_chain_dve")
        s_cent = sem("centroid_norms_ready")
        s_stat = sem("x_variances_ready")
        s_msq = sem("x_mean_squares_ready")
        s_stc = sem("stats_chain")
        s_pow = sem("rsqrts_ready")
        s_r2 = sem("factors_ready")
        s_hat = sem("normalized_by_both")
        s_norm = sem("scaled")
        s_xr = [sem(f"xr_kept{i}") for i in range(2)]
        s_tr = sem("xr_transposed")
        s_xrT = sem("xrT_ready")
        s_xrsq = sem("xrT_squared")
        s_dist = sem("distances_in_psum")
        s_nd = sem("distances_read")
        s_rc = sem("route_chain")
        psT, psD = PS[0:2], PS[2:4]

        def run(eng, step):
            step(0, 0)
            step(0, 1)
            with eng.Fori(1, B // 2) as half:
                step(half, 0)
                step(half, 1)
            step(B // 2, 0)

        def lag(half, p, k):
            h, q = half + (p - k) // 2, (p - k) % 2
            return 2 * h + q, h, q

        def runs(t):
            return not isinstance(t, int) or 0 <= t < B

        block = ctx.enter_context(nc.Block())

        @block.sync
        def _(sp):
            xv = x.rearrange("(t p) d -> p t d", p=P)
            for c in range(NCH):
                sp.dma_start(X[:, c * CH:(c + 1) * CH, :], xv[:, c * CH:(c + 1) * CH, :]).then_inc(s_x[c], 16)
            for dst, src in ((w0[:, :, :], l0_w), (cols[:, :], l0_cols), (cT[:, :], centT),
                             (scale_b[:, :], rms_scale.to_broadcast([P, D]))):
                sp.dma_start(dst, src).then_inc(s_w, 16)
            sp.wait_ge(s_const, 1)
            sp.dma_start(xs_dram.rearrange("(t p) d -> p t d", p=P),
                         zero_tile[:, :].unsqueeze(1).broadcast_to([P, NST, D])).then_inc(s_zero, 16)
            sp.dma_start(up[:, :], up_w).then_inc(s_we, 16)
            sp.dma_start(down[:, :], down_w).then_inc(s_we, 16)

            def step(half, p):
                t, h, q = lag(half, p, 0)
                if runs(t):
                    sp.wait_ge(s_norm, t + 1)
                    apart(sp)
                    sp.dma_start(XR[:, bass.ds(t * TB, TB), :], xr_t[q][:, :, :]).then_inc(s_xr[q], 16)
            run(sp, step)
            for p in range(2):
                sp.wait_ge(s_xr[p], 16 * (B // 2))
            sp.wait_ge(s_zero, 16)
            sp.wait_ge(s_we, 32)

        @block.gpsimd
        def _(pool):
            ch = Chain(pool, s_setup, 2, 0)
            pool.memset(zero_tile[:, :], 0.0).then_inc(s_const, 1)
            pool.memset(ones[:, :], 1.0)
            pool.memset(neg1[:, :], -1.0)
            pool.memset(mhalf[:, :], -0.5)
            pool.memset(ident[:, :], 0.0)
            ch(pool.iota(iota_i[:, :], pattern=[[1, NST]], base=0, channel_multiplier=0))
            pool.affine_select(out=ident[:, :], in_=ident[:, :], compare_op=ALU.not_equal, fill=1.0, base=0,
                               pattern=[[-1, P]], channel_multiplier=1)
            pool.affine_select(out=earlier[:, :], in_=ones[:, 0:P], compare_op=ALU.is_gt, fill=0.0, base=0,
                               pattern=[[1, P]], channel_multiplier=-1)
            ch(pool.tensor_copy(iota_t[:, :], iota_i[:, :]))
            ch.end()
            pool.sem_inc(s_const, 1)
            for c in range(NCH):
                for r, made in ((rstd, s_stat), (rrms, s_msq)):
                    pool.wait_ge(made, c + 1)
                    part = slice(c * CH, (c + 1) * CH)
                    pool.tensor_tensor(r[:, part], r[:, part], mhalf[:, part], ALU.pow).then_inc(s_pow, 1)

            def step(half, p):
                t, h, q = lag(half, p, 1)
                if runs(t):
                    pool.wait_ge(s_xrT, t + 1)
                    after(pool, s_dist, t - 1)
                    pool.tensor_tensor(xrTsq[q][:, :], xrT[q][:, :], xrT[q][:, :], ALU.mult).then_inc(s_xrsq, 1)
            run(pool, step)

        @block.vector
        def _(dve):
            def statistics(c):
                dve.wait_ge(s_x[c], 16)
                sc = Chain(dve, s_stc, 2, c)
                tiles = range(c * CH, (c + 1) * CH)
                for t in tiles:
                    last = dve.bn_stats(st[:, t, :], X[:, t, :])
                sc(last)
                for t in tiles:
                    last = dve.bn_aggr(mv[:, t, :], st[:, t, :])
                sc(last)
                sc.end()
                part = slice(c * CH, (c + 1) * CH)
                dve.tensor_scalar(rstd[:, part], mv[:, part, 1], LN_EPS, None, ALU.add).then_inc(s_stat, 1)

            def mean_squares(c):
                part = slice(c * CH, (c + 1) * CH)
                dve.wait_ge(s_pow, 2 * c + 1)
                mc = Chain(dve, s_setv, 2, c)
                dve.scalar_tensor_tensor(nmr[:, part], mv[:, part, 0], -1.0, rstd[:, part], ALU.mult, ALU.mult)
                mc(dve.tensor_tensor(rrms[:, part], rstd[:, part], rstd[:, part], ALU.mult))
                mc(dve.tensor_tensor(rrms[:, part], rrms[:, part], mv[:, part, 1], ALU.mult))
                mc.end()
                dve.tensor_scalar(rrms[:, part], rrms[:, part], RMS_EPS, None, ALU.add).then_inc(s_msq, 1)

            def factors(c):
                part = slice(c * CH, (c + 1) * CH)
                dve.wait_ge(s_pow, 2 * c + 2)
                dve.tensor_tensor(r2[:, part], rstd[:, part], rrms[:, part], ALU.mult)
                dve.tensor_tensor(nmr2[:, part], nmr[:, part], rrms[:, part], ALU.mult).then_inc(s_r2, 1)

            statistics(0)
            for c in range(1, NCH):
                statistics(c)
                mean_squares(c - 1)
                if c > 1:
                    factors(c - 2)
            dve.wait_ge(s_w, 16 * 4)
            dve.wait_ge(s_const, 2)
            dve.tensor_scalar(decay[:, :], ones[:, :], cols[:, 0:1], None, ALU.mult)
            dve.tensor_scalar(falling[:, :], iota_t[:, 0:NE], -1.0, float(NE), ALU.mult, ALU.add)
            dve.tensor_scalar(cT2[:, :], cT[:, :], 2.0, None, ALU.mult)
            dve.tensor_scalar(w_out[:, :], w0[:, 3, :], 0.25, None, ALU.mult)
            dve.tensor_scalar(ommix[:, :], cols[:, 2:5], -1.0, 1.0, ALU.mult, ALU.add).then_inc(s_cent, 1)
            dve.tensor_tensor(cTsq[:, :], cT[:, :], cT[:, :], ALU.mult).then_inc(s_cent, 1)
            dve.wait_ge(s_cent, 2)
            for j in range(3):
                dve.tensor_scalar(wmix[:, 0, j, :], w0[:, j, :], cols[:, 2 + j:3 + j], None, ALU.mult)
                dve.tensor_scalar(wmix[:, 1, j, :], w0[:, j, :], ommix[:, j:j + 1], None, ALU.mult)
            mean_squares(NCH - 1)
            factors(NCH - 2)
            factors(NCH - 1)
            dve.wait_ge(s_cent, 3)
            dve.tensor_copy(nny[:, :], PS[7][:, 0:NE]).then_inc(s_cent, 1)
            dve.wait_ge(s_cent, 4)

            def step(half, p):
                t, h, q = lag(half, p, 0)
                if runs(t):
                    dve.wait_ge(s_hat, t + 1)
                    after(dve, s_tr, t - 1)
                    after(dve, s_xr[q], 16 * h)
                    dve.tensor_tensor(xr_t[q][:, :, :], xh_t[q][:, :, :],
                                      scale_b[:, :].unsqueeze(1).broadcast_to([P, TB, D]), ALU.mult).then_inc(s_norm, 1)
                t, h, q = lag(half, p, 1)
                if runs(t):
                    dve.wait_ge(s_dist, t + 1)
                    dve.tensor_tensor(nd[:, bass.ds(t * TB, TB), :],
                                      psD[q][:, 0:TB * NE].rearrange("p (j e) -> p j e", e=NE),
                                      nny[:, :].unsqueeze(1).broadcast_to([P, TB, NE]), ALU.add).then_inc(s_nd, 1)
            run(dve, step)
            full = [P, NT, NE]
            rc = Chain(dve, s_rc, 4, 0)
            dve.wait_ge(s_nd, B)
            rc(dve.tensor_reduce(best[:, :], nd[:, :, :], AX.X, ALU.max))
            rc(dve.tensor_tensor(takes[:, :, :], nd[:, :, :], best[:, :].unsqueeze(2).broadcast_to(full), ALU.is_equal))
            rc(dve.tensor_tensor(takes[:, :, :], takes[:, :, :], falling[:, :].unsqueeze(1).broadcast_to(full), ALU.mult))
            rc(dve.tensor_reduce(best[:, :], takes[:, :, :], AX.X, ALU.max))
            rc.end()
            dve.tensor_tensor(onehot[:, :, :], falling[:, :].unsqueeze(1).broadcast_to(full),
                              best[:, :].unsqueeze(2).broadcast_to(full), ALU.is_equal)

        @block.scalar
        def _(act):
            act.wait_ge(s_r2, NCH)

            def step(half, p):
                t, h, q = lag(half, p, 0)
                if runs(t):
                    after(act, s_norm, t - 1)
                    for j in range(TB):
                        n = bass.ds(t * TB + j, 1)
                        last = act.activation(xh_t[q][:, j:j + 1, :], X[:, n, :], ACT.Identity, scale=r2[:, n],
                                              bias=nmr2[:, n])
                    last.then_inc(s_hat, 1)
                t, h, q = lag(half, p, 1)
                if runs(t):
                    act.wait_ge(s_tr, t + 1)
                    after(act, s_dist, t - 1)
                    after(act, s_xrsq, t - 1)
                    act.copy(xrT[q][:, :], psT[q][:, 0:SEQ]).then_inc(s_xrT, 1)
            run(act, step)

        @block.tensor
        def _(pe):
            pe.wait_ge(s_const, 2)
            pe.wait_ge(s_cent, 2)
            pe.matmul(PS[7][:, 0:NE], neg1[:, :], cTsq[:, :], start=True, stop=True).then_inc(s_cent, 1)

            def step(half, p):
                t, h, q = lag(half, p, 0)
                if runs(t):
                    pe.wait_ge(s_norm, t + 1)
                    after(pe, s_xrT, t - 1)
                    for j in range(TB):
                        last = pe.transpose(psT[q][:, j * P:(j + 1) * P], xr_t[q][:, j, :], ident[:, :])
                    last.then_inc(s_tr, 1)
                t, h, q = lag(half, p, 1)
                if runs(t):
                    pe.wait_ge(s_xrT, t + 1)
                    pe.wait_ge(s_xrsq, t + 1)
                    after(pe, s_nd, t - 1)
                    for j in range(TB):
                        o = psD[q][:, NE * j:NE * j + NE]
                        pe.matmul(o, xrT[q][:, j * P:(j + 1) * P], cT2[:, :], start=True, stop=False)
                        last = pe.matmul(o, xrTsq[q][:, j * P:(j + 1) * P], neg1[:, 0:NE], start=False, stop=True)
                    last.then_inc(s_dist, 1)
            run(pe, step)



def place_tokens(dve, s_place, s_counts, s_placed, nc, ctx, onehot, ones, iota_t, slot, tile_expert, PS):
    def sb(name, shape, dt=fp32):
        return ctx.enter_context(nc.sbuf_tensor(name, shape, dt))
    tot = sb("tot", [P, NT, NE])
    cum = sb("cum", [P, NT, NE])
    rank = sb("rank", [P, NT, NE])
    thresholds = sb("thresholds", [P, NT])
    ntiles = sb("ntiles", [P, NE])
    end = sb("end", [P, NE])
    first = sb("first", [P, NE])
    past = sb("past", [P, NST, NE])
    slot_f = sb("slot_f", [P, NT])
    te_f = sb("te_f", [P, NST])
    over = past[:, 0:NT, :].rearrange("p t e -> p (t e)").rearrange("p (e t) -> p e t", e=NE)
    ch = Chain(dve, s_place, 12, 0)
    dve.tensor_scalar(thresholds[:, :], iota_t[:, 0:NT], float(P), None, ALU.mult)
    dve.wait_ge(s_counts, 1)
    ch(dve.tensor_copy(tot[:, :, :], PS[1][:, 0:NT * NE].rearrange("p (t e) -> p t e", e=NE)))
    for e in range(NE):
        last = dve.tensor_tensor_scan(cum[:, :, e], ones[:, 0:NT], tot[:, :, e], 0.0, ALU.mult, ALU.add)
    ch(last)
    ch(dve.tensor_tensor(over, cum[:, NT - 1, :].unsqueeze(2).broadcast_to([P, NE, NT]),
                         thresholds[:, :].unsqueeze(1).broadcast_to([P, NE, NT]), ALU.is_gt))
    ch(dve.tensor_reduce(ntiles[:, :], over, AX.X, ALU.add))
    ch(dve.tensor_tensor_scan(end[:, :], ones[:, 0:NE], ntiles[:, :], 0.0, ALU.mult, ALU.add))
    ch(dve.tensor_tensor(first[:, :], end[:, :], ntiles[:, :], ALU.subtract))
    dve.tensor_tensor(cum[:, :, :], cum[:, :, :], tot[:, :, :], ALU.subtract)
    ch(dve.tensor_scalar(first[:, :], first[:, :], float(P), None, ALU.mult))
    ch(dve.tensor_tensor(rank[:, :, :], PS[0][:, 0:NT * NE].rearrange("p (t e) -> p t e", e=NE), cum[:, :, :], ALU.add))
    ch(dve.tensor_tensor(rank[:, :, :], rank[:, :, :], first[:, :].unsqueeze(1).broadcast_to([P, NT, NE]), ALU.add))
    dve.tensor_tensor(past[:, :, :], iota_t[:, :].unsqueeze(2).broadcast_to([P, NST, NE]),
                      end[:, :].unsqueeze(1).broadcast_to([P, NST, NE]), ALU.is_ge)
    ch(dve.tensor_tensor(rank[:, :, :], rank[:, :, :], onehot[:, :, :], ALU.mult))
    dve.tensor_reduce(te_f[:, :], past[:, :, :], AX.X, ALU.add)
    ch(dve.tensor_reduce(slot_f[:, :], rank[:, :, :], AX.X, ALU.add))
    ch(dve.tensor_scalar(te_f[:, :], te_f[:, :], float(NE - 1), None, ALU.min))
    ch.end()
    dve.tensor_copy(tile_expert[:, :], te_f[:, :])
    dve.tensor_copy(slot[:, :], slot_f[:, :]).then_inc(s_placed, 1)


def experts_and_recurrence(nc, X, S, rstd, nmr, onehot, earlier, ones, iota_t, ident, slot, XR, up, down, cols,
                           decay, wmix, w_out, PS, xs_dram, ys_dram):
    with ExitStack() as ctx:
        def sb(name, shape, dt=fp32):
            return ctx.enter_context(nc.sbuf_tensor(name, shape, dt))

        def two(name, shape, dt=fp32):
            return [sb(f"{name}{i}", shape, dt) for i in range(2)]

        def sem(name):
            return ctx.enter_context(nc.semaphore(name))

        FIRST = 8
        TPS = NST // (B - FIRST)
        assert TPS * (B - FIRST) == NST and FIRST % 2 == 0
        G = 2 * TPS
        NB = 3
        LAST = 6

        xs_t = [sb(f"xs_t{i}", [P, D]) for i in range(NB)]
        xsT = [sb(f"xsT{i}", [P, P]) for i in range(NB)]
        gate = [sb(f"gate{i}", [P, HID]) for i in range(NB)]
        hid = [sb(f"hid{i}", [P, HID]) for i in range(NB)]
        hidT = [sb(f"hidT{i}", [P, 2, P]) for i in range(NB)]
        ys_t = [sb(f"ys_t{i}", [P, D]) for i in range(NB)]
        tile_expert = sb("tile_expert", [P, NST], i32)
        xn_t = two("xn_t", [P, TB, D])
        xnT = two("xnT", [P, SEQ + 1])
        kv = two("kv", [P, 2, SEQ])
        rtanh = two("rtanh", [P, SEQ])
        pp = sb("pp", [P, SEQ + 1])
        aa = sb("aa", [P, SEQ + 1])
        bb = sb("bb", [P, SEQ + 1])
        dcarry = sb("dcarry", [P, SEQ])
        dout = sb("dout", [P, SEQ])
        args = sb("args", [P, 4, SEQ])
        ex = sb("ex", [P, 4, SEQ])
        ev = sb("ev", [P, 2, SEQ])
        num = sb("num", [P, SEQ])
        den = sb("den", [P, SEQ])
        rwkv = two("rwkv", [P, SEQ])

        s_zcol = sem("zero_columns_ready")
        s_counts = sem("counts_in_psum")
        s_place = sem("place_chain")
        s_placed = sem("slots_ready")
        s_scat = sem("tokens_scattered")
        s_xs = [sem(f"xs_loaded{i}") for i in range(NB)]
        s_fx = sem("xs_transposed")
        s_xsT = sem("xsT_ready")
        s_up = sem("hidden_in_psum")
        s_gate = sem("gate_tanh_ready2")
        s_gch = sem("gate_chain")
        s_hid = sem("hidden_ready")
        s_fh = sem("hidden_transposed")
        s_hidT = sem("hidT_ready")
        s_dn = sem("expert_out_in_psum")
        s_y = sem("expert_out_ready")
        s_ys = [sem(f"expert_out_stored{i}") for i in range(NB)]
        s_xn = sem("xn_normalized")
        s_tr = sem("xn_transposed")
        s_xnT = sem("xnT_ready")
        s_kvp = sem("kv_in_psum")
        s_rp = sem("r_in_psum")
        s_kv = sem("kv_ready")
        s_th = sem("gate_tanh_ready")
        s_ec = sem("exponent_chain")
        s_args = sem("exponents_ready")
        s_ex = sem("exponentials_ready")
        s_rwkv = sem("rwkv_ready")
        s_wkv = sem("wkv_chain")
        s_so = sem("s_in_psum")
        s_s = sem("s_kept")
        psU, psX, psH, psY, psT, psKV, psR = PS[0:2], PS[2], PS[3], PS[4], PS[5], PS[6], PS[7]

        def lag(half, p, k):
            h, q = half + (p - k) // 2, (p - k) % 2
            return 2 * h + q, h, q

        def tile(half, p, turn, k):
            place = TPS * p + turn - k
            h, q = half - FIRST // 2 + place // G, place % G
            t = G * h + q
            return None if isinstance(t, int) and not 0 <= t < NST else (t, h, q)

        def runs(t):
            return not isinstance(t, int) or 0 <= t < B

        def run(eng, step):
            for s in range(FIRST + 4):
                step(s // 2, s % 2)
            with eng.Fori(FIRST // 2 + 2, B // 2) as half:
                step(half, 0)
                step(half, 1)
            for s in range(B, B + 4):
                step(s // 2, s % 2)

        def arrivals(h, q):
            return 16 * (G // NB * h + q // NB + 1)

        block = ctx.enter_context(nc.Block())

        @block.gpsimd
        def _(pool):
            pool.memset(pp[:, 0:1], NEG_INF)
            pool.memset(aa[:, 0:1], 0.0)
            pool.memset(bb[:, 0:1], 0.0)
            for i in range(2):
                last = pool.memset(xnT[i][:, 0:1], 0.0)
            last.then_inc(s_zcol, 1)
            pool.wait_ge(s_placed, 1)
            for t in range(NT):
                pool.indirect_dma_start(xs_dram, bass.IndirectOffsetOnAxis(slot[:, t:t + 1], axis=0),
                                        XR[:, t, :], None).then_inc(s_scat, 16)
            pool.wait_ge(s_scat, 16 * NT)

        @block.sync
        def _(sp):
            sp.wait_ge(s_scat, 16 * NT)

            def load(t, h, q):
                after(sp, s_fx, t - NB + 1)
                apart(sp)
                sp.dma_start(xs_t[q % NB][:, :], xs_dram[bass.ds(t * P, P), :]).then_inc(s_xs[q % NB], 16)

            def store(t, h, q):
                sp.wait_ge(s_y, t + 1)
                apart(sp)
                sp.dma_start(ys_dram[bass.ds(t * P, P), :], ys_t[q % NB][:, :]).then_inc(s_ys[q % NB], 16)

            for t in range(NB):
                load(t, 0, t)

            def step(half, p):
                for turn in range(TPS):
                    new = tile(half, p, turn, -NB)
                    if new and (not isinstance(new[0], int) or new[0] >= NB):
                        load(*new)
                    done = tile(half, p, turn, LAST)
                    if done:
                        store(*done)
            for s in range(FIRST, FIRST + 4):
                step(s // 2, s % 2)
            with sp.Fori(FIRST // 2 + 2, B // 2 - 1) as half:
                step(half, 0)
                step(half, 1)
            for s in range(B - 2, B + 2):
                step(s // 2, s % 2)
            for i in range(NB):
                sp.wait_ge(s_ys[i], 16 * (NST // NB))

        @block.vector
        def _(dve):
            place_tokens(dve, s_place, s_counts, s_placed, nc, ctx, onehot, ones, iota_t, slot, tile_expert, PS)

            def exponents(t, h, q):
                dve.wait_ge(s_kv, t + 1)
                k = kv[q][:, 0, :]
                c = Chain(dve, s_ec, 2, t)
                c(dve.tensor_tensor_scan(pp[:, 1:SEQ + 1], decay[:, :], k, NEG_INF, ALU.add, ALU.max))
                dve.scalar_tensor_tensor(dcarry[:, :], pp[:, 0:SEQ], cols[:, 0:1], k, ALU.add, ALU.subtract)
                c(dve.scalar_tensor_tensor(dout[:, :], k, cols[:, 1:2], pp[:, 0:SEQ], ALU.add, ALU.subtract))
                c.end()
                after(dve, s_ex, t)
                dve.tensor_scalar(args[:, 0, :], dcarry[:, :], 0.0, None, ALU.min)
                dve.tensor_scalar(args[:, 1, :], dcarry[:, :], 0.0, -1.0, ALU.max, ALU.mult)
                dve.tensor_scalar(args[:, 2, :], dout[:, :], 0.0, None, ALU.min)
                dve.tensor_scalar(args[:, 3, :], dout[:, :], 0.0, -1.0, ALU.max, ALU.mult).then_inc(s_args, 1)

            def sums(t, h, q):
                dve.wait_ge(s_ex, t + 1)
                c = Chain(dve, s_wkv, 6, t)
                v = kv[q][:, 1, :]
                dve.tensor_tensor(ev[:, 0, :], ex[:, 1, :], v, ALU.mult)
                dve.tensor_tensor(ev[:, 1, :], ex[:, 2, :], v, ALU.mult)
                c(dve.tensor_tensor_scan(bb[:, 1:SEQ + 1], ex[:, 0, :], ex[:, 1, :], 0.0, ALU.mult, ALU.add))
                dve.tensor_tensor_scan(aa[:, 1:SEQ + 1], ex[:, 0, :], ev[:, 0, :], 0.0, ALU.mult, ALU.add)
                c(dve.tensor_tensor(den[:, :], ex[:, 3, :], bb[:, 0:SEQ], ALU.mult))
                dve.scalar_tensor_tensor(den[:, :], den[:, :], WKV_EPS, ex[:, 2, :], ALU.add, ALU.add)
                c(dve.tensor_tensor(num[:, :], ex[:, 3, :], aa[:, 0:SEQ], ALU.mult))
                c(dve.tensor_tensor(num[:, :], num[:, :], ev[:, 1, :], ALU.add))

            def quotient(t, h, q):
                c = Chain(dve, s_wkv, 6, t)
                c.k = 4
                c(dve.reciprocal(den[:, :], den[:, :]))
                dve.wait_ge(s_th, t + 1)
                after(dve, s_so, t - 1)
                c(dve.scalar_tensor_tensor(num[:, :], rtanh[q][:, :], 1.0, num[:, :], ALU.add, ALU.mult))
                c.end()
                dve.tensor_tensor(rwkv[q][:, :], num[:, :], den[:, :], ALU.mult).then_inc(s_rwkv, 1)

            def experts(half, p, turn):
                now = tile(half, p, turn, 5)
                if now:
                    t, h, q = now
                    dve.wait_ge(s_dn, t + 1)
                    after(dve, s_ys[q % NB], arrivals(h, q) - 16)
                    dve.tensor_scalar(ys_t[q % NB][:, :], psY[:, 0:D], 0.5, None, ALU.mult).then_inc(s_y, 1)
                now = tile(half, p, turn, 2)
                if now:
                    t, h, q = now
                    c = Chain(dve, s_gch, 1, t)
                    dve.wait_ge(s_gate, t + 1)
                    after(dve, s_fh, t - NB + 1)
                    g, u = gate[q % NB], psU[q % 2]
                    c(dve.scalar_tensor_tensor(g[:, :], g[:, :], 1.0, u[:, HID:], ALU.add, ALU.mult))
                    dve.tensor_tensor(hid[q % NB][:, :], u[:, 0:HID], g[:, :], ALU.mult).then_inc(s_hid, 1)
                    c.end()

            def step(half, p):
                e, w = lag(half, p, 2), lag(half, p, 3)
                if runs(w[0]):
                    sums(*w)
                experts(half, p, 0)
                if runs(w[0]):
                    quotient(*w)
                experts(half, p, 1)
                if runs(e[0]):
                    exponents(*e)
                experts(half, p, 2)
            run(dve, step)

        @block.scalar
        def _(act):
            act.wait_ge(s_zcol, 1)

            def normalize(t, h, q):
                after(act, s_tr, t - 1)
                for j in range(TB):
                    n = bass.ds(t * TB + j, 1)
                    last = act.activation(xn_t[q][:, j:j + 1, :], X[:, n, :], ACT.Identity, scale=rstd[:, n],
                                          bias=nmr[:, n])
                last.then_inc(s_xn, 1)

            def transposed(t, h, q):
                act.wait_ge(s_tr, t + 1)
                after(act, s_rp, t - 1)
                act.copy(xnT[q][:, 1:SEQ + 1], psT[:, 0:SEQ]).then_inc(s_xnT, 1)

            def keys_values(t, h, q):
                act.wait_ge(s_kvp, t + 1)
                after(act, s_wkv, 6 * (t - 2) + 1)
                act.copy(kv[q][:, :, :], psKV[:, :].rearrange("p (a n) -> p a n", a=2)).then_inc(s_kv, 1)

            def receptance(t, h, q):
                act.wait_ge(s_rp, t + 1)
                after(act, s_rwkv, t - 1)
                act.activation(rtanh[q][:, :], psR[:, 0:SEQ], ACT.Tanh, scale=0.5).then_inc(s_th, 1)

            def exps(t, h, q):
                act.wait_ge(s_args, t + 1)
                after(act, s_rwkv, t)
                act.activation(ex[:, :, :], args[:, :, :], ACT.Exp).then_inc(s_ex, 1)

            def keep(t, h, q):
                act.wait_ge(s_so, t + 1)
                act.copy(S[:, bass.ds(t * TB, TB), :],
                         psR[:, 0:TB * D].rearrange("p (a n) -> p a n", a=TB)).then_inc(s_s, 1)

            def experts(half, p, turn):
                now = tile(half, p, turn, 0)
                if now:
                    t, h, q = now
                    act.wait_ge(s_fx, t + 1)
                    after(act, s_up, t - NB + 1)
                    act.copy(xsT[q % NB][:, :], psX[:, 0:P]).then_inc(s_xsT, 1)
                now = tile(half, p, turn, 1)
                if now:
                    t, h, q = now
                    act.wait_ge(s_up, t + 1)
                    after(act, s_hid, t - NB + 1)
                    act.activation(gate[q % NB][:, :], psU[q % 2][:, HID:], ACT.Tanh, scale=0.5).then_inc(s_gate, 1)
                now = tile(half, p, turn, 3)
                if now:
                    t, h, q = now
                    act.wait_ge(s_fh, t + 1)
                    after(act, s_dn, t - NB + 1)
                    act.copy(hidT[q % NB][:, :, :], psH[:, 0:2 * P].rearrange("p (c n) -> p c n", c=2)).then_inc(s_hidT, 1)

            def step(half, p):
                a, b, e, k = (lag(half, p, n) for n in (0, 1, 2, 4))
                if runs(a[0]):
                    normalize(*a)
                if runs(k[0]):
                    keep(*k)
                experts(half, p, 0)
                if runs(a[0]):
                    transposed(*a)
                if runs(b[0]):
                    keys_values(*b)
                experts(half, p, 1)
                if runs(b[0]):
                    receptance(*b)
                experts(half, p, 2)
                if runs(e[0]):
                    exps(*e)
            run(act, step)

        @block.tensor
        def _(pe):
            pe.matmul(PS[0][:, 0:NT * NE], earlier[:, :], onehot[:, :, :].rearrange("p t e -> p (t e)"), start=True, stop=True)
            pe.matmul(PS[1][:, 0:NT * NE], ones[:, 0:P], onehot[:, :, :].rearrange("p t e -> p (t e)"),
                      start=True, stop=True).then_inc(s_counts, 1)
            experts_of = [pe.alloc_register(f"expert{i}") for i in range(G)]

            def flip(t, h, q):
                pe.wait_ge(s_xn, t + 1)
                after(pe, s_xnT, t)
                for j in range(TB):
                    last = pe.transpose(psT[:, j * P:(j + 1) * P], xn_t[q][:, j, :], ident[:, :])
                last.then_inc(s_tr, 1)

            def project(t, h, q, j, out, done=None):
                pe.matmul(out, wmix[:, 0, j, :], xnT[q][:, 1:SEQ + 1], start=True, stop=False)
                last = pe.matmul(out, wmix[:, 1, j, :], xnT[q][:, 0:SEQ], start=False, stop=True)
                if done is not None:
                    last.then_inc(done, 1)

            def out_projection(t, h, q):
                pe.wait_ge(s_rwkv, t + 1)
                pe.wait_ge(s_th, min(t + 3, B) if isinstance(t, int) else t + 3)
                after(pe, s_s, t)
                for j in range(TB):
                    last = pe.matmul(psR[:, j * D:(j + 1) * D], rwkv[q][:, j * P:(j + 1) * P], w_out[:, :],
                                     start=True, stop=True)
                last.then_inc(s_so, 1)

            def transposes(half, p, turn):
                now = tile(half, p, turn, 0)
                if now:
                    t, h, q = now
                    pe.wait_ge(s_xs[q % NB], arrivals(h, q))
                    after(pe, s_xsT, t)
                    pe.transpose(psX[:, 0:P], xs_t[q % NB][:, :], ident[:, :]).then_inc(s_fx, 1)
                now = tile(half, p, turn, 3)
                if now:
                    t, h, q = now
                    pe.wait_ge(s_hid, t + 1)
                    after(pe, s_hidT, t)
                    for c in range(2):
                        last = pe.transpose(psH[:, c * P:(c + 1) * P], hid[q % NB][:, c * P:(c + 1) * P], ident[:, :])
                    last.then_inc(s_fh, 1)

            def products(half, p, turn):
                now = tile(half, p, turn, 4)
                if now:
                    t, h, q = now
                    e = pe.snap(experts_of[q], min_val=0, max_val=NE - 1)
                    pe.wait_ge(s_hidT, t + 1)
                    after(pe, s_y, t)
                    for c in range(2):
                        last = pe.matmul(psY[:, 0:D], hidT[q % NB][:, c, :], down[:, bass.ds(e * 2 * D + c * D, D)],
                                         start=(c == 0), stop=(c == 1))
                    last.then_inc(s_dn, 1)
                new = tile(half, p, turn, 0)
                if turn == 0 and new:
                    t, h, q = new
                    pe.load(experts_of[q:q + TPS], tile_expert[0:1, bass.ds(t, TPS)])
                now = tile(half, p, turn, 1)
                if now:
                    t, h, q = now
                    e = pe.snap(experts_of[q], min_val=0, max_val=NE - 1)
                    pe.wait_ge(s_xsT, t + 1)
                    after(pe, s_hid, t - 1)
                    pe.matmul(psU[q % 2][:, :], xsT[q % NB][:, :], up[:, bass.ds(e * 2 * HID, 2 * HID)],
                              start=True, stop=True).then_inc(s_up, 1)

            def step(half, p):
                if isinstance(half, int) and 2 * half + p == FIRST:
                    pe.wait_ge(s_placed, 1)
                a, b, w = (lag(half, p, n) for n in (0, 1, 3))
                if runs(a[0]):
                    flip(*a)
                transposes(half, p, 0)
                if runs(b[0]):
                    pe.wait_ge(s_xnT, b[0] + 1)
                    after(pe, s_kv, b[0])
                    project(*b, 0, psKV[:, 0:SEQ])
                products(half, p, 0)
                transposes(half, p, 1)
                if runs(b[0]):
                    project(*b, 1, psKV[:, SEQ:], s_kvp)
                products(half, p, 1)
                transposes(half, p, 2)
                if runs(b[0]):
                    after(pe, s_s, b[0] - 2)
                    project(*b, 2, psR[:, 0:SEQ], s_rp)
                if runs(w[0]):
                    out_projection(*w)
                products(half, p, 2)
            run(pe, step)


def layer_one(nc, X, S, rstd, nmr, slot, ident, ones, mhalf, PS, ys_dram, parts_dram, mrow_dram, l1_w, out_b,
              qkv_w, qkv_b, wr, br, wo, bo, out):
    with ExitStack() as ctx:
        def sb(name, shape, dt=fp32):
            return ctx.enter_context(nc.sbuf_tensor(name, shape, dt))

        def two(name, shape, dt=fp32):
            return [sb(f"{name}{i}", shape, dt) for i in range(2)]

        def sem(name):
            return ctx.enter_context(nc.semaphore(name))

        def sem2(name):
            return [sem(f"{name}{i}") for i in range(2)]

        NP3 = 3
        ROWS = [(0, 0), (0, 1), (0, 2), (1, 0), (1, 1), (2, 0)]
        MROW = 96
        VC = 32
        SS, CS, NS = 2, 5, 22

        identb = sb("identb", [P, P], bf16)
        w1 = sb("w1", [P, 4, D])
        outb_b = sb("outb_b", [P, D])
        bo_b = sb("bo_b", [P, D])
        br_b = sb("br_b", [P, RH])
        wr_s = sb("wr_s", [P, RH])
        wo_s = sb("wo_s", [P, 2, D])
        zerob = sb("zerob", [NP3, H * SEQ], bf16)
        Y = two("Y", [P, TB, D])
        slot_t = two("slot_t", [P, TB], i32)
        xnf = two("xnf", [P, TB, D])
        z = two("z", [P, TB, D])
        zt = two("zt", [P, TB, D])
        st = sb("st", [P, TB, 6])
        mva = sb("mva", [P, TB, 2])
        rs = sb("rs", [P, TB])
        xn1 = two("xn1", [P, TB, D])
        xT = two("xT", [P, SEQ])
        qk = sb("qk", [P, 2, SEQ])
        rest = sb("rest", [P, 2, SEQ])
        parts = two("parts", [P, 2, NP3, SEQ], bf16)
        xsum = sb("xsum", [P, 1])
        xsb = sb("xsb", [P, P])
        lg = sb("lg", [P, RH])
        top = sb("top", [P, 8])
        ntop = sb("ntop", [P, 1])
        prob = sb("prob", [P, RH])
        psum_ = sb("prob_sum", [P, 1])
        pinv = sb("prob_inv", [P, 1])
        ptop = sb("ptop", [P, 8])
        pidx = sb("pidx", [P, 8], u32)
        idx = two("idx", [1, 8], i32)
        nptop = sb("nptop", [P, 1])
        g5 = sb("g5", [P, RK + 1])
        gsum = sb("gsum", [P, 1])
        g4 = sb("g4", [P, RK])
        gc = two("gc", [P, 2, 3])
        QS = two("QS", [P, H, SEQ], bf16)
        KS = two("KS", [P, H, SEQ], bf16)
        bm = sb("bm", [P, TB, H, NBLK])
        m3 = sb("m3", [P, TB, H])
        nm = sb("nm", [P, TB, H])
        nmr_ = sb("nm_rest", [P, TB, H])
        cdiff = sb("cdiff", [P, TB, H])
        corr = sb("corr", [P, TB, H])
        fac = two("fac", [P, TB, H])
        mp = sb("mp", [P, TB, NP3, H], bf16)
        mT = two("mT", [NP3 * H, SEQ], bf16)
        V2 = two("V2", [P, TB, H, VC])
        wsel = two("wsel", [P, 2, 3, P])
        bsel = two("bsel", [P, 2, 3])
        gb = two("gb", [P, 2, 3])
        Qf = sb("Qf", [P, 2, SEQ])
        Kz = sb("Kz", [P, 2, 2, SEQ])
        Vf = sb("Vf", [P, TB, RK * RD])
        nmf = sb("nmf", [P, TB])
        Pf = sb("Pf", [P, TB, SEQ])
        lsum = sb("lsum", [P, TB, RK])
        linv = sb("linv", [P, TB * RK])
        PTf = sb("PTf", [P, TB, SEQ])
        On = sb("On", [P, TB * RK, RD])
        PT = [sb(f"PT{i}", [P, TB * SEQ]) for i in range(8)]
        OT = two("OT", [P, SEQ])
        lf = sb("lf", [P, TB, 4])
        attn = two("attn", [P, TB, H, HD])
        attnT = sb("attnT", [P, SEQ])
        OTf = sb("OTf", [P, 2, SEQ])
        y2 = sb("y2", [P, TB, D])
        y2t = sb("y2t", [P, TB, D])
        g2 = two("g2", [P, TB, D])
        s1 = sb("s1", [P, TB, D])
        o_t = two("o_t", [P, TB, D])

        s_w = sem("l1_weights")
        s_c0 = sem("l1_consts_pool")
        s_c1 = sem("l1_consts_dve")
        s_slot = sem("slots_copied")
        s_fac = sem("factor_ready")
        s_g2 = sem("gate_two_ready")
        s_gch = sem("gate_chain3")
        s_y = sem2("expert_out_gathered")
        s_xnf = sem("xn_ready")
        s_z = sem("z_ready")
        s_zt = sem("z_tanh_ready")
        s_gz = sem("z_gated")
        s_x1c = sem("x1_chain")
        s_x1 = sem("x1_ready")
        s_lnc = sem("ln_chain")
        s_ve = sem("x1_variance_ready")
        s_rs = sem("x1_rstd_ready")
        s_xn1 = sem("xn1_ready")
        s_f1 = sem("x1_transposed")
        s_xT = sem("xT_ready")
        s_qkp = sem("qk_in_psum")
        s_qk = sem("qk_ready")
        s_hi = sem("qk_high_ready")
        s_spc = sem("split_chain")
        s_parts = sem("parts_ready")
        s_pst = sem2("parts_stored")
        s_xsc = sem("xsum_chain")
        s_xsb = sem("xsum_ready")
        s_lgp = sem("logits_in_psum")
        s_lgc = sem("router_chain")
        s_lg = sem("logits_read")
        s_lg2 = sem("logit_max_ready")
        s_pe1 = sem("probs_exp_ready")
        s_pt = sem("prob_top_ready")
        s_pe2 = sem("gates_exp_ready")
        s_idx = sem("heads_chosen")
        s_gc = sem("gates_ready")
        s_wl = sem2("head_weights_loaded")
        s_ql = sem2("qs_ks_loaded")
        s_sp = sem("scores_in_psum")
        s_red = sem("block_maxima_read")
        s_mc = sem("max_chain")
        s_cd = sem("max_difference_ready")
        s_corr = sem("correction_ready")
        s_mp = sem("max_parts_ready")
        s_mTp = sem("max_transposed")
        s_mT = sem("mT_ready")
        s_ms = sem2("max_rows_stored")
        s_ml = sem2("max_rows_loaded")
        s_vp = sem("v_in_psum")
        s_v2 = sem("V2_ready")
        s_gb = sem("head_biases_ready")
        s_fqp = sem("head_qk_in_psum")
        s_fq = sem("head_qk_ready")
        s_fvp = sem("head_v_in_psum")
        s_fv = sem("head_v_ready")
        s_fs = sem("head_scores_in_psum")
        s_fm = sem("head_max_ready")
        s_pf = sem("head_probs_ready")
        s_ptp = sem("head_probs_transposed")
        s_ptf = sem("head_PT_ready")
        s_of = sem("head_out_in_psum")
        s_ofc = sem("head_out_chain")
        s_on = sem("head_out_ready")
        s_otp = sem("head_out_transposed")
        s_otf = sem("head_OT_ready")
        s_wop = sem("routed_out_in_psum")
        s_y2 = sem("routed_out_ready")
        s_y2t = sem("routed_tanh_ready")
        s_st = sem("shifted_scores_in_psum")
        s_exp = sem("exp_scores_ready")
        s_pv = sem("values_in_psum")
        s_oe = sem("OT_ready")
        s_ot = sem("O_transposed")
        s_nc = sem("norm_chain3")
        s_an = sem("attn_normalized")
        s_atp = sem("attn_transposed")
        s_at = sem("attnT_ready")
        s_op = sem("attn_out_in_psum")
        s_fc = sem("final_chain")
        s_fin = sem("attn_out_read")
        s_done = sem("out_ready")
        s_out = sem2("out_stored")

        bS, bT, bC, bA, bF1, bF2 = PS[0:2], PS[2:4], PS[4], PS[5], PS[6], PS[7]
        bAb = bA[:, :].bitcast(bf16)

        def lag(half, p, k):
            h, q = half + (p - k) // 2, (p - k) % 2
            return 2 * h + q, h, q

        def runs(t):
            return not isinstance(t, int) or 0 <= t < B

        def run(eng, step):
            for t in range(6):
                step(t // 2, t % 2)
            with eng.Fori(3, B // 2) as half:
                step(half, 0)
                step(half, 1)
            for t in range(B, B + 4):
                step(t // 2, t % 2)

        def most(t):
            return min(t, B) if isinstance(t, int) else t

        def tiles(t):
            return bass.ds(t * TB, TB)

        block = ctx.enter_context(nc.Block())

        @block.sync
        def _(sp):
            for dst, src in ((w1[:, :, :], l1_w), (outb_b[:, :], out_b.to_broadcast([P, D])),
                             (bo_b[:, :], bo.to_broadcast([P, D])), (br_b[:, :], br.to_broadcast([P, RH])),
                             (wr_s[:, :], wr), (wo_s[:, :, :], wo)):
                sp.dma_start(dst, src).then_inc(s_w, 16)
            sp.wait_ge(s_c1, 2)

            def load_qk(t, h, q):
                sp.wait_ge(s_pst[q], 16 * h + 16)
                apart(sp)
                after(sp, s_st, H * (t - 1))
                apart(sp)
                for r, parts_of in enumerate(ROWS):
                    for k, tile in enumerate((QS[q], KS[q])):
                        src = parts_dram[q, k, parts_of[k]].rearrange("(h d) t -> d h t", d=HD)
                        sp.dma_start(tile[r * HD:(r + 1) * HD, :, :], src).then_inc(s_ql[q], 16)
                sp.dma_start(QS[q][MROW:MROW + NP3, :, :].rearrange("p h t -> p (h t)"), zerob[:, :]).then_inc(s_ql[q], 16)

            def load_max(t, h, q):
                sp.wait_ge(s_mT, t + 1)
                apart(sp)
                sp.wait_ge(s_sp, H * (t + 1))
                apart(sp)
                sp.dma_start(mrow_dram[q].rearrange("a h t -> (a h) t"), mT[q][:, :]).then_inc(s_ms[q], 16)
                sp.wait_ge(s_ms[q], 16 * h + 16)
                apart(sp)
                sp.dma_start(QS[q][MROW:MROW + NP3, :, :], mrow_dram[q]).then_inc(s_ml[q], 16)

            def load_heads(t, h, q):
                sp.wait_ge(s_idx, t + 1)
                apart(sp)
                after(sp, s_fv, t - 1)
                apart(sp)
                after(sp, s_gb, t - 1)
                apart(sp)
                for j in range(RK):
                    head = sp.value_load(idx[q][0:1, j:j + 1], min_val=0, max_val=RH - 1)
                    i, jj = j // 2, j % 2
                    sp.dma_start(wsel[q][:, i, :, jj * RD:(jj + 1) * RD],
                                 qkv_w[bass.ds(head, 1), :, :, :].rearrange("a p c d -> (a p) c d")).then_inc(s_wl[q], 16)
                    sp.dma_start(bsel[q][jj * RD:(jj + 1) * RD, i, :],
                                 qkv_b[bass.ds(head, 1), :, :].rearrange("a d c -> (a d) c")).then_inc(s_wl[q], 16)

            def store_parts(t, h, q):
                sp.wait_ge(s_parts, t + 1)
                apart(sp)
                after(sp, s_ql[q], 16 * 13 * h)
                apart(sp)
                sp.dma_start(parts_dram[q].rearrange("k a p t -> p k a t"), parts[q][:, :, :, :]).then_inc(s_pst[q], 16)

            def store_out(t, h, q):
                sp.wait_ge(s_done, t + 1)
                apart(sp)
                sp.dma_start(out[bass.ds(t * SEQ, SEQ), :].rearrange("(j p) n -> p j n", p=P),
                             o_t[q][:, :, :]).then_inc(s_out[q], 16)

            def step(half, p):
                batch1, batch2, batch4 = (lag(half, p, k) for k in (1, 2, 4))
                run1, run2, run4 = (runs(b[0]) for b in (batch1, batch2, batch4))
                if run1:
                    store_parts(*batch1)
                    load_heads(*batch1)
                if run4:
                    store_out(*batch4)
                if run1:
                    load_qk(*batch1)
                if run2:
                    load_max(*batch2)
            run(sp, step)
            for q in range(2):
                sp.wait_ge(s_out[q], 16 * (B // 2))

        @block.gpsimd
        def _(pool):
            pool.memset(zerob[:, :], 0.0)
            for i in range(2):
                pool.memset(QS[i][:, :, :], 0.0)
                pool.memset(KS[i][:, :, :], 0.0)
                pool.memset(V2[i][:, :, :, :], 0.0)
            pool.memset(Kz[:, :, :, :], 0.0).then_inc(s_c0, 1)
            pool.wait_ge(s_c0, 1)
            pool.tensor_copy(identb[:, :], ident[:, :]).then_inc(s_c1, 1)

            def gather(t, h, q):
                pool.tensor_copy(slot_t[q][:, :], slot[:, tiles(t)]).then_inc(s_slot, 1)
                pool.wait_ge(s_slot, t + 1)
                after(pool, s_z, t - 1)
                apart(pool)
                for j in range(TB):
                    pool.indirect_dma_start(Y[q][:, j, :], None, ys_dram,
                                            bass.IndirectOffsetOnAxis(slot_t[q][:, j:j + 1], axis=0)).then_inc(s_y[q], 16)

            def add_skip(t, h, q):
                pool.wait_ge(s_y[q], 32 * h + 32)
                pool.wait_ge(s_xnf, t + 1)
                after(pool, s_gz, t - 1)
                pool.tensor_tensor(z[q][:, :, :], Y[q][:, :, :], xnf[q][:, :, :], ALU.add).then_inc(s_z, 1)

            def residual(t, h, q):
                pool.wait_ge(s_gz, t + 1)
                ch = Chain(pool, s_x1c, 1, t)
                ch(pool.tensor_tensor(zt[q][:, :, :], zt[q][:, :, :], S[:, tiles(t), :], ALU.mult))
                ch.end()
                pool.tensor_tensor(X[:, tiles(t), :], X[:, tiles(t), :], zt[q][:, :, :], ALU.add).then_inc(s_x1, 1)

            def inverse_std(t, h, q):
                pool.wait_ge(s_ve, t + 1)
                pool.tensor_tensor(rs[:, :], rs[:, :], mhalf[:, 0:TB], ALU.pow).then_inc(s_rs, 1)

            def split(t, h, q):
                ch = Chain(pool, s_spc, 2, t)
                pool.wait_ge(s_hi, t + 1)
                ch(pool.tensor_tensor(rest[:, :, :], qk[:, :, :], parts[q][:, :, 0, :], ALU.subtract))
                apart(pool)
                ch(pool.tensor_copy(parts[q][:, :, 1, :], rest[:, :, :]))
                pool.tensor_tensor(parts[q][:, :, 2, :], rest[:, :, :], parts[q][:, :, 1, :], ALU.subtract).then_inc(s_parts, 1)
                ch.end()

            def step(half, p):
                batch0, batch1 = (lag(half, p, k) for k in (0, 1))
                run0, run1 = (runs(b[0]) for b in (batch0, batch1))
                if run1:
                    residual(*batch1)
                    inverse_std(*batch1)
                    split(*batch1)
                if run0:
                    gather(*batch0)
                    add_skip(*batch0)
            run(pool, step)

        @block.vector
        def _(dve):
            dve.wait_ge(s_w, 16 * 6)
            dve.wait_ge(s_c0, 1)
            for i in range(2):
                dve.memset(KS[i][MROW:MROW + NP3, :, :], 1.0)
                last = dve.memset(V2[i][P - BLK:P, TB - 1, :, HD:HD + 1], 1.0)
            last.then_inc(s_c1, 1)
            dve.wait_ge(s_c1, 2)

            def gated(t, h, q):
                dve.wait_ge(s_zt, t + 1)
                dve.scalar_tensor_tensor(zt[q][:, :, :].rearrange("p j n -> p (j n)"),
                                         zt[q][:, :, :].rearrange("p j n -> p (j n)"), 1.0,
                                         z[q][:, :, :].rearrange("p j n -> p (j n)"), ALU.add, ALU.mult).then_inc(s_gz, 1)

            def ln_stats(t, h, q):
                dve.wait_ge(s_x1, t + 1)
                ch = Chain(dve, s_lnc, 2, t)
                for j in range(TB):
                    last = dve.bn_stats(st[:, j, :], X[:, bass.ds(t * TB + j, 1), :].rearrange("p a n -> p (a n)"))
                ch(last)
                apart(dve)
                for j in range(TB):
                    last = dve.bn_aggr(mva[:, j, :], st[:, j, :])
                ch(last)
                ch.end()
                dve.tensor_scalar(rs[:, :], mva[:, :, 1], LN_EPS, None, ALU.add).then_inc(s_ve, 1)

            def ln_apply(t, h, q):
                dve.wait_ge(s_rs, t + 1)
                after(dve, s_f1, t - 1)
                for j in range(TB):
                    last = dve.tensor_scalar(xn1[q][:, j:j + 1, :], X[:, bass.ds(t * TB + j, 1), :],
                                             mva[:, j, 0:1], rs[:, j:j + 1], ALU.subtract, ALU.mult)
                last.then_inc(s_xn1, 1)

            def token_sum(t, h, q):
                dve.wait_ge(s_xT, t + 1)
                after(dve, s_lgp, t)
                ch = Chain(dve, s_xsc, 1, t)
                ch(dve.tensor_reduce(xsum[:, :], xT[q][:, :], AX.X, ALU.add))
                ch.end()
                dve.tensor_scalar(xsb[:, :], ones[:, 0:P], xsum[:, 0:1], 1.0 / SEQ, ALU.mult, ALU.mult).then_inc(s_xsb, 1)

            def route_a(t, h, q):
                dve.wait_ge(s_lgp, t + 1)
                ch = Chain(dve, s_lgc, 5, t)
                dve.tensor_tensor(lg[:, :], bA[:, 0:RH], br_b[:, :], ALU.add).then_inc(s_lg, 1)
                dve.wait_ge(s_lg, t + 1)
                apart(dve)
                ch(dve.max(top[:, :], lg[:, :]))
                dve.tensor_scalar(ntop[:, :], top[:, 0:1], -1.0, None, ALU.mult).then_inc(s_lg2, 1)

            def route_b(t, h, q):
                dve.wait_ge(s_pe1, t + 1)
                ch = Chain(dve, s_lgc, 5, t)
                ch.k = 1
                ch(dve.reciprocal(pinv[:, :], psum_[:, :]))
                ch(dve.tensor_scalar(prob[:, :], prob[:, :], pinv[:, 0:1], None, ALU.mult))
                apart(dve)
                ch(dve.max(ptop[:, :], prob[:, :]))
                dve.tensor_scalar(nptop[:, :], ptop[:, 0:1], -1.0, None, ALU.mult).then_inc(s_pt, 1)
                apart(dve)
                ch(dve.max_index(pidx[:, :], ptop[:, :], prob[:, :]))
                after(dve, s_wl[q], 128 * h)
                dve.tensor_copy(idx[q][:, :], pidx[0:1, :]).then_inc(s_idx, 1)
                ch.end()

            def route_c(t, h, q):
                dve.wait_ge(s_pe2, t + 1)
                ch = Chain(dve, s_gch, 5, t)
                ch(dve.tensor_reduce(gsum[:, :], g5[:, 0:RK], AX.X, ALU.add))
                ch(dve.scalar_tensor_tensor(gsum[:, :], g5[:, RK:RK + 1], float(RH - RK), gsum[:, :], ALU.mult, ALU.add))
                ch(dve.reciprocal(gsum[:, :], gsum[:, :]))
                ch(dve.tensor_scalar(g4[:, :], g5[:, 0:RK], gsum[:, 0:1], None, ALU.mult))
                g4v = g4[:, :].rearrange("p (i j) -> p i j", j=2)
                for jj in range(2):
                    rows = slice(jj * RD, (jj + 1) * RD)
                    last = dve.tensor_copy(gc[q][rows, :, :], g4v[rows, :, jj:jj + 1].broadcast_to([RD, 2, 3]))
                ch(last)
                ch.end()
                dve.tensor_scalar(gc[q][:, :, 0], gc[q][:, :, 0], RD ** -0.5, None, ALU.mult).then_inc(s_gc, 1)

            def head_biases(t, h, q):
                dve.wait_ge(s_gc, t + 1)
                dve.wait_ge(s_wl[q], 128 * h + 128)
                dve.tensor_tensor(gb[q][:, :, :], bsel[q][:, :, :], gc[q][:, :, :], ALU.mult).then_inc(s_gb, 1)

            def block_max(t, h, q, s):
                dve.wait_ge(s_sp, H * t + s + 1)
                qt, h0 = s // 8, 2 * (s % 8)
                dve.tensor_reduce(bm[:, qt, h0:h0 + 2, :],
                                  bS[s % 2][:, :].rearrange("p (h b k) -> p h b k", h=2, b=NBLK), AX.X, ALU.max)\
                   .then_inc(s_red, 1)

            def row_max(t, h, q):
                ch = Chain(dve, s_mc, 6, t)
                dve.wait_ge(s_red, H * (t + 1))
                ch(dve.tensor_reduce(m3[:, :, :], bm[:, :, :, 0:NBLK - 1], AX.X, ALU.max))
                ch(dve.tensor_tensor(nm[:, :, :], m3[:, :, :], bm[:, :, :, NBLK - 1], ALU.max))
                after(dve, s_corr, t)
                dve.tensor_tensor(cdiff[:, :, :], m3[:, :, :], nm[:, :, :], ALU.subtract).then_inc(s_cd, 1)
                ch(dve.tensor_scalar(nm[:, :, :], nm[:, :, :], -1.0, None, ALU.mult))
                after(dve, s_mTp, t)
                ch(dve.tensor_copy(mp[:, :, 0, :], nm[:, :, :]))
                ch(dve.tensor_tensor(nmr_[:, :, :], nm[:, :, :], mp[:, :, 0, :], ALU.subtract))
                ch(dve.tensor_copy(mp[:, :, 1, :], nmr_[:, :, :]))
                dve.tensor_tensor(mp[:, :, 2, :], nmr_[:, :, :], mp[:, :, 1, :], ALU.subtract).then_inc(s_mp, 1)
                ch.end()

            def factor(t, h, q):
                dve.wait_ge(s_corr, t + 1)
                dve.tensor_scalar(fac[q][:, :, :], corr[:, :, :], 1.0, None, ALU.add).then_inc(s_fac, 1)

            def head_max(t, h, q, j):
                dve.wait_ge(s_fs, RK * t + j + 1)
                after(dve, s_pf, RK * t + j)
                dve.tensor_reduce(nmf[:, :], bF1[:, :].rearrange("p (a k) -> p a k", a=TB), AX.X, ALU.max,
                                  negate=True).then_inc(s_fm, 1)

            def head_pt(t, h, q, j):
                dve.wait_ge(s_ptp, RK * t + j + 1)
                after(dve, s_of, RK * t + j)
                dve.tensor_copy(PTf[:, :, :], bF1[:, :].rearrange("p (a k) -> p a k", a=TB)).then_inc(s_ptf, 1)

            def head_out(t, h, q):
                dve.wait_ge(s_of, RK * (t + 1))
                after(dve, s_otp, t)
                ch = Chain(dve, s_ofc, 1, t)
                ch(dve.reciprocal(linv[:, :], lsum[:, :, :].rearrange("p a j -> p (a j)")))
                ch.end()
                dve.tensor_tensor(On[:, :, :], bF2[:, :].rearrange("p (n d) -> p n d", d=RD),
                                  linv[:, :].unsqueeze(2).broadcast_to([P, TB * RK, RD]), ALU.mult).then_inc(s_on, 1)

            def routed_out(t, h, q):
                dve.wait_ge(s_wop, t + 1)
                after(dve, s_y2t, t)
                dve.tensor_tensor(y2[:, :, :], bF2[:, 0:TB * D].rearrange("p (j n) -> p j n", j=TB),
                                  bo_b[:, :].unsqueeze(1).broadcast_to([P, TB, D]), ALU.add).then_inc(s_y2, 1)

            def routed_gate(t, h, q):
                dve.wait_ge(s_y2t, t + 1)
                dve.scalar_tensor_tensor(g2[q][:, :, :].rearrange("p j n -> p (j n)"),
                                         y2t[:, :, :].rearrange("p j n -> p (j n)"), 1.0,
                                         y2[:, :, :].rearrange("p j n -> p (j n)"), ALU.add, ALU.mult).then_inc(s_g2, 1)

            def attn_norm(t, h, q, g):
                dve.wait_ge(s_ot, 4 * t + g + 1)
                dve.wait_ge(s_fac, t + 1)
                after(dve, s_atp, t - 1)
                ch = Chain(dve, s_nc, 8, t)
                ch.k = 2 * g
                o = bC[:, 0:SEQ].rearrange("p (a j c) -> p a j c", a=TB, c=VC)
                ch(dve.tensor_tensor(lf[:, :, :], o[:, :, :, HD], fac[q][:, :, 4 * g:4 * g + 4], ALU.mult))
                ch(dve.reciprocal(lf[:, :, :], lf[:, :, :]))
                dve.tensor_tensor(attn[q][:, :, 4 * g:4 * g + 4, :], o[:, :, :, 0:HD],
                                  lf[:, :, :].unsqueeze(3).broadcast_to([P, TB, 4, HD]), ALU.mult).then_inc(s_an, 1)

            def final(t, h, q):
                dve.wait_ge(s_op, t + 1)
                dve.wait_ge(s_g2, t + 1)
                ch = Chain(dve, s_fc, 2, t)
                dve.tensor_tensor(s1[:, :, :], bC[:, 0:TB * D].rearrange("p (j n) -> p j n", j=TB),
                                  outb_b[:, :].unsqueeze(1).broadcast_to([P, TB, D]), ALU.add).then_inc(s_fin, 1)
                dve.wait_ge(s_fin, t + 1)
                f = "p j n -> p (j n)"
                ch(dve.scalar_tensor_tensor(s1[:, :, :].rearrange(f), s1[:, :, :].rearrange(f), 0.5,
                                            g2[q][:, :, :].rearrange(f), ALU.mult, ALU.mult))
                after(dve, s_out[q], 16 * h)
                ch(dve.tensor_tensor(o_t[q][:, :, :], s1[:, :, :], X[:, tiles(t), :], ALU.add))
                dve.sem_inc(s_done, 1)
                ch.end()

            def step(half, p):
                batch1, batch2, batch3, batch4 = (lag(half, p, k) for k in (1, 2, 3, 4))
                run1, run2, run3, run4 = (runs(b[0]) for b in (batch1, batch2, batch3, batch4))
                if run4:
                    attn_norm(*batch4, 2)
                if run3:
                    routed_out(*batch3)
                if run2:
                    block_max(*batch2, 0)
                if run1:
                    gated(*batch1)
                if run4:
                    attn_norm(*batch4, 3)
                if run2:
                    block_max(*batch2, 1)
                if run3:
                    routed_gate(*batch3)
                if run2:
                    block_max(*batch2, 2)
                if run1:
                    ln_stats(*batch1)
                if run2:
                    block_max(*batch2, 3)
                    head_max(*batch2, 0)
                    block_max(*batch2, 4)
                if run1:
                    ln_apply(*batch1)
                if run2:
                    block_max(*batch2, 5)
                    head_pt(*batch2, 0)
                if run4:
                    final(*batch4)
                if run2:
                    block_max(*batch2, 6)
                    head_max(*batch2, 1)
                if run1:
                    token_sum(*batch1)
                if run2:
                    block_max(*batch2, 7)
                    block_max(*batch2, 8)
                    block_max(*batch2, 9)
                    head_pt(*batch2, 1)
                    block_max(*batch2, 10)
                if run1:
                    route_a(*batch1)
                if run3:
                    attn_norm(*batch3, 0)
                if run2:
                    block_max(*batch2, 11)
                if run1:
                    route_b(*batch1)
                if run2:
                    head_max(*batch2, 2)
                    block_max(*batch2, 12)
                    block_max(*batch2, 13)
                    head_pt(*batch2, 2)
                    block_max(*batch2, 14)
                if run1:
                    route_c(*batch1)
                if run2:
                    block_max(*batch2, 15)
                    head_max(*batch2, 3)
                if run3:
                    attn_norm(*batch3, 1)
                if run2:
                    row_max(*batch2)
                    head_pt(*batch2, 3)
                    factor(*batch2)
                    head_out(*batch2)
                if run1:
                    head_biases(*batch1)
            run(dve, step)

        @block.scalar
        def _(act):
            act.wait_ge(s_c1, 2)

            def normalized(t, h, q):
                after(act, s_z, t - 1)
                for j in range(TB):
                    n = bass.ds(t * TB + j, 1)
                    last = act.activation(xnf[q][:, j:j + 1, :], X[:, n, :], ACT.Identity, scale=rstd[:, n],
                                          bias=nmr[:, n])
                last.then_inc(s_xnf, 1)

            def z_tanh(t, h, q):
                act.wait_ge(s_z, t + 1)
                after(act, s_x1, t - 1)
                act.activation(zt[q][:, :, :], z[q][:, :, :], ACT.Tanh, scale=0.5).then_inc(s_zt, 1)

            def xT_copy(t, h, q):
                act.wait_ge(s_f1, t + 1)
                after(act, s_fv, t - 1)
                after(act, s_v2, t - 1)
                after(act, s_xsb, t - 1)
                act.copy(xT[q][:, :], bA[:, 0:SEQ]).then_inc(s_xT, 1)

            def qk_copy(t, h, q):
                act.wait_ge(s_qkp, t + 1)
                after(act, s_parts, t)
                act.mul(qk[:, 0, :], bA[:, 0:SEQ], HD ** -0.5)
                act.copy(qk[:, 1, :], bA[:, SEQ:]).then_inc(s_qk, 1)
                act.wait_ge(s_qk, t + 1)
                after(act, s_pst[q], 16 * h)
                act.copy(parts[q][:, :, 0, :], qk[:, :, :]).then_inc(s_hi, 1)

            def probs(t, h, q):
                act.wait_ge(s_lg2, t + 1)
                act.activation(prob[:, :], lg[:, :], ACT.Exp, bias=ntop[:, 0:1], accum_out=psum_[:, :]).then_inc(s_pe1, 1)

            def gate_exps(t, h, q):
                act.wait_ge(s_pt, t + 1)
                act.activation(g5[:, 0:RK], ptop[:, 0:RK], ACT.Exp, bias=nptop[:, 0:1])
                act.activation(g5[:, RK:RK + 1], nptop[:, 0:1], ACT.Exp).then_inc(s_pe2, 1)

            def v_copy(t, h, q):
                act.wait_ge(s_vp, t + 1)
                after(act, s_pv, 4 * (t - 1))
                act.copy(V2[q][:, :, :, 0:HD], bA[:, 0:TB * D].rearrange("p (a h d) -> p a h d", a=TB, h=H)).then_inc(s_v2, 1)

            def mT_copy(t, h, q):
                act.wait_ge(s_mTp, t + 1)
                after(act, s_ms[q], 16 * h)
                act.copy(mT[q][:, :], bAb[0:NP3 * H, 0:SEQ]).then_inc(s_mT, 1)

            def correction(t, h, q):
                act.wait_ge(s_cd, t + 1)
                after(act, s_fac, t)
                act.activation(corr[:, :, :], cdiff[:, :, :], ACT.Exp).then_inc(s_corr, 1)

            def head_qk(t, h, q, i):
                act.wait_ge(s_fqp, 2 * t + i + 1)
                if i == 0:
                    act.wait_ge(s_gb, t + 1)
                    after(act, s_fs, RK * t)
                act.activation(Qf[:, i, :], bF2[:, 0:SEQ], ACT.Identity, scale=gc[q][:, i, 0:1], bias=gb[q][:, i, 0:1])
                for jj in range(2):
                    rows = slice(jj * RD, (jj + 1) * RD)
                    last = act.activation(Kz[rows, i, jj, :], bF2[rows, SEQ:], ACT.Identity,
                                          scale=gc[q][rows, i, 1:2], bias=gb[q][rows, i, 1:2])
                last.then_inc(s_fq, 1)

            def head_v(t, h, q):
                act.wait_ge(s_fvp, t + 1)
                after(act, s_of, RK * t)
                act.copy(Vf[:, :, :], bF2[:, :].rearrange("p (a n) -> p a n", a=TB)).then_inc(s_fv, 1)

            def head_exp(t, h, q, j):
                act.wait_ge(s_fm, RK * t + j + 1)
                after(act, s_ptp, RK * t + j)
                if j == 0:
                    after(act, s_on, t)
                for qt in range(TB):
                    last = act.activation(Pf[:, qt, :], bF1[:, qt * SEQ:(qt + 1) * SEQ], ACT.Exp,
                                          bias=nmf[:, qt:qt + 1], accum_out=lsum[:, qt, j:j + 1])
                last.then_inc(s_pf, 1)

            def head_ot(t, h, q):
                act.wait_ge(s_otp, t + 1)
                after(act, s_wop, t)
                for i in range(2):
                    last = act.activation(OTf[:, i, :], bF2[:, i * SEQ:(i + 1) * SEQ], ACT.Identity,
                                          scale=gc[q][:, i, 2:3], bias=gb[q][:, i, 2:3])
                last.then_inc(s_otf, 1)

            def routed_tanh(t, h, q):
                act.wait_ge(s_y2, t + 1)
                after(act, s_g2, t)
                act.activation(y2t[:, :, :], y2[:, :, :], ACT.Tanh, scale=0.5).then_inc(s_y2t, 1)

            def exp_scores(t, half, q, h):
                act.wait_ge(s_st, H * t + h + 1)
                after(act, s_pv, 4 * t + h // 4 - 1)
                act.activation(PT[h % 8][:, :], bT[h % 2][:, :], ACT.Exp).then_inc(s_exp, 1)

            def ot_copy(t, h, q, g):
                act.wait_ge(s_pv, 4 * t + g + 1)
                after(act, s_ot, 4 * t + g - 1)
                act.copy(OT[g % 2][:, :], bC[:, 0:SEQ]).then_inc(s_oe, 1)

            def attnT_copy(t, h, q):
                act.wait_ge(s_atp, t + 1)
                after(act, s_op, t)
                act.copy(attnT[:, :], bC[:, 0:SEQ]).then_inc(s_at, 1)

            def step(half, p):
                batch0, batch1, batch2, batch3, batch4 = (lag(half, p, k) for k in (0, 1, 2, 3, 4))
                run0, run1, run2, run3, run4 = (runs(b[0]) for b in (batch0, batch1, batch2, batch3, batch4))
                if run3:
                    mT_copy(*batch3)
                if run4:
                    ot_copy(*batch4, 3)
                if run3:
                    routed_tanh(*batch3)
                if run2:
                    head_qk(*batch2, 0)
                    head_qk(*batch2, 1)
                if run3:
                    exp_scores(*batch3, 0)
                if run2:
                    head_v(*batch2)
                if run4:
                    attnT_copy(*batch4)
                if run2:
                    head_exp(*batch2, 0)
                if run3:
                    exp_scores(*batch3, 1)
                    exp_scores(*batch3, 2)
                    exp_scores(*batch3, 3)
                if run1:
                    xT_copy(*batch1)
                if run3:
                    exp_scores(*batch3, 4)
                if run2:
                    head_exp(*batch2, 1)
                if run3:
                    exp_scores(*batch3, 5)
                if run1:
                    qk_copy(*batch1)
                if run3:
                    ot_copy(*batch3, 0)
                    exp_scores(*batch3, 6)
                    exp_scores(*batch3, 7)
                    exp_scores(*batch3, 8)
                if run1:
                    probs(*batch1)
                if run2:
                    head_exp(*batch2, 2)
                if run3:
                    exp_scores(*batch3, 9)
                if run1:
                    gate_exps(*batch1)
                if run3:
                    ot_copy(*batch3, 1)
                if run2:
                    v_copy(*batch2)
                if run3:
                    exp_scores(*batch3, 10)
                    exp_scores(*batch3, 11)
                if run2:
                    head_exp(*batch2, 3)
                if run3:
                    exp_scores(*batch3, 12)
                    exp_scores(*batch3, 13)
                    ot_copy(*batch3, 2)
                if run0:
                    normalized(*batch0)
                if run3:
                    exp_scores(*batch3, 14)
                if run2:
                    correction(*batch2)
                if run3:
                    exp_scores(*batch3, 15)
                if run2:
                    head_ot(*batch2)
                if run0:
                    z_tanh(*batch0)
            run(act, step)

        @block.tensor
        def _(pe):
            pe.wait_ge(s_w, 16 * 6)
            pe.wait_ge(s_c1, 2)

            def transpose_x(t, h, q):
                pe.wait_ge(s_xn1, t + 1)
                after(pe, s_mT, t - 1)
                for j in range(TB):
                    last = pe.transpose(bA[:, j * P:(j + 1) * P], xn1[q][:, j, :], ident[:, :])
                last.then_inc(s_f1, 1)

            def project_qk(t, h, q):
                pe.wait_ge(s_xT, t + 1)
                for k in range(2):
                    last = pe.matmul(bA[:, k * SEQ:(k + 1) * SEQ], w1[:, k, :], xT[q][:, :], start=True, stop=True)
                last.then_inc(s_qkp, 1)

            def logits(t, h, q):
                pe.wait_ge(s_qk, t + 1)
                pe.wait_ge(s_xsb, t + 1)
                pe.matmul(bA[:, 0:RH], xsb[:, :], wr_s[:, :], start=True, stop=True).then_inc(s_lgp, 1)

            def project_v(t, h, q):
                pe.wait_ge(s_lg, most(t + 2))
                for j in range(TB):
                    last = pe.matmul(bA[:, j * D:(j + 1) * D], xT[q][:, j * P:(j + 1) * P], w1[:, 2, :],
                                     start=True, stop=True)
                last.then_inc(s_vp, 1)

            def transpose_max(t, h, q):
                pe.wait_ge(s_mp, t + 1)
                pe.wait_ge(s_v2, most(t + 1))
                apart(pe)
                for j in range(TB):
                    last = pe.transpose(bAb[0:NP3 * H, j * P:(j + 1) * P],
                                        mp[:, j, :, :].rearrange("p a h -> p (a h)"), identb[:, :])
                last.then_inc(s_mTp, 1)

            def scores(t, h, q, s):
                if s == 0:
                    pe.wait_ge(s_ql[q], 16 * 13 * h + 16 * 13)
                after(pe, s_red, H * t + s - 1)
                qt, h0 = s // 8, 2 * (s % 8)
                for k in range(2):
                    last = pe.matmul(bS[s % 2][:, k * SEQ:(k + 1) * SEQ], QS[q][:, h0 + k, qt * P:(qt + 1) * P],
                                     KS[q][:, h0 + k, :], start=True, stop=True)
                last.then_inc(s_sp, 1)

            def shifted_scores(t, half, q, h):
                if h == 0:
                    pe.wait_ge(s_ml[q], 16 * half + 16)
                after(pe, s_exp, H * t + h - 1)
                for kt in range(TB):
                    last = pe.matmul(bT[h % 2][:, kt * SEQ:(kt + 1) * SEQ], KS[q][:, h, kt * P:(kt + 1) * P],
                                     QS[q][:, h, :], start=True, stop=True)
                last.then_inc(s_st, 1)

            def values(t, h, q, g):
                pe.wait_ge(s_exp, H * t + 4 * g + 4)
                pe.wait_ge(s_v2, t + 1)
                if g == 0:
                    after(pe, s_fin, t)
                else:
                    pe.wait_ge(s_an, 4 * t + g)
                for kt in range(TB):
                    for j in range(4):
                        last = pe.matmul(bC[j * VC:(j + 1) * VC, 0:SEQ], V2[q][:, kt, 4 * g + j, :],
                                         PT[(4 * g + j) % 8][:, kt * SEQ:(kt + 1) * SEQ],
                                         start=(kt == 0), stop=(kt == TB - 1))
                last.then_inc(s_pv, 1)

            def transpose_o(t, h, q, g):
                pe.wait_ge(s_oe, 4 * t + g + 1)
                for qt in range(TB):
                    last = pe.transpose(bC[:, qt * P:(qt + 1) * P], OT[g % 2][:, qt * P:(qt + 1) * P], ident[:, :])
                last.then_inc(s_ot, 1)

            def transpose_attn(t, h, q):
                pe.wait_ge(s_an, 4 * t + 4)
                for qt in range(TB):
                    last = pe.transpose(bC[:, qt * P:(qt + 1) * P], attn[q][:, qt, :, :].rearrange("p h d -> p (h d)"),
                                        ident[:, :])
                last.then_inc(s_atp, 1)

            def project_out(t, h, q):
                pe.wait_ge(s_at, t + 1)
                for qt in range(TB):
                    last = pe.matmul(bC[:, qt * D:(qt + 1) * D], attnT[:, qt * P:(qt + 1) * P], w1[:, 3, :],
                                     start=True, stop=True)
                last.then_inc(s_op, 1)

            def head_qk(t, h, q, i):
                if i == 0:
                    pe.wait_ge(s_wl[q], 128 * h + 128)
                    after(pe, s_y2, t)
                else:
                    pe.wait_ge(s_fq, 2 * t + 1)
                for k in range(2):
                    last = pe.matmul(bF2[:, k * SEQ:(k + 1) * SEQ], wsel[q][:, i, k, :], xT[q][:, :],
                                     start=True, stop=True)
                last.then_inc(s_fqp, 1)

            def head_v(t, h, q):
                pe.wait_ge(s_fq, 2 * t + 2)
                for kt in range(TB):
                    last = pe.matmul(bF2[:, kt * SEQ:(kt + 1) * SEQ], xT[q][:, kt * P:(kt + 1) * P],
                                     wsel[q][:, :, 2, :], start=True, stop=True)
                last.then_inc(s_fvp, 1)

            def head_scores(t, h, q, j):
                i, jj = j // 2, j % 2
                pe.wait_ge(s_fq, 2 * t + i + 1)
                after(pe, s_ptf, RK * t + j)
                for qt in range(TB):
                    last = pe.matmul(bF1[:, qt * SEQ:(qt + 1) * SEQ], Qf[:, i, qt * P:(qt + 1) * P], Kz[:, i, jj, :],
                                     start=True, stop=True)
                last.then_inc(s_fs, 1)

            def head_transpose(t, h, q, j):
                pe.wait_ge(s_pf, RK * t + j + 1)
                for kt in range(TB):
                    for qt in range(TB):
                        last = pe.transpose(bF1[:, kt * SEQ + qt * P:kt * SEQ + (qt + 1) * P],
                                            Pf[:, qt, kt * P:(kt + 1) * P], ident[:, :])
                last.then_inc(s_ptp, 1)

            def head_out(t, h, q, j):
                pe.wait_ge(s_fv, t + 1)
                pe.wait_ge(s_ptf, RK * t + j + 1)
                for qt in range(TB):
                    for kt in range(TB):
                        last = pe.matmul(bF2[:, qt * SEQ + j * RD:qt * SEQ + (j + 1) * RD],
                                         PTf[:, kt, qt * P:(qt + 1) * P], Vf[:, kt, j * RD:(j + 1) * RD],
                                         start=(kt == 0), stop=(kt == TB - 1))
                last.then_inc(s_of, 1)

            def head_ot(t, h, q):
                pe.wait_ge(s_on, t + 1)
                for i in range(2):
                    for qt in range(TB):
                        last = pe.transpose(bF2[:, i * SEQ + qt * P:i * SEQ + (qt + 1) * P],
                                            On[:, qt * RK + 2 * i:qt * RK + 2 * i + 2, :].rearrange("p j d -> p (j d)"),
                                            ident[:, :])
                last.then_inc(s_otp, 1)

            def routed_out(t, h, q):
                pe.wait_ge(s_otf, t + 1)
                for qt in range(TB):
                    for i in range(2):
                        last = pe.matmul(bF2[:, qt * D:(qt + 1) * D], OTf[:, i, qt * P:(qt + 1) * P], wo_s[:, i, :],
                                         start=(i == 0), stop=(i == 1))
                last.then_inc(s_wop, 1)

            def step(half, p):
                batch1, batch2, batch3, batch4 = (lag(half, p, k) for k in (1, 2, 3, 4))
                run1, run2, run3, run4 = (runs(b[0]) for b in (batch1, batch2, batch3, batch4))
                if run3:
                    transpose_max(*batch3)
                if run4:
                    values(*batch4, 3)
                if run3:
                    routed_out(*batch3)
                if run2:
                    head_qk(*batch2, 0)
                if run4:
                    transpose_o(*batch4, 3)
                if run2:
                    scores(*batch2, 0)
                    head_qk(*batch2, 1)
                    scores(*batch2, 1)
                    scores(*batch2, 2)
                if run4:
                    transpose_attn(*batch4)
                if run2:
                    scores(*batch2, 3)
                if run3:
                    shifted_scores(*batch3, 0)
                if run2:
                    head_v(*batch2)
                    head_scores(*batch2, 0)
                if run3:
                    shifted_scores(*batch3, 1)
                if run2:
                    scores(*batch2, 4)
                if run3:
                    shifted_scores(*batch3, 2)
                if run4:
                    project_out(*batch4)
                if run2:
                    scores(*batch2, 5)
                    head_transpose(*batch2, 0)
                if run1:
                    transpose_x(*batch1)
                if run3:
                    shifted_scores(*batch3, 3)
                if run2:
                    scores(*batch2, 6)
                    head_scores(*batch2, 1)
                    head_out(*batch2, 0)
                if run3:
                    shifted_scores(*batch3, 4)
                if run2:
                    scores(*batch2, 7)
                if run1:
                    project_qk(*batch1)
                if run3:
                    shifted_scores(*batch3, 5)
                if run2:
                    scores(*batch2, 8)
                if run3:
                    values(*batch3, 0)
                    shifted_scores(*batch3, 6)
                if run2:
                    scores(*batch2, 9)
                if run1:
                    logits(*batch1)
                if run2:
                    head_transpose(*batch2, 1)
                if run3:
                    shifted_scores(*batch3, 7)
                if run2:
                    scores(*batch2, 10)
                if run3:
                    transpose_o(*batch3, 0)
                    shifted_scores(*batch3, 8)
                if run2:
                    scores(*batch2, 11)
                    head_out(*batch2, 1)
                    head_scores(*batch2, 2)
                    scores(*batch2, 12)
                    scores(*batch2, 13)
                if run3:
                    shifted_scores(*batch3, 9)
                    values(*batch3, 1)
                    shifted_scores(*batch3, 10)
                if run2:
                    head_transpose(*batch2, 2)
                    scores(*batch2, 14)
                if run3:
                    shifted_scores(*batch3, 11)
                if run2:
                    project_v(*batch2)
                    scores(*batch2, 15)
                    head_scores(*batch2, 3)
                    head_out(*batch2, 2)
                if run3:
                    shifted_scores(*batch3, 12)
                    transpose_o(*batch3, 1)
                    shifted_scores(*batch3, 13)
                    values(*batch3, 2)
                if run2:
                    head_transpose(*batch2, 3)
                if run3:
                    shifted_scores(*batch3, 14)
                    shifted_scores(*batch3, 15)
                if run2:
                    head_out(*batch2, 3)
                if run3:
                    transpose_o(*batch3, 2)
                if run2:
                    head_ot(*batch2)
            run(pe, step)


def arrange(inputs):
    import numpy as np
    c = np.ascontiguousarray
    a = {k: np.asarray(v) for k, v in inputs.items()}
    heads = [a[f"L1_ffn_W{n}"].reshape(D, RH, RD) for n in "qkv"]
    return {
        "x": c(a["L0_attn_x"].reshape(B * SEQ, D)),
        "l0_w": c(np.stack([a[f"L0_attn_W_{n}"].T for n in "kvro"], axis=1)),
        "l0_cols": c(np.stack([a["L0_attn_time_decay"], a["L0_attn_time_first"]]
                              + [a[f"L0_attn_time_mix_{n}"].reshape(D) for n in "kvr"], axis=1)),
        "rms_scale": c(a["L0_ffn_scale"].reshape(1, D)),
        "centT": c(a["L0_ffn_centroids"].T),
        "up_w": c(a["L0_ffn_up_w"].transpose(1, 0, 2).reshape(D, NE * 2 * HID)),
        "down_w": c(a["L0_ffn_down_w"].reshape(NE, 2, P, D).transpose(2, 0, 1, 3).reshape(P, NE * 2 * D)),
        "l1_w": c(np.stack([a[f"L1_attn_{n}_w"].T for n in ("q", "k", "v", "out")], axis=1)),
        "out_b": c(a["L1_attn_out_b"].reshape(1, D)),
        "qkv_w": c(np.stack(heads, axis=2).transpose(1, 0, 2, 3)),
        "qkv_b": c(np.stack([a[f"L1_ffn_b{n}"].reshape(RH, RD) for n in "qkv"], axis=2)),
        "wr": c(a["L1_ffn_Wr"]),
        "br": c(a["L1_ffn_br"].reshape(1, RH)),
        "wo": c(a["L1_ffn_Wo"].reshape(2, P, D).transpose(1, 0, 2)),
        "bo": c(a["L1_ffn_bo"].reshape(1, D)),
    }


def kernel(**inputs):
    import concourse.bacc as bacc
    from concourse.bass_utils import run_bass_kernel_spmd

    nc = bacc.Bacc("TRN2", target_bir_lowering=False, num_devices=1)
    arrays = arrange(inputs)
    args = [nc.dram_tensor(f"in_{n}", v.shape, mybir.dt.from_np(v.dtype), kind="ExternalInput").ap()
            for n, v in arrays.items()]
    args.append(nc.dram_tensor("out_x", (B * SEQ, D), fp32, kind="ExternalOutput").ap())
    args += [nc.dram_tensor(n, shape, dt, kind="Internal").ap() for n, shape, dt in SCRATCH]
    program(nc, *args)
    r = run_bass_kernel_spmd(nc, [{f"in_{n}": v for n, v in arrays.items()}], core_ids=[0])
    return r.results[0]["out_x"].reshape(B, SEQ, D)
```

```python
import concourse.bass as bass
from concourse import mybir
from contextlib import ExitStack

B, SEQ, D = 32, 256, 128
P = 128
TB = SEQ // P
NT = B * TB
NE, HID = 8, 256
NST = NT + NE
H, HD = 16, 8
BLK = 64
NBLK = SEQ // BLK
RH, RK, RD = 16, 4, 64
LN_EPS, RMS_EPS, WKV_EPS = 1e-5, 1e-6, 1e-9
NEG_INF = -1e38

fp32 = mybir.dt.float32
bf16 = mybir.dt.bfloat16
i32 = mybir.dt.int32
u32 = mybir.dt.uint32
ALU = mybir.AluOpType
ACT = mybir.ActivationFunctionType
AX = mybir.AxisListType


def after(eng, sem, count):
    if not (isinstance(count, int) and count <= 0):
        eng.wait_ge(sem, count)

SCRATCH = [("xs_dram", (NST * P, D), fp32), ("ys_dram", (NST * P, D), fp32),
           ("parts_dram", (2, 2, 3, P, SEQ), bf16), ("mrow_dram", (2, 3, H, SEQ), bf16)]


def apart(eng):
    eng.nop(nofuse=True)


class Chain:

    def __init__(self, eng, sem, n, batch):
        self.eng, self.sem, self.n, self.base, self.k = eng, sem, n, batch * n, 0

    def __call__(self, ins):
        self.k += 1
        ins.then_inc(self.sem, 1)
        self.eng.wait_ge(self.sem, self.base + self.k)

    def end(self):
        assert self.k == self.n, (self.k, self.n)


def program(nc, x, l0_w, l0_cols, rms_scale, centT, up_w, down_w, l1_w, out_b, qkv_w, qkv_b,
            wr, br, wo, bo, out, xs_dram, ys_dram, parts_dram, mrow_dram):
    with ExitStack() as ctx:
        def sb(name, shape, dt=fp32):
            return ctx.enter_context(nc.sbuf_tensor(name, shape, dt))

        ident = sb("ident", [P, P])
        ones = sb("ones", [P, SEQ])
        mhalf = sb("mhalf", [P, NT])
        X = sb("X", [P, NT, D])
        S = sb("S", [P, NT, D])
        rstd = sb("rstd", [P, NT])
        nmr = sb("nmr", [P, NT])
        slot = sb("slot", [P, NT], i32)
        PS = [ctx.enter_context(nc.psum_tensor(f"PS{i}", [P, 512], fp32)) for i in range(8)]
        with ExitStack() as front:
            def sbf(name, shape, dt=fp32):
                return front.enter_context(nc.sbuf_tensor(name, shape, dt))

            XR = sbf("XR", [P, NT, D])
            up = sbf("up", [P, NE * 2 * HID])
            down = sbf("down", [P, NE * 2 * D])
            earlier = sbf("earlier", [P, P])
            iota_t = sbf("iota_t", [P, NST])
            onehot = sbf("onehot", [P, NT, NE])
            cols = sbf("cols", [P, 5])
            decay = sbf("decay", [P, SEQ])
            wmix = sbf("wmix", [P, 2, 3, D])
            w_out = sbf("w_out", [P, D])
            choose_experts(nc, x, l0_w, l0_cols, rms_scale, centT, up_w, down_w, xs_dram, ident, ones, mhalf, X, XR,
                           rstd, nmr, up, down, earlier, iota_t, onehot, cols, decay, wmix, w_out, PS)
            experts_and_recurrence(nc, X, S, rstd, nmr, onehot, earlier, ones, iota_t, ident, slot, XR, up, down, cols,
                                   decay, wmix, w_out, PS, xs_dram, ys_dram)
        layer_one(nc, X, S, rstd, nmr, slot, ident, ones, mhalf, PS, ys_dram, parts_dram, mrow_dram, l1_w, out_b,
                  qkv_w, qkv_b, wr, br, wo, bo, out)


def choose_experts(nc, x, l0_w, l0_cols, rms_scale, centT, up_w, down_w, xs_dram, ident, ones, mhalf, X, XR,
                   rstd, nmr, up, down, earlier, iota_t, onehot, cols, decay, wmix, w_out, PS):
    with ExitStack() as ctx:
        def sb(name, shape, dt=fp32):
            return ctx.enter_context(nc.sbuf_tensor(name, shape, dt))

        def sem(name):
            return ctx.enter_context(nc.semaphore(name))

        NCH = 4
        CH = NT // NCH
        iota_i = sb("iota_i", [P, NST], i32)
        w0 = sb("w0", [P, 4, D])
        ommix = sb("ommix", [P, 3])
        scale_b = sb("scale_b", [P, D])
        cT = sb("cT", [P, NE])
        cTsq = sb("cTsq", [P, NE])
        cT2 = sb("cT2", [P, NE])
        neg1 = sb("neg1", [P, P])
        nny = sb("nny", [P, NE])
        zero_tile = sb("zero_tile", [P, D])
        st = sb("stats_x", [P, NT, 6])
        mv = sb("mv", [P, NT, 2])
        rrms = sb("rrms", [P, NT])
        r2 = sb("r2", [P, NT])
        nmr2 = sb("nmr2", [P, NT])
        xh_t = [sb(f"xh_t{i}", [P, TB, D]) for i in range(2)]
        xr_t = [sb(f"xr_t{i}", [P, TB, D]) for i in range(2)]
        xrT = [sb(f"xrT{i}", [P, SEQ]) for i in range(2)]
        sq = [sb(f"sq{i}", [P, TB, D]) for i in range(2)]
        nxx = sb("nxx", [P, NT])
        nd = sb("nd", [P, NT, NE])
        best = sb("best", [P, NT])
        falling = sb("falling", [P, NE])
        takes = sb("takes", [P, NT, NE])

        s_const = sem("consts_ready")
        s_x = [sem(f"x_loaded{i}") for i in range(NCH)]
        s_w = sem("weights_loaded")
        s_we = sem("expert_weights_loaded")
        s_zero = sem("sorted_zeroed")
        s_setup = sem("setup_chain_pool")
        s_setv = sem("setup_chain_dve")
        s_cent = sem("centroid_norms_ready")
        s_stat = sem("x_variances_ready")
        s_msq = sem("x_mean_squares_ready")
        s_stc = sem("stats_and_route_chain")
        s_pow = sem("rsqrts_ready")
        s_r2 = sem("factors_ready")
        s_hat = sem("normalized_by_both")
        s_norm = sem("scaled")
        s_tr = sem("xr_transposed")
        s_xrT = sem("xrT_ready")
        s_xrsq = sem("xr_squared")
        s_nxx = sem("norms_ready")
        s_dist = sem("distances_in_psum")
        s_nd = sem("distances_read")
        psT, psD = PS[0:2], PS[2:4]

        def run(eng, step):
            for t in range(6):
                step(t // 2, t % 2)
            with eng.Fori(3, B // 2) as half:
                step(half, 0)
                step(half, 1)
            for t in range(B, B + 5):
                step(t // 2, t % 2)

        def lag(half, p, k):
            h, q = half + (p - k) // 2, (p - k) % 2
            return 2 * h + q, h, q

        def runs(t):
            return not isinstance(t, int) or 0 <= t < B

        block = ctx.enter_context(nc.Block())

        @block.sync
        def _(sp):
            xv = x.rearrange("(t p) d -> p t d", p=P)
            for c in range(NCH):
                sp.dma_start(X[:, c * CH:(c + 1) * CH, :], xv[:, c * CH:(c + 1) * CH, :]).then_inc(s_x[c], 16)
            for dst, src in ((w0[:, :, :], l0_w), (cols[:, :], l0_cols), (cT[:, :], centT),
                             (scale_b[:, :], rms_scale.to_broadcast([P, D]))):
                sp.dma_start(dst, src).then_inc(s_w, 16)
            sp.wait_ge(s_const, 1)
            sp.dma_start(xs_dram.rearrange("(t p) d -> p t d", p=P),
                         zero_tile[:, :].unsqueeze(1).broadcast_to([P, NST, D])).then_inc(s_zero, 16)
            sp.dma_start(up[:, :], up_w).then_inc(s_we, 16)
            sp.dma_start(down[:, :], down_w).then_inc(s_we, 16)
            sp.wait_ge(s_zero, 16)
            sp.wait_ge(s_we, 32)

        @block.gpsimd
        def _(pool):
            ch = Chain(pool, s_setup, 2, 0)
            pool.memset(zero_tile[:, :], 0.0).then_inc(s_const, 1)
            pool.memset(ones[:, :], 1.0)
            pool.memset(neg1[:, :], -1.0)
            pool.memset(mhalf[:, :], -0.5)
            pool.memset(ident[:, :], 0.0)
            ch(pool.iota(iota_i[:, :], pattern=[[1, NST]], base=0, channel_multiplier=0))
            pool.affine_select(out=ident[:, :], in_=ident[:, :], compare_op=ALU.not_equal, fill=1.0, base=0,
                               pattern=[[-1, P]], channel_multiplier=1)
            pool.affine_select(out=earlier[:, :], in_=ones[:, 0:P], compare_op=ALU.is_gt, fill=0.0, base=0,
                               pattern=[[1, P]], channel_multiplier=-1)
            ch(pool.tensor_copy(iota_t[:, :], iota_i[:, :]))
            ch.end()
            pool.sem_inc(s_const, 1)
            for c in range(NCH):
                for r, made in ((rstd, s_stat), (rrms, s_msq)):
                    pool.wait_ge(made, c + 1)
                    part = slice(c * CH, (c + 1) * CH)
                    pool.tensor_tensor(r[:, part], r[:, part], mhalf[:, part], ALU.pow).then_inc(s_pow, 1)

            def step(half, p):
                t, h, q = lag(half, p, 2)
                if runs(t):
                    pool.wait_ge(s_norm, t + 1)
                    after(pool, s_nxx, t - 1)
                    pool.tensor_tensor(sq[q][:, :, :], xr_t[q][:, :, :], xr_t[q][:, :, :], ALU.mult).then_inc(s_xrsq, 1)
            run(pool, step)

        @block.vector
        def _(dve):
            def statistics(c):
                dve.wait_ge(s_x[c], 16)
                sc = Chain(dve, s_stc, 2, c)
                tiles = range(c * CH, (c + 1) * CH)
                for t in tiles:
                    last = dve.bn_stats(st[:, t, :], X[:, t, :])
                sc(last)
                for t in tiles:
                    last = dve.bn_aggr(mv[:, t, :], st[:, t, :])
                sc(last)
                sc.end()
                part = slice(c * CH, (c + 1) * CH)
                dve.tensor_scalar(rstd[:, part], mv[:, part, 1], LN_EPS, None, ALU.add).then_inc(s_stat, 1)

            def mean_squares(c):
                part = slice(c * CH, (c + 1) * CH)
                dve.wait_ge(s_pow, 2 * c + 1)
                mc = Chain(dve, s_setv, 2, c)
                dve.scalar_tensor_tensor(nmr[:, part], mv[:, part, 0], -1.0, rstd[:, part], ALU.mult, ALU.mult)
                mc(dve.tensor_tensor(rrms[:, part], rstd[:, part], rstd[:, part], ALU.mult))
                mc(dve.tensor_tensor(rrms[:, part], rrms[:, part], mv[:, part, 1], ALU.mult))
                mc.end()
                dve.tensor_scalar(rrms[:, part], rrms[:, part], RMS_EPS, None, ALU.add).then_inc(s_msq, 1)

            def factors(c):
                part = slice(c * CH, (c + 1) * CH)
                dve.wait_ge(s_pow, 2 * c + 2)
                dve.tensor_tensor(r2[:, part], rstd[:, part], rrms[:, part], ALU.mult)
                dve.tensor_tensor(nmr2[:, part], nmr[:, part], rrms[:, part], ALU.mult).then_inc(s_r2, 1)

            statistics(0)
            for c in range(1, NCH):
                statistics(c)
                mean_squares(c - 1)
                if c > 1:
                    factors(c - 2)
            dve.wait_ge(s_w, 16 * 4)
            dve.wait_ge(s_const, 2)
            dve.tensor_scalar(decay[:, :], ones[:, :], cols[:, 0:1], None, ALU.mult)
            dve.tensor_scalar(falling[:, :], iota_t[:, 0:NE], -1.0, float(NE), ALU.mult, ALU.add)
            dve.tensor_scalar(cT2[:, :], cT[:, :], 2.0, None, ALU.mult)
            dve.tensor_scalar(w_out[:, :], w0[:, 3, :], 0.25, None, ALU.mult)
            dve.tensor_scalar(ommix[:, :], cols[:, 2:5], -1.0, 1.0, ALU.mult, ALU.add).then_inc(s_cent, 1)
            dve.tensor_tensor(cTsq[:, :], cT[:, :], cT[:, :], ALU.mult).then_inc(s_cent, 1)
            dve.wait_ge(s_cent, 2)
            for j in range(3):
                dve.tensor_scalar(wmix[:, 0, j, :], w0[:, j, :], cols[:, 2 + j:3 + j], None, ALU.mult)
                dve.tensor_scalar(wmix[:, 1, j, :], w0[:, j, :], ommix[:, j:j + 1], None, ALU.mult)
            mean_squares(NCH - 1)
            factors(NCH - 2)
            factors(NCH - 1)
            dve.wait_ge(s_cent, 3)
            dve.tensor_copy(nny[:, :], PS[7][:, 0:NE]).then_inc(s_cent, 1)
            dve.wait_ge(s_cent, 4)

            def step(half, p):
                t, h, q = lag(half, p, 1)
                if runs(t):
                    dve.wait_ge(s_hat, t + 1)
                    after(dve, s_tr, t - 1)
                    after(dve, s_xrsq, t - 1)
                    for dst in (XR[:, bass.ds(t * TB, TB), :], xr_t[q][:, :, :]):
                        last = dve.tensor_tensor(dst, xh_t[q][:, :, :],
                                                 scale_b[:, :].unsqueeze(1).broadcast_to([P, TB, D]), ALU.mult)
                    last.then_inc(s_norm, 1)
                t, h, q = lag(half, p, 3)
                if runs(t):
                    dve.wait_ge(s_xrsq, t + 1)
                    dve.tensor_reduce(nxx[:, bass.ds(t * TB, TB)], sq[q][:, :, :], AX.X, ALU.add,
                                      negate=True).then_inc(s_nxx, 1)
                t, h, q = lag(half, p, 5)
                if runs(t):
                    dve.wait_ge(s_dist, t + 1)
                    dve.tensor_tensor(nd[:, bass.ds(t * TB, TB), :],
                                      psD[q][:, 0:TB * NE].rearrange("p (j e) -> p j e", e=NE),
                                      nny[:, :].unsqueeze(1).broadcast_to([P, TB, NE]), ALU.add).then_inc(s_nd, 1)
            run(dve, step)
            full = [P, NT, NE]
            rc = Chain(dve, s_stc, 5, 0)
            rc.base = 2 * NCH
            dve.wait_ge(s_nd, B)
            dve.wait_ge(s_nxx, B)
            rc(dve.tensor_tensor(nd[:, :, :], nd[:, :, :], nxx[:, :].unsqueeze(2).broadcast_to(full), ALU.add))
            rc(dve.tensor_reduce(best[:, :], nd[:, :, :], AX.X, ALU.max))
            rc(dve.tensor_tensor(takes[:, :, :], nd[:, :, :], best[:, :].unsqueeze(2).broadcast_to(full), ALU.is_equal))
            rc(dve.tensor_tensor(takes[:, :, :], takes[:, :, :], falling[:, :].unsqueeze(1).broadcast_to(full), ALU.mult))
            rc(dve.tensor_reduce(best[:, :], takes[:, :, :], AX.X, ALU.max))
            rc.end()
            dve.tensor_tensor(onehot[:, :, :], falling[:, :].unsqueeze(1).broadcast_to(full),
                              best[:, :].unsqueeze(2).broadcast_to(full), ALU.is_equal)

        @block.scalar
        def _(act):
            act.wait_ge(s_r2, NCH)

            def step(half, p):
                t, h, q = lag(half, p, 0)
                if runs(t):
                    after(act, s_norm, t - 1)
                    for j in range(TB):
                        n = bass.ds(t * TB + j, 1)
                        last = act.activation(xh_t[q][:, j:j + 1, :], X[:, n, :], ACT.Identity, scale=r2[:, n],
                                              bias=nmr2[:, n])
                    last.then_inc(s_hat, 1)
                t, h, q = lag(half, p, 3)
                if runs(t):
                    act.wait_ge(s_tr, t + 1)
                    after(act, s_dist, t - 1)
                    act.copy(xrT[q][:, :], psT[q][:, 0:SEQ]).then_inc(s_xrT, 1)
            run(act, step)

        @block.tensor
        def _(pe):
            pe.wait_ge(s_const, 2)
            pe.wait_ge(s_cent, 2)
            pe.matmul(PS[7][:, 0:NE], neg1[:, :], cTsq[:, :], start=True, stop=True).then_inc(s_cent, 1)

            def step(half, p):
                t, h, q = lag(half, p, 2)
                if runs(t):
                    pe.wait_ge(s_norm, t + 1)
                    after(pe, s_xrT, t - 1)
                    for j in range(TB):
                        last = pe.transpose(psT[q][:, j * P:(j + 1) * P], xr_t[q][:, j, :], ident[:, :])
                    last.then_inc(s_tr, 1)
                t, h, q = lag(half, p, 4)
                if runs(t):
                    pe.wait_ge(s_xrT, t + 1)
                    after(pe, s_nd, t - 1)
                    for j in range(TB):
                        last = pe.matmul(psD[q][:, NE * j:NE * j + NE], xrT[q][:, j * P:(j + 1) * P], cT2[:, :],
                                         start=True, stop=True)
                    last.then_inc(s_dist, 1)
            run(pe, step)



def place_tokens(dve, s_place, s_counts, s_placed, nc, ctx, onehot, ones, iota_t, slot, tile_expert, PS):
    def sb(name, shape, dt=fp32):
        return ctx.enter_context(nc.sbuf_tensor(name, shape, dt))
    tot = sb("tot", [P, NT, NE])
    cum = sb("cum", [P, NT, NE])
    rank = sb("rank", [P, NT, NE])
    thresholds = sb("thresholds", [P, NT])
    ntiles = sb("ntiles", [P, NE])
    end = sb("end", [P, NE])
    first = sb("first", [P, NE])
    past = sb("past", [P, NST, NE])
    slot_f = sb("slot_f", [P, NT])
    te_f = sb("te_f", [P, NST])
    over = past[:, 0:NT, :].rearrange("p t e -> p (t e)").rearrange("p (e t) -> p e t", e=NE)
    ch = Chain(dve, s_place, 12, 0)
    dve.tensor_scalar(thresholds[:, :], iota_t[:, 0:NT], float(P), None, ALU.mult)
    dve.wait_ge(s_counts, 1)
    ch(dve.tensor_copy(tot[:, :, :], PS[1][:, 0:NT * NE].rearrange("p (t e) -> p t e", e=NE)))
    for e in range(NE):
        last = dve.tensor_tensor_scan(cum[:, :, e], ones[:, 0:NT], tot[:, :, e], 0.0, ALU.mult, ALU.add)
    ch(last)
    ch(dve.tensor_tensor(over, cum[:, NT - 1, :].unsqueeze(2).broadcast_to([P, NE, NT]),
                         thresholds[:, :].unsqueeze(1).broadcast_to([P, NE, NT]), ALU.is_gt))
    ch(dve.tensor_reduce(ntiles[:, :], over, AX.X, ALU.add))
    ch(dve.tensor_tensor_scan(end[:, :], ones[:, 0:NE], ntiles[:, :], 0.0, ALU.mult, ALU.add))
    ch(dve.tensor_tensor(first[:, :], end[:, :], ntiles[:, :], ALU.subtract))
    dve.tensor_tensor(cum[:, :, :], cum[:, :, :], tot[:, :, :], ALU.subtract)
    ch(dve.tensor_scalar(first[:, :], first[:, :], float(P), None, ALU.mult))
    ch(dve.tensor_tensor(rank[:, :, :], PS[0][:, 0:NT * NE].rearrange("p (t e) -> p t e", e=NE), cum[:, :, :], ALU.add))
    ch(dve.tensor_tensor(rank[:, :, :], rank[:, :, :], first[:, :].unsqueeze(1).broadcast_to([P, NT, NE]), ALU.add))
    dve.tensor_tensor(past[:, :, :], iota_t[:, :].unsqueeze(2).broadcast_to([P, NST, NE]),
                      end[:, :].unsqueeze(1).broadcast_to([P, NST, NE]), ALU.is_ge)
    ch(dve.tensor_tensor(rank[:, :, :], rank[:, :, :], onehot[:, :, :], ALU.mult))
    dve.tensor_reduce(te_f[:, :], past[:, :, :], AX.X, ALU.add)
    ch(dve.tensor_reduce(slot_f[:, :], rank[:, :, :], AX.X, ALU.add))
    ch(dve.tensor_scalar(te_f[:, :], te_f[:, :], float(NE - 1), None, ALU.min))
    ch.end()
    dve.tensor_copy(tile_expert[:, :], te_f[:, :])
    dve.tensor_copy(slot[:, :], slot_f[:, :]).then_inc(s_placed, 1)


def experts_and_recurrence(nc, X, S, rstd, nmr, onehot, earlier, ones, iota_t, ident, slot, XR, up, down, cols,
                           decay, wmix, w_out, PS, xs_dram, ys_dram):
    with ExitStack() as ctx:
        def sb(name, shape, dt=fp32):
            return ctx.enter_context(nc.sbuf_tensor(name, shape, dt))

        def two(name, shape, dt=fp32):
            return [sb(f"{name}{i}", shape, dt) for i in range(2)]

        def sem(name):
            return ctx.enter_context(nc.semaphore(name))

        FIRST = 12
        TPS = 3
        END = FIRST + NST // TPS
        assert NST % TPS == 0 and FIRST % 2 == 0 and END % 2 == 0 and B <= END
        G = 2 * TPS
        NB = 3
        LAST = 6

        xs_t = [sb(f"xs_t{i}", [P, D]) for i in range(NB)]
        xsT = [sb(f"xsT{i}", [P, P]) for i in range(NB)]
        gate = [sb(f"gate{i}", [P, HID]) for i in range(NB)]
        hid = [sb(f"hid{i}", [P, HID]) for i in range(NB)]
        hidT = [sb(f"hidT{i}", [P, 2, P]) for i in range(NB)]
        ys_t = [sb(f"ys_t{i}", [P, D]) for i in range(NB)]
        tile_expert = sb("tile_expert", [P, NST], i32)
        xn_t = two("xn_t", [P, TB, D])
        xnT = two("xnT", [P, SEQ + 1])
        kv = two("kv", [P, 2, SEQ])
        rtanh = two("rtanh", [P, SEQ])
        pp = sb("pp", [P, SEQ + 1])
        aa = sb("aa", [P, SEQ + 1])
        bb = sb("bb", [P, SEQ + 1])
        diff = sb("diff", [P, 2, SEQ])
        args = sb("args", [P, 2, 2, SEQ])
        ex = two("ex", [P, 4, SEQ])
        ev = two("ev", [P, 2, SEQ])
        num = two("num", [P, SEQ])
        den = two("den", [P, SEQ])
        rwkv = two("rwkv", [P, SEQ])

        s_counts = sem("counts_in_psum")
        s_place = sem("place_chain")
        s_placed = sem("slots_ready")
        s_scat = sem("tokens_scattered")
        s_xs = [sem(f"xs_loaded{i}") for i in range(NB)]
        s_fx = sem("xs_transposed")
        s_xsT = sem("xsT_ready")
        s_up = sem("hidden_in_psum")
        s_gate = sem("gate_tanh_ready2")
        s_gch = sem("gate_chain")
        s_hid = sem("hidden_ready")
        s_fh = sem("hidden_transposed")
        s_hidT = sem("hidT_ready")
        s_dn = sem("expert_out_in_psum")
        s_y = sem("expert_out_ready")
        s_ys = [sem(f"expert_out_stored{i}") for i in range(NB)]
        s_xn = sem("xn_normalized")
        s_tr = sem("xn_transposed")
        s_xnT = sem("xnT_ready")
        s_kvp = sem("kv_in_psum")
        s_rp = sem("r_in_psum")
        s_kv = sem("kv_ready")
        s_th = sem("gate_tanh_ready")
        s_ec = sem("exponent_chain")
        s_args = sem("differences_ready")
        s_relu = sem("exponents_ready")
        s_ex = sem("exponentials_ready")
        s_ev = sem("weighed_values_ready")
        s_rwkv = sem("rwkv_ready")
        s_wkv = sem("wkv_chain")
        s_so = sem("s_in_psum")
        s_s = sem("s_kept")
        psU, psX, psH, psY, psT, psKV, psR = PS[0:2], PS[2], PS[3], PS[4], PS[5], PS[6], PS[7]

        def lag(half, p, k):
            h, q = half + (p - k) // 2, (p - k) % 2
            return 2 * h + q, h, q

        def tile(half, p, turn, k):
            place = TPS * p + turn - k
            h, q = half - FIRST // 2 + place // G, place % G
            t = G * h + q
            return None if isinstance(t, int) and not 0 <= t < NST else (t, h, q)

        def runs(t):
            return not isinstance(t, int) or 0 <= t < B

        def run(eng, step):
            for s in range(FIRST + 4):
                step(s // 2, s % 2)
            with eng.Fori(FIRST // 2 + 2, B // 2) as half:
                step(half, 0)
                step(half, 1)
            for s in range(B, END + 2):
                step(s // 2, s % 2)

        def arrivals(h, q):
            return 16 * (G // NB * h + q // NB + 1)

        block = ctx.enter_context(nc.Block())

        @block.gpsimd
        def _(pool):
            pool.wait_ge(s_placed, 1)

            def scatter(s):
                for t in range(s * NT // FIRST, (s + 1) * NT // FIRST):
                    pool.indirect_dma_start(xs_dram, bass.IndirectOffsetOnAxis(slot[:, t:t + 1], axis=0),
                                            XR[:, t, :], None).then_inc(s_scat, 16)

            def weigh(t, h, q):
                pool.wait_ge(s_ex, t + 1)
                after(pool, s_wkv, 6 * (t - 2) + 4)
                pool.tensor_tensor(ev[q][:, :, :], ex[q][:, 1:3, :],
                                   kv[q][:, 1:2, :].broadcast_to([P, 2, SEQ]), ALU.mult).then_inc(s_ev, 1)

            def divide(t, h, q):
                pool.wait_ge(s_wkv, 6 * t + 6)
                after(pool, s_so, t - 1)
                pool.tensor_tensor(rwkv[q][:, :], num[q][:, :], den[q][:, :], ALU.mult).then_inc(s_rwkv, 1)

            def step(half, p):
                e, w = lag(half, p, 3), lag(half, p, 4)
                if isinstance(half, int) and 2 * half + p < FIRST:
                    scatter(2 * half + p)
                if runs(e[0]):
                    weigh(*e)
                if runs(w[0]):
                    divide(*w)
            run(pool, step)
            pool.wait_ge(s_scat, 16 * NT)

        @block.sync
        def _(sp):
            sp.wait_ge(s_scat, 16 * NT)

            def load(t, h, q):
                after(sp, s_fx, t - NB + 1)
                apart(sp)
                sp.dma_start(xs_t[q % NB][:, :], xs_dram[bass.ds(t * P, P), :]).then_inc(s_xs[q % NB], 16)

            def store(t, h, q):
                sp.wait_ge(s_y, t + 1)
                apart(sp)
                sp.dma_start(ys_dram[bass.ds(t * P, P), :], ys_t[q % NB][:, :]).then_inc(s_ys[q % NB], 16)

            for t in range(NB):
                load(t, 0, t)

            def step(half, p):
                for turn in range(TPS):
                    new = tile(half, p, turn, -NB)
                    if new and (not isinstance(new[0], int) or new[0] >= NB):
                        load(*new)
                    done = tile(half, p, turn, LAST)
                    if done:
                        store(*done)
            for s in range(FIRST, FIRST + 4):
                step(s // 2, s % 2)
            with sp.Fori(FIRST // 2 + 2, END // 2 - 1) as half:
                step(half, 0)
                step(half, 1)
            for s in range(END - 2, END + 2):
                step(s // 2, s % 2)
            for i in range(NB):
                sp.wait_ge(s_ys[i], 16 * (NST // NB))

        @block.vector
        def _(dve):
            dve.memset(pp[:, 0:1], NEG_INF)
            dve.memset(aa[:, 0:1], 0.0)
            dve.memset(bb[:, 0:1], 0.0)
            place_tokens(dve, s_place, s_counts, s_placed, nc, ctx, onehot, ones, iota_t, slot, tile_expert, PS)

            def exponents(t, h, q):
                dve.wait_ge(s_kv, t + 1)
                k = kv[q][:, 0, :]
                c = Chain(dve, s_ec, 1, t)
                c(dve.tensor_tensor_scan(pp[:, 1:SEQ + 1], decay[:, :], k, NEG_INF, ALU.add, ALU.max))
                c.end()
                after(dve, s_relu, t)
                dve.scalar_tensor_tensor(diff[:, 0, :], pp[:, 0:SEQ], cols[:, 0:1], k, ALU.add, ALU.subtract)
                dve.scalar_tensor_tensor(diff[:, 1, :], k, cols[:, 1:2], pp[:, 0:SEQ],
                                         ALU.add, ALU.subtract).then_inc(s_args, 1)

            def sums(t, h, q):
                dve.wait_ge(s_ex, t + 1)
                c = Chain(dve, s_wkv, 6, t)
                after(dve, s_rwkv, t - 1)
                c(dve.tensor_tensor_scan(bb[:, 1:SEQ + 1], ex[q][:, 0, :], ex[q][:, 1, :], 0.0, ALU.mult, ALU.add))
                dve.wait_ge(s_ev, t + 1)
                dve.tensor_tensor_scan(aa[:, 1:SEQ + 1], ex[q][:, 0, :], ev[q][:, 0, :], 0.0, ALU.mult, ALU.add)
                c(dve.tensor_tensor(den[q][:, :], ex[q][:, 3, :], bb[:, 0:SEQ], ALU.mult))
                dve.scalar_tensor_tensor(den[q][:, :], den[q][:, :], WKV_EPS, ex[q][:, 2, :], ALU.add, ALU.add)
                c(dve.tensor_tensor(num[q][:, :], ex[q][:, 3, :], aa[:, 0:SEQ], ALU.mult))
                c(dve.tensor_tensor(num[q][:, :], num[q][:, :], ev[q][:, 1, :], ALU.add))

            def quotient(t, h, q):
                c = Chain(dve, s_wkv, 6, t)
                c.k = 4
                c(dve.reciprocal(den[q][:, :], den[q][:, :]))
                dve.wait_ge(s_th, t + 1)
                c(dve.scalar_tensor_tensor(num[q][:, :], rtanh[q][:, :], 1.0, num[q][:, :], ALU.add, ALU.mult))
                c.end()

            def experts(half, p, turn):
                now = tile(half, p, turn, 2)
                if now:
                    t, h, q = now
                    c = Chain(dve, s_gch, 1, t)
                    dve.wait_ge(s_gate, t + 1)
                    after(dve, s_fh, t - NB + 1)
                    g, u = gate[q % NB], psU[q % 2]
                    c(dve.scalar_tensor_tensor(g[:, :], g[:, :], 1.0, u[:, HID:], ALU.add, ALU.mult))
                    dve.tensor_tensor(hid[q % NB][:, :], u[:, 0:HID], g[:, :], ALU.mult).then_inc(s_hid, 1)
                    c.end()

            def step(half, p):
                e, w = lag(half, p, 3), lag(half, p, 4)
                if runs(e[0]):
                    exponents(*e)
                experts(half, p, 0)
                if runs(w[0]):
                    sums(*w)
                experts(half, p, 1)
                if runs(w[0]):
                    quotient(*w)
                experts(half, p, 2)
            run(dve, step)

        @block.scalar
        def _(act):
            for i in range(2):
                act.mul(xnT[i][:, 0:1], ones[:, 0:1], 0.0)

            def normalize(t, h, q):
                after(act, s_tr, t - 1)
                for j in range(TB):
                    n = bass.ds(t * TB + j, 1)
                    last = act.activation(xn_t[q][:, j:j + 1, :], X[:, n, :], ACT.Identity, scale=rstd[:, n],
                                          bias=nmr[:, n])
                last.then_inc(s_xn, 1)

            def transposed(t, h, q):
                act.wait_ge(s_tr, t + 1)
                after(act, s_rp, t - 1)
                act.copy(xnT[q][:, 1:SEQ + 1], psT[:, 0:SEQ]).then_inc(s_xnT, 1)

            def keys_values(t, h, q):
                act.wait_ge(s_kvp, t + 1)
                after(act, s_ev, t - 1)
                act.copy(kv[q][:, :, :], psKV[:, :].rearrange("p (a n) -> p a n", a=2)).then_inc(s_kv, 1)

            def receptance(t, h, q):
                act.wait_ge(s_rp, t + 1)
                after(act, s_wkv, 6 * (t - 1))
                act.activation(rtanh[q][:, :], psR[:, 0:SEQ], ACT.Tanh, scale=0.5).then_inc(s_th, 1)

            def exps(t, h, q):
                act.wait_ge(s_args, t + 1)
                act.activation(args[:, :, 0, :], diff[:, :, :], ACT.Relu, scale=-1.0)
                act.activation(args[:, :, 1, :], diff[:, :, :], ACT.Relu).then_inc(s_relu, 1)
                act.wait_ge(s_relu, t + 1)
                after(act, s_wkv, 6 * (t - 2) + 4)
                act.activation(ex[q][:, :, :], args[:, :, :, :].rearrange("p a b n -> p (a b) n"), ACT.Exp, scale=-1.0).then_inc(s_ex, 1)

            def keep(t, h, q):
                act.wait_ge(s_so, t + 1)
                act.copy(S[:, bass.ds(t * TB, TB), :],
                         psR[:, 0:TB * D].rearrange("p (a n) -> p a n", a=TB)).then_inc(s_s, 1)

            def experts(half, p, turn):
                now = tile(half, p, turn, 0)
                if now:
                    t, h, q = now
                    act.wait_ge(s_fx, t + 1)
                    after(act, s_up, t - NB + 1)
                    act.copy(xsT[q % NB][:, :], psX[:, 0:P]).then_inc(s_xsT, 1)
                now = tile(half, p, turn, 3)
                if now:
                    t, h, q = now
                    act.wait_ge(s_fh, t + 1)
                    after(act, s_dn, t - NB + 1)
                    act.copy(hidT[q % NB][:, :, :], psH[:, 0:2 * P].rearrange("p (c n) -> p c n", c=2)).then_inc(s_hidT, 1)
                now = tile(half, p, turn, 4)
                if now:
                    t, h, q = now
                    act.wait_ge(s_dn, t + 1)
                    after(act, s_ys[q % NB], arrivals(h, q) - 16)
                    act.mul(ys_t[q % NB][:, :], psY[:, 0:D], 0.5).then_inc(s_y, 1)
                now = tile(half, p, turn, 1)
                if now:
                    t, h, q = now
                    act.wait_ge(s_up, t + 1)
                    after(act, s_hid, t - NB + 1)
                    act.activation(gate[q % NB][:, :], psU[q % 2][:, HID:], ACT.Tanh, scale=0.5).then_inc(s_gate, 1)

            def step(half, p):
                a, f, b, e, k = (lag(half, p, n) for n in (0, 1, 2, 3, 5))
                experts(half, p, 0)
                if runs(e[0]):
                    exps(*e)
                experts(half, p, 1)
                if runs(k[0]):
                    keep(*k)
                if runs(b[0]):
                    keys_values(*b)
                if runs(a[0]):
                    normalize(*a)
                if runs(f[0]):
                    transposed(*f)
                experts(half, p, 2)
                if runs(b[0]):
                    receptance(*b)
            run(act, step)

        @block.tensor
        def _(pe):
            pe.matmul(PS[0][:, 0:NT * NE], earlier[:, :], onehot[:, :, :].rearrange("p t e -> p (t e)"), start=True, stop=True)
            pe.matmul(PS[1][:, 0:NT * NE], ones[:, 0:P], onehot[:, :, :].rearrange("p t e -> p (t e)"),
                      start=True, stop=True).then_inc(s_counts, 1)
            experts_of = [pe.alloc_register(f"expert{i}") for i in range(G)]

            def flip(t, h, q):
                pe.wait_ge(s_xn, t + 1)
                after(pe, s_xnT, t)
                for j in range(TB):
                    last = pe.transpose(psT[:, j * P:(j + 1) * P], xn_t[q][:, j, :], ident[:, :])
                last.then_inc(s_tr, 1)

            def project(t, h, q, j, out, done=None):
                pe.matmul(out, wmix[:, 0, j, :], xnT[q][:, 1:SEQ + 1], start=True, stop=False)
                last = pe.matmul(out, wmix[:, 1, j, :], xnT[q][:, 0:SEQ], start=False, stop=True)
                if done is not None:
                    last.then_inc(done, 1)

            def out_projection(t, h, q):
                pe.wait_ge(s_rwkv, t + 1)
                pe.wait_ge(s_th, min(t + 3, B) if isinstance(t, int) else t + 3)
                after(pe, s_s, t)
                for j in range(TB):
                    last = pe.matmul(psR[:, j * D:(j + 1) * D], rwkv[q][:, j * P:(j + 1) * P], w_out[:, :],
                                     start=True, stop=True)
                last.then_inc(s_so, 1)

            def transposes(half, p, turn):
                now = tile(half, p, turn, 0)
                if now:
                    t, h, q = now
                    pe.wait_ge(s_xs[q % NB], arrivals(h, q))
                    after(pe, s_xsT, t)
                    pe.transpose(psX[:, 0:P], xs_t[q % NB][:, :], ident[:, :]).then_inc(s_fx, 1)
                now = tile(half, p, turn, 3)
                if now:
                    t, h, q = now
                    pe.wait_ge(s_hid, t + 1)
                    after(pe, s_hidT, t)
                    for c in range(2):
                        last = pe.transpose(psH[:, c * P:(c + 1) * P], hid[q % NB][:, c * P:(c + 1) * P], ident[:, :])
                    last.then_inc(s_fh, 1)

            def products(half, p, turn):
                now = tile(half, p, turn, 4)
                if now:
                    t, h, q = now
                    e = pe.snap(experts_of[q], min_val=0, max_val=NE - 1)
                    pe.wait_ge(s_hidT, t + 1)
                    after(pe, s_y, t)
                    for c in range(2):
                        last = pe.matmul(psY[:, 0:D], hidT[q % NB][:, c, :], down[:, bass.ds(e * 2 * D + c * D, D)],
                                         start=(c == 0), stop=(c == 1))
                    last.then_inc(s_dn, 1)
                new = tile(half, p, turn, 0)
                if turn == 0 and new:
                    t, h, q = new
                    pe.load(experts_of[q:q + TPS], tile_expert[0:1, bass.ds(t, TPS)])
                now = tile(half, p, turn, 1)
                if now:
                    t, h, q = now
                    e = pe.snap(experts_of[q], min_val=0, max_val=NE - 1)
                    pe.wait_ge(s_xsT, t + 1)
                    after(pe, s_hid, t - 1)
                    pe.matmul(psU[q % 2][:, :], xsT[q % NB][:, :], up[:, bass.ds(e * 2 * HID, 2 * HID)],
                              start=True, stop=True).then_inc(s_up, 1)

            def step(half, p):
                if isinstance(half, int) and 2 * half + p == FIRST:
                    pe.wait_ge(s_placed, 1)
                f, b, w = (lag(half, p, n) for n in (1, 2, 5))
                transposes(half, p, 0)
                if runs(b[0]):
                    pe.wait_ge(s_xnT, b[0] + 1)
                    after(pe, s_kv, b[0])
                    project(*b, 0, psKV[:, 0:SEQ])
                products(half, p, 0)
                transposes(half, p, 1)
                if runs(b[0]):
                    project(*b, 1, psKV[:, SEQ:], s_kvp)
                if runs(w[0]):
                    out_projection(*w)
                products(half, p, 1)
                if runs(f[0]):
                    flip(*f)
                transposes(half, p, 2)
                if runs(b[0]):
                    after(pe, s_th, b[0])
                    after(pe, s_s, b[0] - 2)
                    project(*b, 2, psR[:, 0:SEQ], s_rp)
                products(half, p, 2)
            run(pe, step)


def layer_one(nc, X, S, rstd, nmr, slot, ident, ones, mhalf, PS, ys_dram, parts_dram, mrow_dram, l1_w, out_b,
              qkv_w, qkv_b, wr, br, wo, bo, out):
    with ExitStack() as ctx:
        def sb(name, shape, dt=fp32):
            return ctx.enter_context(nc.sbuf_tensor(name, shape, dt))

        def two(name, shape, dt=fp32):
            return [sb(f"{name}{i}", shape, dt) for i in range(2)]

        def sem(name):
            return ctx.enter_context(nc.semaphore(name))

        def sem2(name):
            return [sem(f"{name}{i}") for i in range(2)]

        NP3 = 3
        ROWS = [(0, 0), (0, 1), (0, 2), (1, 0), (1, 1), (2, 0)]
        MROW = 96
        VC = 32

        identb = sb("identb", [P, P], bf16)
        w1 = sb("w1", [P, 4, D])
        outb_b = sb("outb_b", [P, D])
        bo_b = sb("bo_b", [P, D])
        br_b = sb("br_b", [P, RH])
        wr_s = sb("wr_s", [P, RH])
        wo_s = sb("wo_s", [P, 2, D])
        zerob = sb("zerob", [P, SEQ], bf16)
        minus = sb("minus", [NP3, SEQ], bf16)
        Y = two("Y", [P, TB, D])
        slot_t = two("slot_t", [P, TB], i32)
        xnf = two("xnf", [P, TB, D])
        z = two("z", [P, TB, D])
        zt = two("zt", [P, TB, D])
        st = sb("st", [P, TB, 6])
        mva = sb("mva", [P, TB, 2])
        rs = sb("rs", [P, TB])
        xn1 = two("xn1", [P, TB, D])
        xT = two("xT", [P, SEQ])
        qk = sb("qk", [P, 2, SEQ])
        rest = sb("rest", [P, 2, SEQ])
        parts = two("parts", [P, 2, NP3, SEQ], bf16)
        xsum = sb("xsum", [P, 1])
        xsb = sb("xsb", [P, P])
        lg = sb("lg", [P, RH])
        top = sb("top", [P, 8])
        ntop = sb("ntop", [P, 1])
        prob = sb("prob", [P, RH])
        psum_ = sb("prob_sum", [P, 1])
        pinv = sb("prob_inv", [P, 1])
        ptop = sb("ptop", [P, 8])
        pidx = sb("pidx", [P, 8], u32)
        idx = two("idx", [1, 8], i32)
        nptop = sb("nptop", [P, 1])
        g5 = sb("g5", [P, RK + 1])
        gexp = sb("gexp", [P, 1])
        gsum = sb("gsum", [P, 1])
        gc = two("gc", [P, 2, 3])
        QS = two("QS", [P, H, SEQ], bf16)
        KS = two("KS", [P, H, SEQ], bf16)
        bm = sb("bm", [P, TB, H, NBLK])
        m3 = sb("m3", [P, TB, H])
        nm = sb("nm", [P, TB, H])
        nmr_ = sb("nm_rest", [P, TB, H])
        cdiff = sb("cdiff", [P, TB, H])
        corr = sb("corr", [P, TB, H])
        fac = two("fac", [P, TB, H])
        mp = sb("mp", [P, TB, NP3, H], bf16)
        mT = two("mT", [NP3 * H, SEQ], bf16)
        V2 = two("V2", [P, TB, H, VC])
        wsel = two("wsel", [P, 2, 3, P])
        bsel = two("bsel", [P, 2, 3])
        gb = two("gb", [P, 2, 3])
        Qf = sb("Qf", [P, 2, SEQ])
        Kz = sb("Kz", [P, 2, 2, SEQ])
        Vf = sb("Vf", [P, TB, RK * RD])
        nmf = sb("nmf", [P, TB])
        Pf = sb("Pf", [P, TB, SEQ])
        lsum = sb("lsum", [P, TB, RK])
        linv = sb("linv", [P, TB * RK])
        PTf = sb("PTf", [P, TB, SEQ])
        On = sb("On", [P, TB * RK, RD])
        PT = [sb(f"PT{i}", [P, TB * SEQ]) for i in range(8)]
        OT = two("OT", [P, SEQ])
        lf = sb("lf", [P, TB, 4])
        attn = two("attn", [P, TB, H, HD])
        attnT = sb("attnT", [P, SEQ])
        OTf = sb("OTf", [P, 2, SEQ])
        y2 = sb("y2", [P, TB, D])
        y2t = sb("y2t", [P, TB, D])
        g2 = two("g2", [P, TB, D])
        s1 = sb("s1", [P, TB, D])
        o_t = two("o_t", [P, TB, D])

        s_w = sem("l1_weights")
        s_c0 = sem("l1_consts_pool")
        s_c1 = sem("l1_consts_dve")
        s_c2 = sem("values_set_up")
        s_clear = sem("operands_cleared")
        s_slot = sem("slots_copied")
        s_fac = sem("factor_ready")
        s_g2 = sem("gate_two_ready")
        s_gch = sem("gate_chain3")
        s_y = sem2("expert_out_gathered")
        s_xnf = sem("xn_ready")
        s_z = sem("z_ready")
        s_zt = sem("z_tanh_ready")
        s_gz = sem("z_gated")
        s_x1c = sem("x1_chain")
        s_x1 = sem("x1_ready")
        s_lnc = sem("ln_chain")
        s_ve = sem("x1_variance_ready")
        s_rs = sem("x1_rstd_ready")
        s_xn1 = sem("xn1_ready")
        s_f1 = sem("x1_transposed")
        s_xT = sem("xT_ready")
        s_qkp = sem("qk_in_psum")
        s_qk = sem("qk_ready")
        s_hi = sem("qk_high_ready")
        s_spc = sem("split_chain")
        s_parts = sem("parts_ready")
        s_pst = sem2("parts_stored")
        s_xsc = sem("token_sum_ready")
        s_xsb = sem("token_mean_ready")
        s_lgp = sem("logits_in_psum")
        s_lgc = sem("router_chain")
        s_lg = sem("logits_read")
        s_lg2 = sem("logit_max_ready")
        s_pe1 = sem("probs_exp_ready")
        s_pt = sem("prob_top_ready")
        s_pe2 = sem("gates_exp_ready")
        s_idx = sem("heads_chosen")
        s_gc = sem("gates_ready")
        s_wl = sem2("head_weights_loaded")
        s_bl = sem2("head_biases_loaded")
        s_ql = sem2("qs_ks_loaded")
        s_sp = sem("scores_in_psum")
        s_red = sem("block_maxima_read")
        s_mc = sem("max_chain")
        s_cd = sem("max_difference_ready")
        s_corr = sem("correction_ready")
        s_nm = sem("maxima_ready")
        s_mpc = sem("max_split_chain")
        s_mp = sem("max_parts_ready")
        s_mTp = sem("max_transposed")
        s_mT = sem("mT_ready")
        s_ms = sem2("max_rows_stored")
        s_ml = sem2("max_rows_loaded")
        s_vp = sem("v_in_psum")
        s_v2 = sem("V2_ready")
        s_gb = sem("head_biases_ready")
        s_fqp = sem("head_qk_in_psum")
        s_fq = sem("head_qk_ready")
        s_fvp = sem("head_v_in_psum")
        s_fv = sem("head_v_ready")
        s_fs = sem("head_scores_in_psum")
        s_fm = sem("head_max_ready")
        s_pf = sem("head_probs_ready")
        s_ptp = sem("head_probs_transposed")
        s_ptf = sem("head_PT_ready")
        s_of = sem("head_out_in_psum")
        s_ofc = sem("head_out_chain")
        s_on = sem("head_out_ready")
        s_otp = sem("head_out_transposed")
        s_otf = sem("head_OT_ready")
        s_wop = sem("routed_out_in_psum")
        s_y2 = sem("routed_out_ready")
        s_y2t = sem("routed_tanh_ready")
        s_st = sem("shifted_scores_in_psum")
        s_exp = sem("exp_scores_ready")
        s_pv = sem("values_in_psum")
        s_oe = sem("OT_ready")
        s_ot = sem("O_transposed")
        s_lf = sem("attn_sums_ready")
        s_li = sem("attn_inverses_ready")
        s_an = sem("attn_normalized")
        s_atp = sem("attn_transposed")
        s_at = sem("attnT_ready")
        s_op = sem("attn_out_in_psum")
        s_fc = sem("final_chain")
        s_fin = sem("attn_out_read")
        s_done = sem("out_ready")
        s_out = sem2("out_stored")

        bS, bT, bC, bA, bF1, bF2 = PS[0:2], PS[2:4], PS[4], PS[5], PS[6], PS[7]
        bAb = bA[:, :].bitcast(bf16)

        def lag(half, p, k):
            h, q = half + (p - k) // 2, (p - k) % 2
            return 2 * h + q, h, q

        def runs(t):
            return not isinstance(t, int) or 0 <= t < B

        def run(eng, step):
            for t in range(6):
                step(t // 2, t % 2)
            with eng.Fori(3, B // 2) as half:
                step(half, 0)
                step(half, 1)
            for t in range(B, B + 4):
                step(t // 2, t % 2)

        def most(t):
            return min(t, B) if isinstance(t, int) else t

        def tiles(t):
            return bass.ds(t * TB, TB)

        block = ctx.enter_context(nc.Block())

        @block.sync
        def _(sp):
            for dst, src in ((w1[:, :, :], l1_w), (outb_b[:, :], out_b.to_broadcast([P, D])),
                             (bo_b[:, :], bo.to_broadcast([P, D])), (br_b[:, :], br.to_broadcast([P, RH])),
                             (wr_s[:, :], wr), (wo_s[:, :, :], wo)):
                sp.dma_start(dst, src).then_inc(s_w, 16)
            sp.wait_ge(s_c0, 1)
            for tile in (QS[1], KS[1]):
                sp.dma_start(tile[:, :, :], zerob[:, :].unsqueeze(1).broadcast_to([P, H, SEQ])).then_inc(s_clear, 16)
            sp.wait_ge(s_c1, 1)
            sp.wait_ge(s_clear, 32)
            for i in range(2):
                sp.dma_start(KS[i][MROW:MROW + NP3, :, :],
                             minus[:, :].unsqueeze(1).broadcast_to([NP3, H, SEQ])).then_inc(s_w, 16)
            sp.wait_ge(s_w, 16 * 8)

            def load_qk(t, h, q):
                sp.wait_ge(s_pst[q], 16 * h + 16)
                apart(sp)
                after(sp, s_st, H * (t - 1))
                apart(sp)
                for r, parts_of in enumerate(ROWS):
                    for k, tile in enumerate((QS[q], KS[q])):
                        src = parts_dram[q, k, parts_of[k]].rearrange("(h d) t -> d h t", d=HD)
                        sp.dma_start(tile[r * HD:(r + 1) * HD, :, :], src).then_inc(s_ql[q], 16)
                sp.dma_start(QS[q][MROW:MROW + NP3, :, :],
                             zerob[0:NP3, :].unsqueeze(1).broadcast_to([NP3, H, SEQ])).then_inc(s_ql[q], 16)

            def load_max(t, h, q):
                sp.wait_ge(s_mT, t + 1)
                apart(sp)
                sp.wait_ge(s_sp, H * (t + 1))
                apart(sp)
                sp.dma_start(mrow_dram[q].rearrange("a h t -> (a h) t"), mT[q][:, :]).then_inc(s_ms[q], 16)
                sp.wait_ge(s_ms[q], 16 * h + 16)
                apart(sp)
                sp.dma_start(QS[q][MROW:MROW + NP3, :, :], mrow_dram[q]).then_inc(s_ml[q], 16)

            head_registers = [sp.alloc_register(f"head{i}") for i in range(RK)]

            def load_heads(t, h, q):
                sp.wait_ge(s_idx, t + 1)
                apart(sp)
                after(sp, s_fv, t - 1)
                apart(sp)
                after(sp, s_gb, t - 1)
                apart(sp)
                sp.load(head_registers, idx[q][0:1, 0:RK])
                heads = [sp.snap(r, min_val=0, max_val=RH - 1) for r in head_registers]
                for j, head in enumerate(heads):
                    i, jj = j // 2, j % 2
                    sp.dma_start(wsel[q][:, i, :, jj * RD:(jj + 1) * RD],
                                 qkv_w[bass.ds(head, 1), :, :, :].rearrange("a p c d -> (a p) c d")).then_inc(s_wl[q], 16)
                for j, head in enumerate(heads):
                    i, jj = j // 2, j % 2
                    sp.dma_start(bsel[q][jj * RD:(jj + 1) * RD, i, :],
                                 qkv_b[bass.ds(head, 1), :, :].rearrange("a d c -> (a d) c")).then_inc(s_bl[q], 16)

            def store_parts(t, h, q):
                sp.wait_ge(s_parts, t + 1)
                apart(sp)
                after(sp, s_ql[q], 16 * 13 * h)
                apart(sp)
                sp.dma_start(parts_dram[q].rearrange("k a p t -> p k a t"), parts[q][:, :, :, :]).then_inc(s_pst[q], 16)

            def store_out(t, h, q):
                sp.wait_ge(s_done, t + 1)
                apart(sp)
                sp.dma_start(out[bass.ds(t * SEQ, SEQ), :].rearrange("(j p) n -> p j n", p=P),
                             o_t[q][:, :, :]).then_inc(s_out[q], 16)

            def step(half, p):
                batch0, batch2, batch4 = (lag(half, p, k) for k in (0, 2, 4))
                run0, run2, run4 = (runs(b[0]) for b in (batch0, batch2, batch4))
                if run2:
                    load_max(*batch2)
                if run4:
                    store_out(*batch4)
                if run0:
                    store_parts(*batch0)
                    load_heads(*batch0)
                    load_qk(*batch0)
            run(sp, step)
            for q in range(2):
                sp.wait_ge(s_out[q], 16 * (B // 2))

        @block.gpsimd
        def _(pool):
            pool.memset(zerob[:, :], 0.0)
            pool.memset(minus[:, :], -1.0)
            for i in range(2):
                pool.memset(V2[i][:, :, :, :], 0.0)
            pool.memset(Kz[:, :, :, :], 0.0).then_inc(s_c0, 1)
            pool.tensor_copy(identb[:, :], ident[:, :]).then_inc(s_c2, 1)

            def gather(t, h, q):
                pool.tensor_copy(slot_t[q][:, :], slot[:, tiles(t)]).then_inc(s_slot, 1)
                pool.wait_ge(s_slot, t + 1)
                after(pool, s_z, t - 1)
                apart(pool)
                for j in range(TB):
                    pool.indirect_dma_start(Y[q][:, j, :], None, ys_dram,
                                            bass.IndirectOffsetOnAxis(slot_t[q][:, j:j + 1], axis=0)).then_inc(s_y[q], 16)

            def add_skip(t, h, q):
                pool.wait_ge(s_y[q], 32 * h + 32)
                pool.wait_ge(s_xnf, t + 1)
                after(pool, s_gz, t - 1)
                pool.tensor_tensor(z[q][:, :, :], Y[q][:, :, :], xnf[q][:, :, :], ALU.add).then_inc(s_z, 1)

            def residual(t, h, q):
                pool.wait_ge(s_gz, t + 1)
                ch = Chain(pool, s_x1c, 1, t)
                ch(pool.tensor_tensor(zt[q][:, :, :], zt[q][:, :, :], S[:, tiles(t), :], ALU.mult))
                ch.end()
                pool.tensor_tensor(X[:, tiles(t), :], X[:, tiles(t), :], zt[q][:, :, :], ALU.add).then_inc(s_x1, 1)

            def inverse_std(t, h, q):
                pool.wait_ge(s_ve, t + 1)
                pool.tensor_tensor(rs[:, :], rs[:, :], mhalf[:, 0:TB], ALU.pow).then_inc(s_rs, 1)

            def split(t, h, q):
                ch = Chain(pool, s_spc, 2, t)
                pool.wait_ge(s_hi, t + 1)
                ch(pool.tensor_tensor(rest[:, :, :], qk[:, :, :], parts[q][:, :, 0, :], ALU.subtract))
                apart(pool)
                ch(pool.tensor_copy(parts[q][:, :, 1, :], rest[:, :, :]))
                pool.tensor_tensor(parts[q][:, :, 2, :], rest[:, :, :], parts[q][:, :, 1, :], ALU.subtract).then_inc(s_parts, 1)
                ch.end()

            def split_max(t, h, q):
                pool.wait_ge(s_nm, t + 1)
                after(pool, s_mTp, t)
                ch = Chain(pool, s_mpc, 3, t)
                apart(pool)
                ch(pool.tensor_copy(mp[:, :, 0, :], nm[:, :, :]))
                ch(pool.tensor_tensor(nmr_[:, :, :], nm[:, :, :], mp[:, :, 0, :], ALU.subtract))
                apart(pool)
                ch(pool.tensor_copy(mp[:, :, 1, :], nmr_[:, :, :]))
                pool.tensor_tensor(mp[:, :, 2, :], nmr_[:, :, :], mp[:, :, 1, :], ALU.subtract).then_inc(s_mp, 1)
                ch.end()

            def finish(t, h, q):
                pool.wait_ge(s_fin, t + 1)
                pool.wait_ge(s_g2, t + 1)
                ch = Chain(pool, s_fc, 1, t)
                ch(pool.tensor_tensor(s1[:, :, :], s1[:, :, :], g2[q][:, :, :], ALU.mult))
                ch.end()
                after(pool, s_out[q], 16 * h)
                pool.tensor_tensor(o_t[q][:, :, :], s1[:, :, :], X[:, tiles(t), :], ALU.add).then_inc(s_done, 1)

            def step(half, p):
                batch0, batch1, batch2, batch4 = (lag(half, p, k) for k in (0, 1, 2, 4))
                run0, run1, run2, run4 = (runs(b[0]) for b in (batch0, batch1, batch2, batch4))
                if run0:
                    gather(*batch0)
                if run1:
                    inverse_std(*batch1)
                    split(*batch1)
                if run4:
                    finish(*batch4)
                if run2:
                    split_max(*batch2)
                if run0:
                    add_skip(*batch0)
                    residual(*batch0)
            run(pool, step)

        @block.vector
        def _(dve):
            dve.memset(QS[0][:, :, :], 0.0)
            dve.memset(KS[0][:, :, :], 0.0).then_inc(s_c1, 1)
            dve.wait_ge(s_c0, 1)
            for i in range(2):
                last = dve.memset(V2[i][P - BLK:P, TB - 1, :, HD:HD + 1], 1.0)
            dve.wait_ge(s_w, 16 * 6)
            dve.tensor_scalar(w1[:, 3, :], w1[:, 3, :], 0.5, None, ALU.mult)
            dve.tensor_scalar(outb_b[:, :], outb_b[:, :], 0.5, None, ALU.mult).then_inc(s_c2, 1)
            dve.wait_ge(s_c2, 2)

            def gated(t, h, q):
                dve.wait_ge(s_zt, t + 1)
                dve.scalar_tensor_tensor(zt[q][:, :, :].rearrange("p j n -> p (j n)"),
                                         zt[q][:, :, :].rearrange("p j n -> p (j n)"), 1.0,
                                         z[q][:, :, :].rearrange("p j n -> p (j n)"), ALU.add, ALU.mult).then_inc(s_gz, 1)

            def ln_stats(t, h, q):
                dve.wait_ge(s_x1, t + 1)
                ch = Chain(dve, s_lnc, 2, t)
                for j in range(TB):
                    last = dve.bn_stats(st[:, j, :], X[:, bass.ds(t * TB + j, 1), :].rearrange("p a n -> p (a n)"))
                ch(last)
                apart(dve)
                for j in range(TB):
                    last = dve.bn_aggr(mva[:, j, :], st[:, j, :])
                ch(last)
                ch.end()
                dve.tensor_scalar(rs[:, :], mva[:, :, 1], LN_EPS, None, ALU.add).then_inc(s_ve, 1)

            def ln_apply(t, h, q):
                dve.wait_ge(s_rs, t + 1)
                after(dve, s_f1, t - 1)
                for j in range(TB):
                    last = dve.tensor_scalar(xn1[q][:, j:j + 1, :], X[:, bass.ds(t * TB + j, 1), :],
                                             mva[:, j, 0:1], rs[:, j:j + 1], ALU.subtract, ALU.mult)
                last.then_inc(s_xn1, 1)

            def token_sum(t, h, q):
                dve.wait_ge(s_xT, t + 1)
                dve.tensor_reduce(xsum[:, :], xT[q][:, :], AX.X, ALU.add).then_inc(s_xsc, 1)

            def token_mean(t, h, q):
                dve.wait_ge(s_xsc, t + 1)
                after(dve, s_lgp, t)
                dve.tensor_scalar(xsb[:, :], ones[:, 0:P], xsum[:, 0:1], 1.0 / SEQ, ALU.mult, ALU.mult).then_inc(s_xsb, 1)

            def route_a(t, h, q):
                dve.wait_ge(s_lgp, t + 1)
                ch = Chain(dve, s_lgc, 5, t)
                dve.tensor_tensor(lg[:, :], bA[:, 0:RH], br_b[:, :], ALU.add).then_inc(s_lg, 1)
                dve.wait_ge(s_lg, t + 1)
                apart(dve)
                ch(dve.max(top[:, :], lg[:, :]))
                dve.tensor_scalar(ntop[:, :], top[:, 0:1], -1.0, None, ALU.mult).then_inc(s_lg2, 1)

            def route_b(t, h, q):
                dve.wait_ge(s_pe1, t + 1)
                ch = Chain(dve, s_lgc, 5, t)
                ch.k = 1
                ch(dve.reciprocal(pinv[:, :], psum_[:, :]))
                ch(dve.tensor_scalar(prob[:, :], prob[:, :], pinv[:, 0:1], None, ALU.mult))
                apart(dve)
                ch(dve.max(ptop[:, :], prob[:, :]))
                dve.tensor_scalar(nptop[:, :], ptop[:, 0:1], -1.0, None, ALU.mult).then_inc(s_pt, 1)
                apart(dve)
                ch(dve.max_index(pidx[:, :], ptop[:, :], prob[:, :]))
                after(dve, s_wl[q], 64 * h)
                dve.tensor_copy(idx[q][:, :], pidx[0:1, :]).then_inc(s_idx, 1)
                ch.end()

            def route_c(t, h, q):
                dve.wait_ge(s_pe2, t + 1)
                ch = Chain(dve, s_gch, 3, t)
                ch(dve.scalar_tensor_tensor(gsum[:, :], g5[:, RK:RK + 1], float(RH - RK), gexp[:, :], ALU.mult, ALU.add))
                ch(dve.reciprocal(gsum[:, :], gsum[:, :]))
                g5v = g5[:, 0:RK].rearrange("p (i j) -> p i j", j=2)
                for jj in range(2):
                    rows = slice(jj * RD, (jj + 1) * RD)
                    last = dve.tensor_scalar(gc[q][rows, :, :], g5v[rows, :, jj:jj + 1].broadcast_to([RD, 2, 3]),
                                             gsum[rows, 0:1], None, ALU.mult)
                ch(last)
                ch.end()
                dve.tensor_scalar(gc[q][:, :, 0], gc[q][:, :, 0], RD ** -0.5, None, ALU.mult).then_inc(s_gc, 1)

            def head_biases(t, h, q):
                dve.wait_ge(s_gc, t + 1)
                dve.wait_ge(s_bl[q], 64 * h + 64)
                dve.tensor_tensor(gb[q][:, :, :], bsel[q][:, :, :], gc[q][:, :, :], ALU.mult).then_inc(s_gb, 1)

            def block_max(t, h, q, s):
                dve.wait_ge(s_sp, H * t + s + 1)
                qt, h0 = s // 8, 2 * (s % 8)
                dve.tensor_reduce(bm[:, qt, h0:h0 + 2, :],
                                  bS[s % 2][:, :].rearrange("p (h b k) -> p h b k", h=2, b=NBLK), AX.X, ALU.max)\
                   .then_inc(s_red, 1)

            def row_max(t, h, q):
                ch = Chain(dve, s_mc, 1, t)
                dve.wait_ge(s_red, H * (t + 1))
                ch(dve.tensor_reduce(m3[:, :, :], bm[:, :, :, 0:NBLK - 1], AX.X, ALU.max))
                after(dve, s_mp, t)
                dve.tensor_tensor(nm[:, :, :], m3[:, :, :], bm[:, :, :, NBLK - 1], ALU.max).then_inc(s_nm, 1)
                ch.end()
                dve.wait_ge(s_nm, t + 1)
                after(dve, s_corr, t)
                dve.tensor_tensor(cdiff[:, :, :], m3[:, :, :], nm[:, :, :], ALU.subtract).then_inc(s_cd, 1)

            def factor(t, h, q):
                dve.wait_ge(s_corr, t + 1)
                dve.tensor_scalar(fac[q][:, :, :], corr[:, :, :], 1.0, None, ALU.add).then_inc(s_fac, 1)

            def head_max(t, h, q, j):
                dve.wait_ge(s_fs, RK * t + j + 1)
                after(dve, s_pf, RK * t + j)
                dve.tensor_reduce(nmf[:, :], bF1[:, :].rearrange("p (a k) -> p a k", a=TB), AX.X, ALU.max,
                                  negate=True).then_inc(s_fm, 1)

            def head_pt(t, h, q, j):
                dve.wait_ge(s_ptp, RK * t + j + 1)
                after(dve, s_of, RK * t + j)
                dve.tensor_copy(PTf[:, :, :], bF1[:, :].rearrange("p (a k) -> p a k", a=TB)).then_inc(s_ptf, 1)

            def head_out(t, h, q):
                dve.wait_ge(s_of, RK * (t + 1))
                after(dve, s_otp, t)
                ch = Chain(dve, s_ofc, 1, t)
                ch(dve.reciprocal(linv[:, :], lsum[:, :, :].rearrange("p a j -> p (a j)")))
                ch.end()
                dve.tensor_tensor(On[:, :, :], bF2[:, :].rearrange("p (n d) -> p n d", d=RD),
                                  linv[:, :].unsqueeze(2).broadcast_to([P, TB * RK, RD]), ALU.mult).then_inc(s_on, 1)

            def routed_out(t, h, q):
                dve.wait_ge(s_wop, t + 1)
                after(dve, s_y2t, t)
                dve.tensor_tensor(y2[:, :, :], bA[:, 0:TB * D].rearrange("p (j n) -> p j n", j=TB),
                                  bo_b[:, :].unsqueeze(1).broadcast_to([P, TB, D]), ALU.add).then_inc(s_y2, 1)

            def routed_gate(t, h, q):
                dve.wait_ge(s_y2t, t + 1)
                after(dve, s_done, t - 1)
                dve.scalar_tensor_tensor(g2[q][:, :, :].rearrange("p j n -> p (j n)"),
                                         y2t[:, :, :].rearrange("p j n -> p (j n)"), 1.0,
                                         y2[:, :, :].rearrange("p j n -> p (j n)"), ALU.add, ALU.mult).then_inc(s_g2, 1)

            def attn_sums(t, h, q, g):
                dve.wait_ge(s_ot, 4 * t + g + 1)
                dve.wait_ge(s_fac, t + 1)
                o = bC[:, 0:SEQ].rearrange("p (a j c) -> p a j c", a=TB, c=VC)
                dve.tensor_tensor(lf[:, :, :], o[:, :, :, HD], fac[q][:, :, 4 * g:4 * g + 4], ALU.mult).then_inc(s_lf, 1)

            def attn_inverse(t, h, q, g):
                dve.wait_ge(s_lf, 4 * t + g + 1)
                dve.reciprocal(lf[:, :, :], lf[:, :, :]).then_inc(s_li, 1)

            def attn_norm(t, h, q, g):
                dve.wait_ge(s_li, 4 * t + g + 1)
                after(dve, s_atp, t - 1)
                o = bC[:, 0:SEQ].rearrange("p (a j c) -> p a j c", a=TB, c=VC)
                dve.tensor_tensor(attn[q][:, :, 4 * g:4 * g + 4, :], o[:, :, :, 0:HD],
                                  lf[:, :, :].unsqueeze(3).broadcast_to([P, TB, 4, HD]), ALU.mult).then_inc(s_an, 1)

            def final(t, h, q):
                dve.wait_ge(s_op, t + 1)
                after(dve, s_done, t)
                dve.tensor_tensor(s1[:, :, :], bC[:, 0:TB * D].rearrange("p (j n) -> p j n", j=TB),
                                  outb_b[:, :].unsqueeze(1).broadcast_to([P, TB, D]), ALU.add).then_inc(s_fin, 1)

            def step(half, p):
                batch0, batch1, batch2, batch3, batch4 = (lag(half, p, k) for k in (0, 1, 2, 3, 4))
                run0, run1, run2, run3, run4 = (runs(b[0]) for b in (batch0, batch1, batch2, batch3, batch4))
                if run2:
                    head_pt(*batch2, 0)
                if run1:
                    ln_apply(*batch1)
                if run2:
                    block_max(*batch2, 3)
                    block_max(*batch2, 4)
                    head_max(*batch2, 1)
                    block_max(*batch2, 5)
                if run4:
                    final(*batch4)
                if run2:
                    block_max(*batch2, 6)
                if run1:
                    token_sum(*batch1)
                if run2:
                    block_max(*batch2, 7)
                if run1:
                    token_mean(*batch1)
                if run2:
                    head_pt(*batch2, 1)
                if run1:
                    route_a(*batch1)
                if run2:
                    block_max(*batch2, 8)
                    head_max(*batch2, 2)
                if run3:
                    attn_sums(*batch3, 0)
                    attn_inverse(*batch3, 0)
                if run2:
                    block_max(*batch2, 9)
                if run3:
                    attn_norm(*batch3, 0)
                if run1:
                    route_b(*batch1)
                if run2:
                    head_pt(*batch2, 2)
                    block_max(*batch2, 10)
                    block_max(*batch2, 11)
                    head_max(*batch2, 3)
                    block_max(*batch2, 12)
                if run3:
                    attn_sums(*batch3, 1)
                    attn_inverse(*batch3, 1)
                if run2:
                    block_max(*batch2, 13)
                    head_pt(*batch2, 3)
                    block_max(*batch2, 14)
                    block_max(*batch2, 15)
                if run3:
                    attn_norm(*batch3, 1)
                if run2:
                    head_out(*batch2)
                    row_max(*batch2)
                if run3:
                    routed_gate(*batch3)
                if run1:
                    route_c(*batch1)
                if run3:
                    attn_sums(*batch3, 2)
                if run1:
                    head_biases(*batch1)
                if run3:
                    attn_inverse(*batch3, 2)
                    attn_norm(*batch3, 2)
                if run2:
                    routed_out(*batch2)
                if run0:
                    gated(*batch0)
                    ln_stats(*batch0)
                if run2:
                    factor(*batch2)
                if run1:
                    block_max(*batch1, 0)
                    head_max(*batch1, 0)
                if run3:
                    attn_sums(*batch3, 3)
                if run1:
                    block_max(*batch1, 1)
                if run3:
                    attn_inverse(*batch3, 3)
                    attn_norm(*batch3, 3)
                if run1:
                    block_max(*batch1, 2)
            run(dve, step)

        @block.scalar
        def _(act):
            def normalized(t, h, q):
                after(act, s_z, t - 1)
                for j in range(TB):
                    n = bass.ds(t * TB + j, 1)
                    last = act.activation(xnf[q][:, j:j + 1, :], X[:, n, :], ACT.Identity, scale=rstd[:, n],
                                          bias=nmr[:, n])
                last.then_inc(s_xnf, 1)

            def z_tanh(t, h, q):
                act.wait_ge(s_z, t + 1)
                after(act, s_x1, t - 1)
                act.activation(zt[q][:, :, :], z[q][:, :, :], ACT.Tanh, scale=0.5).then_inc(s_zt, 1)

            def xT_copy(t, h, q):
                act.wait_ge(s_f1, t + 1)
                after(act, s_fv, t - 1)
                after(act, s_v2, t - 1)
                after(act, s_xsb, t - 1)
                act.copy(xT[q][:, :], bA[:, 0:SEQ]).then_inc(s_xT, 1)

            def qk_copy(t, h, q):
                act.wait_ge(s_qkp, t + 1)
                after(act, s_parts, t)
                act.mul(qk[:, 0, :], bA[:, 0:SEQ], HD ** -0.5)
                act.copy(qk[:, 1, :], bA[:, SEQ:]).then_inc(s_qk, 1)
                act.wait_ge(s_qk, t + 1)
                after(act, s_pst[q], 16 * h)
                act.copy(parts[q][:, :, 0, :], qk[:, :, :]).then_inc(s_hi, 1)

            def probs(t, h, q):
                act.wait_ge(s_lg2, t + 1)
                act.activation(prob[:, :], lg[:, :], ACT.Exp, bias=ntop[:, 0:1], accum_out=psum_[:, :]).then_inc(s_pe1, 1)

            def gate_exps(t, h, q):
                act.wait_ge(s_pt, t + 1)
                act.activation(g5[:, 0:RK], ptop[:, 0:RK], ACT.Exp, bias=nptop[:, 0:1], accum_out=gexp[:, :])
                act.activation(g5[:, RK:RK + 1], nptop[:, 0:1], ACT.Exp).then_inc(s_pe2, 1)

            def v_copy(t, h, q):
                act.wait_ge(s_vp, t + 1)
                if isinstance(t, int) and t < 2:
                    act.wait_ge(s_c2, 2)
                after(act, s_pv, 4 * (t - 1))
                act.copy(V2[q][:, :, :, 0:HD], bA[:, 0:TB * D].rearrange("p (a h d) -> p a h d", a=TB, h=H)).then_inc(s_v2, 1)

            def mT_copy(t, h, q):
                act.wait_ge(s_mTp, t + 1)
                after(act, s_ms[q], 16 * h)
                act.copy(mT[q][:, :], bAb[0:NP3 * H, 0:SEQ]).then_inc(s_mT, 1)

            def correction(t, h, q):
                act.wait_ge(s_cd, t + 1)
                after(act, s_fac, t)
                act.activation(corr[:, :, :], cdiff[:, :, :], ACT.Exp).then_inc(s_corr, 1)

            def head_qk(t, h, q, i):
                if isinstance(t, int) and t == 0:
                    act.wait_ge(s_c0, 1)
                act.wait_ge(s_fqp, 2 * t + i + 1)
                if i == 0:
                    act.wait_ge(s_gb, t + 1)
                    after(act, s_fs, RK * t)
                act.activation(Qf[:, i, :], bA[:, 0:SEQ], ACT.Identity, scale=gc[q][:, i, 0:1], bias=gb[q][:, i, 0:1])
                for jj in range(2):
                    rows = slice(jj * RD, (jj + 1) * RD)
                    last = act.activation(Kz[rows, i, jj, :], bA[rows, SEQ:], ACT.Identity,
                                          scale=gc[q][rows, i, 1:2], bias=gb[q][rows, i, 1:2])
                last.then_inc(s_fq, 1)

            def head_v(t, h, q):
                act.wait_ge(s_fvp, t + 1)
                after(act, s_of, RK * t)
                act.copy(Vf[:, :, :], bA[:, :].rearrange("p (a n) -> p a n", a=TB)).then_inc(s_fv, 1)

            def head_exp(t, h, q, j):
                act.wait_ge(s_fm, RK * t + j + 1)
                after(act, s_ptp, RK * t + j)
                if j == 0:
                    after(act, s_on, t)
                for qt in range(TB):
                    last = act.activation(Pf[:, qt, :], bF1[:, qt * SEQ:(qt + 1) * SEQ], ACT.Exp,
                                          bias=nmf[:, qt:qt + 1], accum_out=lsum[:, qt, j:j + 1])
                last.then_inc(s_pf, 1)

            def head_ot(t, h, q):
                act.wait_ge(s_otp, t + 1)
                after(act, s_wop, t)
                for i in range(2):
                    last = act.activation(OTf[:, i, :], bA[:, i * SEQ:(i + 1) * SEQ], ACT.Identity,
                                          scale=gc[q][:, i, 2:3], bias=gb[q][:, i, 2:3])
                last.then_inc(s_otf, 1)

            def routed_tanh(t, h, q):
                act.wait_ge(s_y2, t + 1)
                after(act, s_g2, t)
                act.activation(y2t[:, :, :], y2[:, :, :], ACT.Tanh, scale=0.5).then_inc(s_y2t, 1)

            def exp_scores(t, half, q, h):
                act.wait_ge(s_st, H * t + h + 1)
                after(act, s_pv, 4 * t + h // 4 - 1)
                act.activation(PT[h % 8][:, :], bT[h % 2][:, :], ACT.Exp).then_inc(s_exp, 1)

            def ot_copy(t, h, q, g):
                act.wait_ge(s_pv, 4 * t + g + 1)
                after(act, s_ot, 4 * t + g - 1)
                act.copy(OT[g % 2][:, :], bC[:, 0:SEQ]).then_inc(s_oe, 1)

            def attnT_copy(t, h, q):
                act.wait_ge(s_atp, t + 1)
                after(act, s_op, t)
                act.copy(attnT[:, :], bC[:, 0:SEQ]).then_inc(s_at, 1)

            def step(half, p):
                batch0, batch1, batch2, batch3, batch4 = (lag(half, p, k) for k in (0, 1, 2, 3, 4))
                run0, run1, run2, run3, run4 = (runs(b[0]) for b in (batch0, batch1, batch2, batch3, batch4))
                if run2:
                    head_qk(*batch2, 1)
                    head_exp(*batch2, 0)
                    head_v(*batch2)
                if run3:
                    exp_scores(*batch3, 0)
                    exp_scores(*batch3, 1)
                if run4:
                    attnT_copy(*batch4)
                if run1:
                    xT_copy(*batch1)
                if run3:
                    exp_scores(*batch3, 2)
                    exp_scores(*batch3, 3)
                if run2:
                    head_exp(*batch2, 1)
                if run3:
                    exp_scores(*batch3, 4)
                if run1:
                    qk_copy(*batch1)
                if run3:
                    exp_scores(*batch3, 5)
                    ot_copy(*batch3, 0)
                    exp_scores(*batch3, 6)
                    routed_tanh(*batch3)
                    exp_scores(*batch3, 7)
                if run1:
                    probs(*batch1)
                if run2:
                    head_exp(*batch2, 2)
                if run1:
                    gate_exps(*batch1)
                if run3:
                    exp_scores(*batch3, 8)
                if run2:
                    v_copy(*batch2)
                if run3:
                    ot_copy(*batch3, 1)
                    exp_scores(*batch3, 9)
                if run0:
                    normalized(*batch0)
                if run2:
                    head_exp(*batch2, 3)
                if run3:
                    exp_scores(*batch3, 10)
                    exp_scores(*batch3, 11)
                    exp_scores(*batch3, 12)
                    exp_scores(*batch3, 13)
                if run2:
                    head_ot(*batch2)
                if run3:
                    ot_copy(*batch3, 2)
                if run2:
                    mT_copy(*batch2)
                if run3:
                    exp_scores(*batch3, 14)
                    exp_scores(*batch3, 15)
                if run2:
                    correction(*batch2)
                if run0:
                    z_tanh(*batch0)
                if run1:
                    head_qk(*batch1, 0)
                if run3:
                    ot_copy(*batch3, 3)
            run(act, step)

        @block.tensor
        def _(pe):
            pe.wait_ge(s_w, 16 * 6)
            pe.wait_ge(s_c2, 2)

            def transpose_x(t, h, q):
                pe.wait_ge(s_xn1, t + 1)
                after(pe, s_fv, t)
                for j in range(TB):
                    last = pe.transpose(bA[:, j * P:(j + 1) * P], xn1[q][:, j, :], ident[:, :])
                last.then_inc(s_f1, 1)

            def project_qk(t, h, q):
                pe.wait_ge(s_xT, t + 1)
                for k in range(2):
                    last = pe.matmul(bA[:, k * SEQ:(k + 1) * SEQ], w1[:, k, :], xT[q][:, :], start=True, stop=True)
                last.then_inc(s_qkp, 1)

            def logits(t, h, q):
                pe.wait_ge(s_qk, t + 1)
                pe.wait_ge(s_xsb, t + 1)
                pe.matmul(bA[:, 0:RH], xsb[:, :], wr_s[:, :], start=True, stop=True).then_inc(s_lgp, 1)

            def project_v(t, h, q):
                pe.wait_ge(s_fv, t + 1)
                pe.wait_ge(s_lg, most(t + 2))
                for j in range(TB):
                    last = pe.matmul(bA[:, j * D:(j + 1) * D], xT[q][:, j * P:(j + 1) * P], w1[:, 2, :],
                                     start=True, stop=True)
                last.then_inc(s_vp, 1)

            def transpose_max(t, h, q):
                pe.wait_ge(s_mp, t + 1)
                pe.wait_ge(s_otf, t + 1)
                apart(pe)
                for j in range(TB):
                    last = pe.transpose(bAb[0:NP3 * H, j * P:(j + 1) * P],
                                        mp[:, j, :, :].rearrange("p a h -> p (a h)"), identb[:, :])
                last.then_inc(s_mTp, 1)

            def scores(t, h, q, s):
                if s == 0:
                    pe.wait_ge(s_ql[q], 16 * 13 * h + 16 * 13)
                after(pe, s_red, H * t + s - 1)
                qt, h0 = s // 8, 2 * (s % 8)
                for k in range(2):
                    last = pe.matmul(bS[s % 2][:, k * SEQ:(k + 1) * SEQ], QS[q][:, h0 + k, qt * P:(qt + 1) * P],
                                     KS[q][:, h0 + k, :], start=True, stop=True)
                last.then_inc(s_sp, 1)

            def shifted_scores(t, half, q, h):
                if h == 0:
                    pe.wait_ge(s_ml[q], 16 * half + 16)
                after(pe, s_exp, H * t + h - 1)
                for kt in range(TB):
                    last = pe.matmul(bT[h % 2][:, kt * SEQ:(kt + 1) * SEQ], KS[q][:, h, kt * P:(kt + 1) * P],
                                     QS[q][:, h, :], start=True, stop=True)
                last.then_inc(s_st, 1)

            def values(t, h, q, g):
                pe.wait_ge(s_exp, H * t + 4 * g + 4)
                pe.wait_ge(s_v2, t + 1)
                if g == 0:
                    after(pe, s_fin, t)
                else:
                    pe.wait_ge(s_an, 4 * t + g)
                for kt in range(TB):
                    for j in range(4):
                        last = pe.matmul(bC[j * VC:(j + 1) * VC, 0:SEQ], V2[q][:, kt, 4 * g + j, :],
                                         PT[(4 * g + j) % 8][:, kt * SEQ:(kt + 1) * SEQ],
                                         start=(kt == 0), stop=(kt == TB - 1))
                last.then_inc(s_pv, 1)

            def transpose_o(t, h, q, g):
                pe.wait_ge(s_oe, 4 * t + g + 1)
                for qt in range(TB):
                    last = pe.transpose(bC[:, qt * P:(qt + 1) * P], OT[g % 2][:, qt * P:(qt + 1) * P], ident[:, :])
                last.then_inc(s_ot, 1)

            def transpose_attn(t, h, q):
                pe.wait_ge(s_an, 4 * t + 4)
                for qt in range(TB):
                    last = pe.transpose(bC[:, qt * P:(qt + 1) * P], attn[q][:, qt, :, :].rearrange("p h d -> p (h d)"),
                                        ident[:, :])
                last.then_inc(s_atp, 1)

            def project_out(t, h, q):
                pe.wait_ge(s_at, t + 1)
                for qt in range(TB):
                    last = pe.matmul(bC[:, qt * D:(qt + 1) * D], attnT[:, qt * P:(qt + 1) * P], w1[:, 3, :],
                                     start=True, stop=True)
                last.then_inc(s_op, 1)

            def head_qk(t, h, q, i):
                if i == 0:
                    pe.wait_ge(s_wl[q], 64 * h + 64)
                    after(pe, s_y2, t)
                else:
                    pe.wait_ge(s_fq, 2 * t + 1)
                for k in range(2):
                    last = pe.matmul(bA[:, k * SEQ:(k + 1) * SEQ], wsel[q][:, i, k, :], xT[q][:, :],
                                     start=True, stop=True)
                last.then_inc(s_fqp, 1)

            def head_v(t, h, q):
                pe.wait_ge(s_fq, 2 * t + 2)
                for kt in range(TB):
                    last = pe.matmul(bA[:, kt * SEQ:(kt + 1) * SEQ], xT[q][:, kt * P:(kt + 1) * P],
                                     wsel[q][:, :, 2, :], start=True, stop=True)
                last.then_inc(s_fvp, 1)

            def head_scores(t, h, q, j):
                i, jj = j // 2, j % 2
                pe.wait_ge(s_fq, 2 * t + i + 1)
                after(pe, s_ptf, RK * t + j)
                for qt in range(TB):
                    last = pe.matmul(bF1[:, qt * SEQ:(qt + 1) * SEQ], Qf[:, i, qt * P:(qt + 1) * P], Kz[:, i, jj, :],
                                     start=True, stop=True)
                last.then_inc(s_fs, 1)

            def head_transpose(t, h, q, j):
                pe.wait_ge(s_pf, RK * t + j + 1)
                for kt in range(TB):
                    for qt in range(TB):
                        last = pe.transpose(bF1[:, kt * SEQ + qt * P:kt * SEQ + (qt + 1) * P],
                                            Pf[:, qt, kt * P:(kt + 1) * P], ident[:, :])
                last.then_inc(s_ptp, 1)

            def head_out(t, h, q, j):
                pe.wait_ge(s_fv, t + 1)
                pe.wait_ge(s_ptf, RK * t + j + 1)
                if j == 0:
                    after(pe, s_on, t)
                for qt in range(TB):
                    for kt in range(TB):
                        last = pe.matmul(bF2[:, qt * SEQ + j * RD:qt * SEQ + (j + 1) * RD],
                                         PTf[:, kt, qt * P:(qt + 1) * P], Vf[:, kt, j * RD:(j + 1) * RD],
                                         start=(kt == 0), stop=(kt == TB - 1))
                last.then_inc(s_of, 1)

            def head_ot(t, h, q):
                pe.wait_ge(s_on, t + 1)
                pe.wait_ge(s_v2, t + 1)
                for i in range(2):
                    for qt in range(TB):
                        last = pe.transpose(bA[:, i * SEQ + qt * P:i * SEQ + (qt + 1) * P],
                                            On[:, qt * RK + 2 * i:qt * RK + 2 * i + 2, :].rearrange("p j d -> p (j d)"),
                                            ident[:, :])
                last.then_inc(s_otp, 1)

            def routed_out(t, h, q):
                pe.wait_ge(s_otf, t + 1)
                pe.wait_ge(s_mT, t + 1)
                for qt in range(TB):
                    for i in range(2):
                        last = pe.matmul(bA[:, qt * D:(qt + 1) * D], OTf[:, i, qt * P:(qt + 1) * P], wo_s[:, i, :],
                                         start=(i == 0), stop=(i == 1))
                last.then_inc(s_wop, 1)

            def step(half, p):
                batch1, batch2, batch3, batch4 = (lag(half, p, k) for k in (1, 2, 3, 4))
                run1, run2, run3, run4 = (runs(b[0]) for b in (batch1, batch2, batch3, batch4))
                if run4:
                    transpose_o(*batch4, 3)
                if run2:
                    scores(*batch2, 1)
                    scores(*batch2, 2)
                    head_v(*batch2)
                    head_transpose(*batch2, 0)
                    scores(*batch2, 3)
                    scores(*batch2, 4)
                if run3:
                    shifted_scores(*batch3, 0)
                if run4:
                    transpose_attn(*batch4)
                if run3:
                    shifted_scores(*batch3, 1)
                if run2:
                    head_scores(*batch2, 1)
                if run1:
                    transpose_x(*batch1)
                if run3:
                    shifted_scores(*batch3, 2)
                    shifted_scores(*batch3, 3)
                if run2:
                    scores(*batch2, 5)
                    scores(*batch2, 6)
                if run4:
                    project_out(*batch4)
                if run1:
                    project_qk(*batch1)
                if run3:
                    shifted_scores(*batch3, 4)
                if run2:
                    scores(*batch2, 7)
                    head_out(*batch2, 0)
                if run3:
                    shifted_scores(*batch3, 5)
                if run2:
                    head_transpose(*batch2, 1)
                    scores(*batch2, 8)
                if run1:
                    logits(*batch1)
                if run3:
                    values(*batch3, 0)
                    shifted_scores(*batch3, 6)
                if run2:
                    head_scores(*batch2, 2)
                if run3:
                    shifted_scores(*batch3, 7)
                if run2:
                    scores(*batch2, 9)
                if run3:
                    transpose_o(*batch3, 0)
                if run2:
                    head_out(*batch2, 1)
                if run3:
                    shifted_scores(*batch3, 8)
                if run2:
                    scores(*batch2, 10)
                    project_v(*batch2)
                    scores(*batch2, 11)
                    head_transpose(*batch2, 2)
                if run3:
                    values(*batch3, 1)
                    shifted_scores(*batch3, 9)
                if run2:
                    head_scores(*batch2, 3)
                    scores(*batch2, 12)
                if run3:
                    shifted_scores(*batch3, 10)
                if run2:
                    scores(*batch2, 13)
                if run3:
                    shifted_scores(*batch3, 11)
                    transpose_o(*batch3, 1)
                if run2:
                    head_out(*batch2, 2)
                    head_transpose(*batch2, 3)
                if run3:
                    shifted_scores(*batch3, 12)
                if run2:
                    scores(*batch2, 14)
                    scores(*batch2, 15)
                if run3:
                    shifted_scores(*batch3, 13)
                if run2:
                    head_out(*batch2, 3)
                if run3:
                    shifted_scores(*batch3, 14)
                    shifted_scores(*batch3, 15)
                if run2:
                    head_ot(*batch2)
                if run3:
                    values(*batch3, 2)
                if run2:
                    transpose_max(*batch2)
                if run3:
                    transpose_o(*batch3, 2)
                if run2:
                    routed_out(*batch2)
                if run1:
                    head_qk(*batch1, 0)
                if run3:
                    values(*batch3, 3)
                if run1:
                    head_qk(*batch1, 1)
                    scores(*batch1, 0)
                    head_scores(*batch1, 0)
            run(pe, step)


def arrange(inputs):
    import numpy as np
    c = np.ascontiguousarray
    a = {k: np.asarray(v) for k, v in inputs.items()}
    heads = [a[f"L1_ffn_W{n}"].reshape(D, RH, RD) for n in "qkv"]
    return {
        "x": c(a["L0_attn_x"].reshape(B * SEQ, D)),
        "l0_w": c(np.stack([a[f"L0_attn_W_{n}"].T for n in "kvro"], axis=1)),
        "l0_cols": c(np.stack([a["L0_attn_time_decay"], a["L0_attn_time_first"]]
                              + [a[f"L0_attn_time_mix_{n}"].reshape(D) for n in "kvr"], axis=1)),
        "rms_scale": c(a["L0_ffn_scale"].reshape(1, D)),
        "centT": c(a["L0_ffn_centroids"].T),
        "up_w": c(a["L0_ffn_up_w"].transpose(1, 0, 2).reshape(D, NE * 2 * HID)),
        "down_w": c(a["L0_ffn_down_w"].reshape(NE, 2, P, D).transpose(2, 0, 1, 3).reshape(P, NE * 2 * D)),
        "l1_w": c(np.stack([a[f"L1_attn_{n}_w"].T for n in ("q", "k", "v", "out")], axis=1)),
        "out_b": c(a["L1_attn_out_b"].reshape(1, D)),
        "qkv_w": c(np.stack(heads, axis=2).transpose(1, 0, 2, 3)),
        "qkv_b": c(np.stack([a[f"L1_ffn_b{n}"].reshape(RH, RD) for n in "qkv"], axis=2)),
        "wr": c(a["L1_ffn_Wr"]),
        "br": c(a["L1_ffn_br"].reshape(1, RH)),
        "wo": c(a["L1_ffn_Wo"].reshape(2, P, D).transpose(1, 0, 2)),
        "bo": c(a["L1_ffn_bo"].reshape(1, D)),
    }


def kernel(**inputs):
    import concourse.bacc as bacc
    from concourse.bass_utils import run_bass_kernel_spmd

    nc = bacc.Bacc("TRN2", target_bir_lowering=False, num_devices=1)
    arrays = arrange(inputs)
    args = [nc.dram_tensor(f"in_{n}", v.shape, mybir.dt.from_np(v.dtype), kind="ExternalInput").ap()
            for n, v in arrays.items()]
    args.append(nc.dram_tensor("out_x", (B * SEQ, D), fp32, kind="ExternalOutput").ap())
    args += [nc.dram_tensor(n, shape, dt, kind="Internal").ap() for n, shape, dt in SCRATCH]
    program(nc, *args)
    r = run_bass_kernel_spmd(nc, [{f"in_{n}": v for n, v in arrays.items()}], core_ids=[0])
    return r.results[0]["out_x"].reshape(B, SEQ, D)
```
